# Optimizing a Trainium2 kernel written in Bass

```python
import numpy as np
import jax
import jax.numpy as jnp

def _softmax(x, axis=-1):
    return jax.nn.softmax(x, axis=axis)

def _gelu(x):
    return jax.nn.gelu(x, approximate=True)

def _silu(x):
    return jax.nn.silu(x)

def _sigmoid(x):
    return jax.nn.sigmoid(x)

def _layernorm(x, axis=-1, eps=1e-05):
    m = jnp.mean(x, axis=axis, keepdims=True)
    v = jnp.var(x, axis=axis, keepdims=True)
    return (x - m) / jnp.sqrt(v + eps)

def _scatter_add(tgt, idx, src, axis=0):
    return tgt.at[idx].add(src)

def _segment_sum(src, seg, n):
    return jax.ops.segment_sum(src, seg, n)
kernel_name = 'mk_macaron_d2_jaxref_r8_2c658b'

def setup_inputs(seed: int=0):
    np.random.seed(seed)
    _w = jnp.asarray

    def _L0_attn_setup():
        import jax, jax.numpy as jnp
        import numpy as np
        B_SZ, L, D_MODEL = (2, 256, 128)
        EXPAND, D_STATE, D_CONV = (2, 16, 4)
        D_INNER = EXPAND * D_MODEL
        DT_RANK = D_MODEL // 16

        def _layernorm(x, g, b, eps=1e-05):
            mu = x.mean(-1, keepdims=True)
            var = ((x - mu) ** 2).mean(-1, keepdims=True)
            return (x - mu) * jax.lax.rsqrt(var + eps) * g + b

        def _causal_dwconv(x, w, b):
            xt = x.transpose(0, 2, 1)
            k = w[:, None, :]
            y = jax.lax.conv_general_dilated(xt, k, window_strides=(1,), padding=[(D_CONV - 1, 0)], dimension_numbers=('NCH', 'OIH', 'NCH'), feature_group_count=D_INNER)
            return (y + b[None, :, None]).transpose(0, 2, 1)

        def _selective_scan(u, dt, A, Bm, C, D):

            def step(h, inp):
                u_t, dt_t, B_t, C_t = inp
                dA = jnp.exp(dt_t[..., None] * A)
                h = dA * h + (dt_t * u_t)[..., None] * B_t[:, None, :]
                y = jnp.einsum('bdn,bn->bd', h, C_t)
                return (h, y)
            h0 = jnp.zeros((u.shape[0], A.shape[0], A.shape[1]), u.dtype)
            xs = (u.transpose(1, 0, 2), dt.transpose(1, 0, 2), Bm.transpose(1, 0, 2), C.transpose(1, 0, 2))
            _, ys = jax.lax.scan(step, h0, xs)
            return ys.transpose(1, 0, 2) + u * D

        def _mamba_layer(x, p):
            xz = x @ p['in_proj_w']
            xi, z = jnp.split(xz, 2, axis=-1)
            xi = jax.nn.silu(_causal_dwconv(xi, p['conv_w'], p['conv_b']))
            xdb = xi @ p['x_proj_w']
            dt = xdb[..., :DT_RANK]
            Bm = xdb[..., DT_RANK:DT_RANK + D_STATE]
            C = xdb[..., DT_RANK + D_STATE:]
            dt = jax.nn.softplus(dt @ p['dt_proj_w'] + p['dt_proj_b'])
            A = -jnp.exp(p['A_log'])
            y = _selective_scan(xi, dt, A, Bm, C, p['D'])
            return y * jax.nn.silu(z) @ p['out_proj_w']
        key = jax.random.key(seed)
        ks = jax.random.split(key, 14)
        s = 0.02
        inp = {'x': jax.random.normal(ks[0], (B_SZ, L, D_MODEL), jnp.float32), 'ln_gamma': jnp.ones((D_MODEL,), jnp.float32), 'ln_beta': jnp.zeros((D_MODEL,), jnp.float32), 'in_proj_w': jax.random.normal(ks[1], (D_MODEL, 2 * D_INNER), jnp.float32) * s, 'conv_w': jax.random.normal(ks[2], (D_INNER, D_CONV), jnp.float32) * 0.2, 'conv_b': jnp.zeros((D_INNER,), jnp.float32), 'x_proj_w': jax.random.normal(ks[3], (D_INNER, DT_RANK + 2 * D_STATE), jnp.float32) * s, 'dt_proj_w': jax.random.normal(ks[4], (DT_RANK, D_INNER), jnp.float32) * DT_RANK ** (-0.5), 'dt_proj_b': jnp.log(jnp.expm1(jax.random.uniform(ks[5], (D_INNER,), jnp.float32, 0.001, 0.1))), 'A_log': jnp.log(jnp.broadcast_to(jnp.arange(1, D_STATE + 1, dtype=jnp.float32), (D_INNER, D_STATE))), 'D': jnp.ones((D_INNER,), jnp.float32), 'out_proj_w': jax.random.normal(ks[6], (D_INNER, D_MODEL), jnp.float32) * s, 'glu_w': jax.random.normal(ks[7], (D_MODEL, 2 * D_MODEL), jnp.float32) * s, 'glu_b': jnp.zeros((2 * D_MODEL,), jnp.float32)}
        return inp
    _L0_attn_in = _L0_attn_setup()

    def _L0_ffn_setup():
        import jax, jax.numpy as jnp
        import numpy as np
        B, S, D, E, K = (2, 256, 128, 8, 2)
        H = 4 * D
        key = jax.random.key(seed)
        ks = jax.random.split(key, 6)
        x = jax.random.normal(ks[0], (B, S, D), dtype=jnp.float32)
        lim_g = np.sqrt(6.0 / (D + E)).astype(np.float32)
        W_gate = jax.random.uniform(ks[1], (D, E), minval=-lim_g, maxval=lim_g, dtype=jnp.float32)
        lim1 = np.sqrt(1.0 / D).astype(np.float32)
        lim2 = np.sqrt(1.0 / H).astype(np.float32)
        W1 = jax.random.uniform(ks[2], (E, D, H), minval=-lim1, maxval=lim1, dtype=jnp.float32)
        b1 = jax.random.uniform(ks[3], (E, H), minval=-lim1, maxval=lim1, dtype=jnp.float32)
        W2 = jax.random.uniform(ks[4], (E, H, D), minval=-lim2, maxval=lim2, dtype=jnp.float32)
        b2 = jax.random.uniform(ks[5], (E, D), minval=-lim2, maxval=lim2, dtype=jnp.float32)
        return {'x': x, 'W_gate': W_gate, 'W1': W1, 'b1': b1, 'W2': W2, 'b2': b2}
    _L0_ffn_in = _L0_ffn_setup()

    def _L1_attn_setup():
        import jax, jax.numpy as jnp
        import numpy as np
        H = 16
        WIN = 64
        key = jax.random.key(seed)
        ks = jax.random.split(key, 4)
        B, S, D = (1, 512, 128)
        s = 1.0 / np.sqrt(D)
        x = jax.random.normal(ks[0], (B, S, D), jnp.float32)
        Wqkv = jax.random.normal(ks[1], (3 * D, D), jnp.float32) * s
        bqkv = jnp.zeros((3 * D,), jnp.float32)
        Wout = jax.random.normal(ks[2], (D, D), jnp.float32) * s
        bout = jnp.zeros((D,), jnp.float32)
        return {'x': x, 'Wqkv': Wqkv, 'bqkv': bqkv, 'Wout': Wout, 'bout': bout}
    _L1_attn_in = _L1_attn_setup()

    def _L1_ffn_setup():
        import jax, jax.numpy as jnp
        import numpy as np
        HIDDEN = 128
        INTER = 512
        N_EXPERTS = 8

        def geglu(x, w1, w2, w3):
            return jax.nn.gelu(x @ w1, approximate=False) * (x @ w2) @ w3
        key = jax.random.key(seed)
        ks = jax.random.split(key, 8)
        s = 0.02
        x = jax.random.normal(ks[0], (2, 256, HIDDEN), dtype=jnp.float32)
        w1s = jax.random.normal(ks[1], (HIDDEN, INTER), dtype=jnp.float32) * s
        w2s = jax.random.normal(ks[2], (HIDDEN, INTER), dtype=jnp.float32) * s
        w3s = jax.random.normal(ks[3], (INTER, HIDDEN), dtype=jnp.float32) * s
        W1 = jax.random.normal(ks[4], (N_EXPERTS, HIDDEN, INTER), dtype=jnp.float32) * s
        W2 = jax.random.normal(ks[5], (N_EXPERTS, HIDDEN, INTER), dtype=jnp.float32) * s
        W3 = jax.random.normal(ks[6], (N_EXPERTS, INTER, HIDDEN), dtype=jnp.float32) * s
        Wg = jax.random.normal(ks[7], (HIDDEN, N_EXPERTS), dtype=jnp.float32) * s
        return {'x': x, 'w1s': w1s, 'w2s': w2s, 'w3s': w3s, 'W1': W1, 'W2': W2, 'W3': W3, 'Wg': Wg}
    _L1_ffn_in = _L1_ffn_setup()
    _d = {'L0_attn_x': _L0_attn_in['x'], 'L0_attn_ln_gamma': _L0_attn_in['ln_gamma'], 'L0_attn_ln_beta': _L0_attn_in['ln_beta'], 'L0_attn_in_proj_w': _L0_attn_in['in_proj_w'], 'L0_attn_conv_w': _L0_attn_in['conv_w'], 'L0_attn_conv_b': _L0_attn_in['conv_b'], 'L0_attn_x_proj_w': _L0_attn_in['x_proj_w'], 'L0_attn_dt_proj_w': _L0_attn_in['dt_proj_w'], 'L0_attn_dt_proj_b': _L0_attn_in['dt_proj_b'], 'L0_attn_A_log': _L0_attn_in['A_log'], 'L0_attn_D': _L0_attn_in['D'], 'L0_attn_out_proj_w': _L0_attn_in['out_proj_w'], 'L0_attn_glu_w': _L0_attn_in['glu_w'], 'L0_attn_glu_b': _L0_attn_in['glu_b'], 'L0_ffn_W_gate': _L0_ffn_in['W_gate'], 'L0_ffn_W1': _L0_ffn_in['W1'], 'L0_ffn_b1': _L0_ffn_in['b1'], 'L0_ffn_W2': _L0_ffn_in['W2'], 'L0_ffn_b2': _L0_ffn_in['b2'], 'L1_attn_Wqkv': _L1_attn_in['Wqkv'], 'L1_attn_bqkv': _L1_attn_in['bqkv'], 'L1_attn_Wout': _L1_attn_in['Wout'], 'L1_attn_bout': _L1_attn_in['bout'], 'L1_ffn_w1s': _L1_ffn_in['w1s'], 'L1_ffn_w2s': _L1_ffn_in['w2s'], 'L1_ffn_w3s': _L1_ffn_in['w3s'], 'L1_ffn_W1': _L1_ffn_in['W1'], 'L1_ffn_W2': _L1_ffn_in['W2'], 'L1_ffn_W3': _L1_ffn_in['W3'], 'L1_ffn_Wg': _L1_ffn_in['Wg']}
    _x0 = _d['L0_attn_x']
    _d['L0_attn_x'] = jax.random.normal(jax.random.fold_in(jax.random.key(seed), 1), (8, 512, 128), dtype=_x0.dtype)
    del _x0
    return _d

def reference(L0_attn_x, L0_attn_ln_gamma, L0_attn_ln_beta, L0_attn_in_proj_w, L0_attn_conv_w, L0_attn_conv_b, L0_attn_x_proj_w, L0_attn_dt_proj_w, L0_attn_dt_proj_b, L0_attn_A_log, L0_attn_D, L0_attn_out_proj_w, L0_attn_glu_w, L0_attn_glu_b, L0_ffn_W_gate, L0_ffn_W1, L0_ffn_b1, L0_ffn_W2, L0_ffn_b2, L1_attn_Wqkv, L1_attn_bqkv, L1_attn_Wout, L1_attn_bout, L1_ffn_w1s, L1_ffn_w2s, L1_ffn_w3s, L1_ffn_W1, L1_ffn_W2, L1_ffn_W3, L1_ffn_Wg):

    def _L0_attn_ref(x, ln_gamma, ln_beta, in_proj_w, conv_w, conv_b, x_proj_w, dt_proj_w, dt_proj_b, A_log, D, out_proj_w, glu_w, glu_b):
        import jax, jax.numpy as jnp
        import numpy as np
        B_SZ, L, D_MODEL = (2, 256, 128)
        EXPAND, D_STATE, D_CONV = (2, 16, 4)
        D_INNER = EXPAND * D_MODEL
        DT_RANK = D_MODEL // 16

        def _layernorm(x, g, b, eps=1e-05):
            mu = x.mean(-1, keepdims=True)
            var = ((x - mu) ** 2).mean(-1, keepdims=True)
            return (x - mu) * jax.lax.rsqrt(var + eps) * g + b

        def _causal_dwconv(x, w, b):
            xt = x.transpose(0, 2, 1)
            k = w[:, None, :]
            y = jax.lax.conv_general_dilated(xt, k, window_strides=(1,), padding=[(D_CONV - 1, 0)], dimension_numbers=('NCH', 'OIH', 'NCH'), feature_group_count=D_INNER)
            return (y + b[None, :, None]).transpose(0, 2, 1)

        def _selective_scan(u, dt, A, Bm, C, D):

            def step(h, inp):
                u_t, dt_t, B_t, C_t = inp
                dA = jnp.exp(dt_t[..., None] * A)
                h = dA * h + (dt_t * u_t)[..., None] * B_t[:, None, :]
                y = jnp.einsum('bdn,bn->bd', h, C_t)
                return (h, y)
            h0 = jnp.zeros((u.shape[0], A.shape[0], A.shape[1]), u.dtype)
            xs = (u.transpose(1, 0, 2), dt.transpose(1, 0, 2), Bm.transpose(1, 0, 2), C.transpose(1, 0, 2))
            _, ys = jax.lax.scan(step, h0, xs)
            return ys.transpose(1, 0, 2) + u * D

        def _mamba_layer(x, p):
            xz = x @ p['in_proj_w']
            xi, z = jnp.split(xz, 2, axis=-1)
            xi = jax.nn.silu(_causal_dwconv(xi, p['conv_w'], p['conv_b']))
            xdb = xi @ p['x_proj_w']
            dt = xdb[..., :DT_RANK]
            Bm = xdb[..., DT_RANK:DT_RANK + D_STATE]
            C = xdb[..., DT_RANK + D_STATE:]
            dt = jax.nn.softplus(dt @ p['dt_proj_w'] + p['dt_proj_b'])
            A = -jnp.exp(p['A_log'])
            y = _selective_scan(xi, dt, A, Bm, C, p['D'])
            return y * jax.nn.silu(z) @ p['out_proj_w']
        p = dict(in_proj_w=in_proj_w, conv_w=conv_w, conv_b=conv_b, x_proj_w=x_proj_w, dt_proj_w=dt_proj_w, dt_proj_b=dt_proj_b, A_log=A_log, D=D, out_proj_w=out_proj_w)
        skip = x
        h = _layernorm(x, ln_gamma, ln_beta)
        h = _mamba_layer(h, p)
        h = jax.nn.gelu(h, approximate=False)
        g = h @ glu_w + glu_b
        h = g[..., :D_MODEL] * jax.nn.sigmoid(g[..., D_MODEL:])
        return h + skip

    def _L0_ffn_ref(x, W_gate, W1, b1, W2, b2):
        import jax, jax.numpy as jnp
        import numpy as np
        B, S, D, E, K = (2, 256, 128, 8, 2)
        H = 4 * D
        gate = jnp.einsum('bsd,de->bse', x, W_gate)
        kth = jax.lax.top_k(gate, K)[0][..., -1:]
        mask = jax.nn.softmax(jnp.where(gate >= kth, gate, -jnp.inf), axis=-1)
        h = jax.nn.relu(jnp.einsum('bsd,edh->bseh', x, W1) + b1)
        y = jnp.einsum('bseh,ehd->bsed', h, W2) + b2
        return (y * mask[..., None]).mean(axis=-2)

    def _L1_attn_ref(x, Wqkv, bqkv, Wout, bout):
        import jax, jax.numpy as jnp
        import numpy as np
        H = 16
        WIN = 64
        B, S, D = x.shape
        d = D // H
        pads = WIN // 2
        C = WIN
        N = S // C
        L = C + WIN - 1
        qkv = (x @ Wqkv.T + bqkv).reshape(B, S, 3, H, d).transpose(2, 0, 3, 1, 4)
        q, k, v = (qkv[0], qkv[1], qkv[2])
        kp = jnp.pad(k, ((0, 0), (0, 0), (pads, pads), (0, 0)))
        vp = jnp.pad(v, ((0, 0), (0, 0), (pads, pads), (0, 0)))
        idx = jnp.arange(N)[:, None] * C + jnp.arange(L)[None, :]
        kb = kp[:, :, idx, :]
        vb = vp[:, :, idx, :]
        qc = q.reshape(B, H, N, C, d)
        scores = jnp.einsum('bhncd,bhnld->bhncl', qc, kb) / np.sqrt(d).astype(np.float32)
        c = jnp.arange(C)[:, None]
        j = jnp.arange(L)[None, :]
        band = (j >= c) & (j < c + WIN)
        scores = jnp.where(band, scores, -jnp.inf)
        attn = jax.nn.softmax(scores, axis=-1)
        o = jnp.einsum('bhncl,bhnld->bhncd', attn, vb).reshape(B, H, S, d)
        o = o.transpose(0, 2, 1, 3).reshape(B, S, D)
        return o @ Wout.T + bout

    def _L1_ffn_ref(x, w1s, w2s, w3s, W1, W2, W3, Wg):
        import jax, jax.numpy as jnp
        import numpy as np
        HIDDEN = 128
        INTER = 512
        N_EXPERTS = 8

        def geglu(x, w1, w2, w3):
            return jax.nn.gelu(x @ w1, approximate=False) * (x @ w2) @ w3
        B, T, C = x.shape
        xf = x.reshape(-1, C)
        shared = geglu(xf, w1s, w2s, w3s)
        logits = xf @ Wg
        idx = jnp.argmax(logits, axis=-1)
        final = jnp.zeros_like(xf)
        for e in range(N_EXPERTS):
            y = geglu(xf, W1[e], W2[e], W3[e])
            final = final + jnp.where((idx == e)[:, None], y, 0.0)
        return (shared + final).reshape(B, T, C)
    x = L0_attn_x
    x = x + 0.5 * _L0_ffn_ref(_layernorm(x, axis=-1), L0_ffn_W_gate, L0_ffn_W1, L0_ffn_b1, L0_ffn_W2, L0_ffn_b2)
    x = x + _L0_attn_ref(_layernorm(x, axis=-1), L0_attn_ln_gamma, L0_attn_ln_beta, L0_attn_in_proj_w, L0_attn_conv_w, L0_attn_conv_b, L0_attn_x_proj_w, L0_attn_dt_proj_w, L0_attn_dt_proj_b, L0_attn_A_log, L0_attn_D, L0_attn_out_proj_w, L0_attn_glu_w, L0_attn_glu_b)
    x = x + 0.5 * _L0_ffn_ref(_layernorm(x, axis=-1), L0_ffn_W_gate, L0_ffn_W1, L0_ffn_b1, L0_ffn_W2, L0_ffn_b2)
    x = x + 0.5 * _L1_ffn_ref(_layernorm(x, axis=-1), L1_ffn_w1s, L1_ffn_w2s, L1_ffn_w3s, L1_ffn_W1, L1_ffn_W2, L1_ffn_W3, L1_ffn_Wg)
    x = x + _L1_attn_ref(_layernorm(x, axis=-1), L1_attn_Wqkv, L1_attn_bqkv, L1_attn_Wout, L1_attn_bout)
    x = x + 0.5 * _L1_ffn_ref(_layernorm(x, axis=-1), L1_ffn_w1s, L1_ffn_w2s, L1_ffn_w3s, L1_ffn_W1, L1_ffn_W2, L1_ffn_W3, L1_ffn_Wg)
    return x

_drawn_inputs = setup_inputs


def setup_inputs(seed=0):
    import zlib

    import numpy as np

    out = dict(_drawn_inputs(seed))
    spreads = {'L0_attn_ln_gamma': (1.0, 0.2),
     'L0_attn_ln_beta': (0.0, 0.1),
     'L0_attn_conv_b': (0.0, 0.1),
     'L0_attn_D': (1.0, 0.2),
     'L0_attn_glu_b': (0.0, 0.1),
     'L1_attn_bqkv': (0.0, 0.1),
     'L1_attn_bout': (0.0, 0.1)}
    factors = {}
    for name, (base, spread) in spreads.items():
        noise = np.random.default_rng([zlib.crc32(name.encode()), seed]).standard_normal(out[name].shape)
        drawn = base * np.exp(spread * noise) if base else spread * noise
        out[name] = jnp.asarray(drawn.astype(out[name].dtype))
    for name, factor in factors.items():
        out[name] = (out[name] * factor).astype(out[name].dtype)
    return out
```

```python
from contextlib import ExitStack

import numpy as np
import concourse.bass as bass
from concourse import mybir

F32 = mybir.dt.float32
F32R = mybir.dt.float32r
ALU = mybir.AluOpType
ACT = mybir.ActivationFunctionType
AX = mybir.AxisListType

NSEQ, SEQ, D = 8, 512, 128
P = 128
NT = SEQ // P
EPS = 1e-5
E = 8
HID = 512
HC = HID // P
INNER, NST, RANK, TAPS = 256, 16, 8, 4
NH = INNER // P
HEADS, WIN = 16, 64
HD = D // HEADS
HG = 4
QB = 32
PAD = WIN // 2
KW = 96

ENGINES = ("pe", "act", "dve", "pool", "sp")
HEADROOM = 1 << 14


class Sems:

    def __init__(self, nc, ctx):
        self.nc, self.ctx = nc, ctx
        self.sem = {e: ctx.enter_context(nc.semaphore("done_" + e)) for e in ENGINES}
        self.at = {e: HEADROOM for e in ENGINES}
        self.started = False

    def dma(self, name):
        if name not in self.sem:
            self.sem[name] = self.ctx.enter_context(self.nc.semaphore("dma_" + name))
            self.at[name] = HEADROOM
        return self.sem[name]


class Steps:

    def __init__(self):
        self.steps = []

    def add(self, engine, name, emit, after=()):
        self.steps.append((engine, name, emit, after.split() if isinstance(after, str) else list(after), False))

    def dma(self, name, emit, after="", engine="sp"):
        self.steps.append((engine, name, emit, after.split(), True))

    def run(self, nc, sems, count=None):
        place, per, new = {}, {e: 0 for e in ENGINES}, []
        for engine, name, _, _, is_dma in self.steps:
            assert name not in place, name
            if is_dma:
                if name not in sems.sem:
                    sems.dma(name)
                    new.append(name)
                place[name], per[name] = (name, 16), 16
            else:
                per[engine] += 1
                place[name] = (engine, per[engine])
        new_engines, sems.started = not sems.started, True
        base = dict(sems.at)

        def emit_all(engine, eng, i):
            waited = {}
            for who, name, emit, after, is_dma in self.steps:
                if who != engine:
                    continue
                for a in after:
                    what, _, lag = a.partition("@")
                    s, k = place[what]
                    rel = k - int(lag or 0) * per[s]
                    if waited.get(s, -HEADROOM) >= rel:
                        continue
                    waited[s] = rel
                    eng.wait_ge(sems.sem[s], base[s] + rel if i is None else i * per[s] + (base[s] + rel))
                emit(eng, i).then_inc(sems.sem[name if is_dma else engine], 16 if is_dma else 1)

        def stream(engine):
            def body(eng):
                if new_engines:
                    eng.sem_inc(sems.sem[engine], HEADROOM)
                if engine == "sp":
                    for n in new:
                        eng.sem_inc(sems.sem[n], HEADROOM)
                if count is None:
                    emit_all(engine, eng, None)
                elif any(s[0] == engine for s in self.steps):
                    with eng.Fori(0, count) as i:
                        emit_all(engine, eng, i)
                if engine == "sp":
                    for s in self.steps:
                        if s[4]:
                            eng.wait_ge(sems.sem[s[1]], base[s[1]] + 16 * (count or 1))
            return body

        with nc.Block() as block:
            block.sync(stream("sp"))
            block.gpsimd(stream("pool"))
            block.scalar(stream("act"))
            block.vector(stream("dve"))
            block.tensor(stream("pe"))
        for s, n in per.items():
            sems.at[s] = base[s] + n * (count or 1)


def merge(main, side):
    out, n, m = [], len(main.steps), len(side.steps)
    j = 0
    for k, s in enumerate(main.steps):
        out.append(s)
        while j < m and (j + 1) * n <= (k + 1) * m:
            out.append(side.steps[j])
            j += 1
    out += side.steps[j:]
    main.steps = out
    return main


def tokens(dram, g):
    return dram[bass.ds(g * SEQ, SEQ), :].rearrange("(k p) d -> p k d", p=P)


def group_of(i, par, ahead=0):
    if i is None:
        return par
    g = i * 2 + (par + ahead)
    if par + ahead >= 2:
        g = (i * 2 + 2) % NSEQ
    return g


def layernorm(st, n, src, dst, T, after, write_after=""):
    stats, mv, sd, rs = T["stats"], T["mv"], T["sd"], T["rs"]

    def bn(eng, i):
        for k in range(NT):
            x = eng.bn_stats(stats[:, k, :], src[:, k, :])
        return x

    def agg(eng, i):
        eng.memset(T["tick"][:], 0.0)
        for k in range(NT):
            x = eng.bn_aggr(mv[:, k, :], stats[:, k, :])
        return x

    def norm(eng, i):
        for k in range(NT):
            x = eng.tensor_scalar(dst[:, k, :], src[:, k, :], mv[:, k, 0:1], rs[:, k:k + 1], ALU.subtract, ALU.mult)
        return x

    st.add("dve", n + ".stats", bn, after)
    st.add("dve", n + ".mv", agg, n + ".stats")
    st.add("act", n + ".sd", lambda eng, i: eng.activation(sd[:], mv[:, :, 1], ACT.Sqrt, bias=T["eps"][:, 0:1]), n + ".mv")
    st.add("dve", n + ".rs", lambda eng, i: eng.reciprocal(rs[:], sd[:]), n + ".sd")
    st.add("dve", n + ".out", norm, n + ".rs " + write_after)


def ln_tiles(sb):
    return dict(stats=sb("stats", [P, NT, 6]), mv=sb("mv", [P, NT, 2]), sd=sb("sd", [P, NT]), rs=sb("rs", [P, NT]), tick=sb("tick", [P, 1]))


def transposes(out, src, ident, n=NT):
    def emit(eng, i):
        for k in range(n):
            x = eng.transpose(out[:, k * P:(k + 1) * P], src[:, k, :], ident[:])
        return x
    return emit


def split_load(st, name, dram, raw, hi, lo, free=""):
    st.dma(name + ".ld", lambda eng, i: eng.dma_start(raw, dram), free)
    st.add("act", name + ".hi", lambda eng, i: eng.copy(hi, raw), name + ".ld")
    st.add("dve", name + ".lo", lambda eng, i: eng.tensor_tensor(lo, raw, hi.bitcast(F32), ALU.subtract), name + ".hi")


def three(eng, out, ahi, alo, bhi, blo, start, stop, skip=False):
    eng.matmul(out, ahi, bhi, start=start, stop=False, skip_group_check=skip)
    eng.matmul(out, ahi, blo, start=False, stop=False, skip_group_check=skip)
    return eng.matmul(out, alo, bhi, start=False, stop=stop, skip_group_check=skip)


def ffn(nc, sems, C, bank, xin, xout, w, gated):
    NE = E + 1 if gated else E
    NU = 2 if gated else 1
    with ExitStack() as ctx:
        def sb(name, shape, dt=F32):
            return ctx.enter_context(nc.sbuf_tensor(name + w["tag"], shape, dt))

        T = ln_tiles(sb)
        T["eps"] = C["eps"]
        up_hi = [sb(f"up_hi{u}", [P, NE, HID], F32R) for u in range(NU)]
        up_lo = [sb(f"up_lo{u}", [P, NE, HID], F32R) for u in range(NU)]
        dn_hi = sb("dn_hi", [P, NE, HC, D], F32R)
        dn_lo = sb("dn_lo", [P, NE, HC, D], F32R)
        wg_raw, wg_hi, wg_lo = sb("wg_raw", [P, E]), sb("wg_hi", [P, E], F32R), sb("wg_lo", [P, E], F32R)
        if not gated:
            b1, b1_rows = sb("b1", [P, E, HC]), sb("b1_rows", [E * HC, P])
            b2 = sb("b2", [E, D])
        xp = sb("xp", [P, NT, D])
        xn = sb("xn", [P, NT, D])
        xT_hi = [sb(f"xT_hi{p}", [P, SEQ], F32R) for p in range(2)]
        xT_lo = [sb(f"xT_lo{p}", [P, SEQ], F32R) for p in range(2)]
        lg = sb("lg", [P, NT, E])
        top = sb("top", [P, NT, 8])
        sel = sb("sel", [P, NT, E])
        ex = sb("ex", [P, NT, E])
        den = sb("den", [P, NT])
        mk = [sb(f"mk{p}", [P, NT, NE]) for p in range(2)]
        mkT = sb("mkT", [E, SEQ])
        acc = [sb(f"acc{p}", [P, NT, D]) for p in range(2)]
        NR = 2
        gel = [sb(f"gel{r}", [P, SEQ]) for r in range(NR)] if gated else None
        hf = [sb(f"hf{r}", [P, SEQ]) for r in range(NR)]
        h_hi = [sb(f"h_hi{r}", [P, SEQ], F32R) for r in range(NR)]
        h_lo = [sb(f"h_lo{r}", [P, SEQ], F32R) for r in range(NR)]
        HB = bank[0:4]
        YB = bank[4:6]
        TB, GB = bank[6], bank[7]

        st = Steps()
        raws = [hf[0], hf[1], gel[0], gel[1]] if gated else [hf[0], hf[1]]
        users, n = ["" for _ in raws], 0
        for u in range(NU):
            for e in range(NE):
                r = n % len(raws)
                split_load(st, f"w{n}", w["up"][u](e), raws[r][:], up_hi[u][:, e, :], up_lo[u][:, e, :], users[r])
                users[r] = f"w{n}.lo"
                n += 1
        for e in range(NE):
            r = n % len(raws)
            raw = raws[r][:].rearrange("p (c d) -> p c d", c=HC)
            split_load(st, f"w{n}", w["down"](e), raw, dn_hi[:, e, :, :], dn_lo[:, e, :, :], users[r])
            users[r] = f"w{n}.lo"
            n += 1
        split_load(st, "wg", w["gate"], wg_raw[:], wg_hi[:], wg_lo[:])
        if not gated:
            st.dma("b1.ld", lambda eng, i: eng.dma_start(b1_rows[:], w["b1"]))
            st.dma("b2.ld", lambda eng, i: eng.dma_start(b2[:], w["b2"]))
            st.add("pe", "b1.T", lambda eng, i: eng.transpose(GB[:, 0:E * HC], b1_rows[:], C["ident"][0:E * HC, 0:E * HC]), "b1.ld")
            st.add("dve", "b1", lambda eng, i: eng.tensor_copy(b1[:].rearrange("p e c -> p (e c)"), GB[:, 0:E * HC]), "b1.T")

        def prep(st, par, ahead, q):
            n = f"p{q}"
            last = lambda name: "" if ahead == 0 else name
            prev = 1 - q
            st.dma(f"{n}.x", lambda eng, i: eng.dma_start(xp[:], tokens(xin, group_of(i, par, ahead))),
                   last(f"p{prev}.ln.out" + ("@1" if q == 1 else "")))
            layernorm(st, n + ".ln", xp, xn, T, f"{n}.x", last(f"p{prev}.T" + ("@1" if q == 1 else "")))
            st.add("pe", n + ".T", transposes(TB, xn, C["ident"]), n + ".ln.out " + last(f"p{prev}.xlo" + ("@1" if q == 1 else "")))
            free = last(f"h{q}.last" + ("@1" if q == 1 else ""))
            st.add("act", n + ".xhi", lambda eng, i: eng.copy(xT_hi[q][:], TB[:]), n + ".T " + free)
            st.add("dve", n + ".xlo", lambda eng, i: eng.tensor_tensor(xT_lo[q][:], TB[:], xT_hi[q][:].bitcast(F32), ALU.subtract), n + ".xhi")

            def gate(eng, i):
                for k in range(NT):
                    t = slice(k * P, (k + 1) * P)
                    x = three(eng, GB[:, k * E:(k + 1) * E], xT_hi[q][:, t], xT_lo[q][:, t], wg_hi[:], wg_lo[:], True, True)
                return x
            st.add("pe", n + ".gate", gate, n + ".xlo " + last(f"p{prev}.lg" + ("@1" if q == 1 else "")) + ("" if gated or ahead == 0 else f" b{prev}.acc"))
            st.add("dve", n + ".lg", lambda eng, i: eng.tensor_copy(lg[:], GB[:, 0:NT * E].rearrange("p (k e) -> p k e", e=E)), n + ".gate")

            def top8(eng, i):
                eng.memset(T["tick"][:], 0.0)
                for k in range(NT):
                    x = eng.max(top[:, k, :], lg[:, k, :])
                return x
            st.add("dve", n + ".top", top8, n + ".lg")
            wfree = last(f"acc{q}.last" + ("@1" if q == 1 else ""))
            if gated:
                st.add("dve", n + ".sel", lambda eng, i: eng.tensor_tensor(sel[:], lg[:], top[:, :, 0:1].to_broadcast([P, NT, E]), ALU.is_ge), n + ".top")
                st.add("dve", n + ".ex", lambda eng, i: eng.tensor_tensor(ex[:], sel[:], C["pow2"][:, None, :].to_broadcast([P, NT, E]), ALU.mult), n + ".sel")
                st.add("dve", n + ".den", lambda eng, i: eng.reduce_sum(den[:], ex[:], AX.X), n + ".ex")
                st.add("dve", n + ".step", lambda eng, i: eng.tensor_tensor(ex[:], den[:, :, None].to_broadcast([P, NT, E]), C["pow2"][:, None, :].to_broadcast([P, NT, E]), ALU.is_ge), n + ".den")
                st.add("dve", n + ".half", lambda eng, i: eng.tensor_scalar(sel[:], ex[:], 0.5, None, ALU.mult), n + ".step " + wfree)
                st.add("dve", n + ".m0", lambda eng, i: eng.tensor_copy(mk[q][:, :, 0:1], sel[:, :, 0:1]), n + ".half")
                st.add("dve", n + ".mk", lambda eng, i: eng.tensor_tensor(mk[q][:, :, 1:E], sel[:, :, 1:E], sel[:, :, 0:E - 1], ALU.subtract), n + ".m0")
            else:
                st.add("dve", n + ".sel", lambda eng, i: eng.tensor_tensor(sel[:], lg[:], top[:, :, 1:2].to_broadcast([P, NT, E]), ALU.is_ge), n + ".top")
                st.add("dve", n + ".sub", lambda eng, i: eng.tensor_tensor(lg[:], lg[:], top[:, :, 0:1].to_broadcast([P, NT, E]), ALU.subtract), n + ".sel")
                st.add("act", n + ".exp", lambda eng, i: eng.activation(ex[:], lg[:], ACT.Exp), n + ".sub")
                st.add("dve", n + ".pick", lambda eng, i: eng.tensor_tensor(ex[:], ex[:], sel[:], ALU.mult), n + ".exp")
                st.add("dve", n + ".sum", lambda eng, i: eng.reduce_sum(den[:], ex[:], AX.X), n + ".pick")
                st.add("dve", n + ".rec", lambda eng, i: eng.reciprocal(den[:], den[:]), n + ".sum")
                st.add("dve", n + ".wsum", lambda eng, i: eng.tensor_tensor(ex[:], ex[:], den[:, :, None].to_broadcast([P, NT, E]), ALU.mult), n + ".rec")
                st.add("dve", n + ".mk", lambda eng, i: eng.tensor_scalar(mk[q][:], ex[:], 0.5 / E, None, ALU.mult), n + ".wsum " + wfree)

        if gated:
            for q in range(2):
                st.add("dve", f"shared{q}", lambda eng, i, q=q: eng.memset(mk[q][:, :, E:E + 1], 0.5))
        pre = Steps()
        prep(pre, 0, 0, 0)
        pre.steps = [(a, b, c, d + ((["wg.lo"] + ([] if gated else ["b1"])) if b == "p0.gate" else []), f) for a, b, c, d, f in pre.steps]
        st.steps += pre.steps
        st.run(nc, sems)

        loop = Steps()
        for q in range(2):
            main, side = Steps(), Steps()
            jobs = [(e, c) for e in range(NE) for c in range(HC)]
            pn = f"p{q}.mk" + ("@1" if q == 0 else "")
            px = f"p{q}.xlo" + ("@1" if q == 0 else "")
            main.dma(f"acc{q}.x", lambda eng, i, q=q: eng.dma_start(acc[q][:], tokens(xin, group_of(i, q))), f"out{q}@1")
            if not gated:
                def mT(eng, i, q=q):
                    for k in range(NT):
                        x = eng.transpose(GB[0:E, k * P:(k + 1) * P], mk[q][:, k, :], C["ident"][:])
                    return x
                main.add("pe", f"b{q}.T", mT, pn + (f" b{1 - q}.acc" + ("@1" if q == 0 else "")))
                main.add("act", f"b{q}.mT", lambda eng, i: eng.copy(mkT[:], GB[0:E, :]), f"b{q}.T b{1 - q}.mm" + ("@1" if q == 0 else ""))

                def b2mm(eng, i):
                    for k in range(NT):
                        x = eng.matmul(GB[:, k * P:(k + 1) * P], mkT[:, k * P:(k + 1) * P], b2[:], start=True, stop=True)
                    return x
                main.add("pe", f"b{q}.mm", b2mm, f"b{q}.mT")
                main.add("dve", f"b{q}.acc", lambda eng, i, q=q: eng.tensor_tensor(acc[q][:], acc[q][:], GB[:].rearrange("p (k d) -> p k d", d=D), ALU.add), f"b{q}.mm acc{q}.x")

            def nm(kind, j, dj=0):
                k = j - dj
                if k >= 0:
                    return f"{kind}{q}.{k}"
                k += len(jobs)
                return f"{kind}{1 - q}.{k}" + ("@1" if q == 0 else "")

            nb = len(HB) // NU
            depth = 2 if gated else 2
            def up(j, q=q):
                e, c = jobs[j]
                def emit(eng, i):
                    for u in range(NU):
                        s = slice(c * P, (c + 1) * P)
                        x = three(eng, HB[(j % nb) * NU + u][:], up_hi[u][:, e, s], up_lo[u][:, e, s], xT_hi[q][:], xT_lo[q][:], True, True)
                    return x
                name = f"h{q}.last" if j == len(jobs) - 1 else f"h{q}.{j}"
                main.add("pe", name, emit, px + " " + rd(j, nb))
                r = j % NR
                hn = name
                if gated:
                    main.add("act", f"g{q}.{j}", lambda eng, i: eng.activation(gel[r][:], HB[(j % nb) * NU][:], ACT.Gelu), hn + " " + nm("f", j, NR))
                    main.add("dve", f"f{q}.{j}", lambda eng, i: eng.tensor_tensor(hf[r][:], gel[r][:], HB[(j % nb) * NU + 1][:], ALU.mult), f"g{q}.{j} " + nm("l", j, NR))
                    main.add("act", f"i{q}.{j}", lambda eng, i: eng.copy(h_hi[r][:], hf[r][:]), f"f{q}.{j} " + nm("y", j, NR))
                else:
                    b = b1[:, e, c:c + 1]
                    main.add("act", f"f{q}.{j}", lambda eng, i: eng.activation(hf[r][:], HB[j % nb][:], ACT.Relu, bias=b), hn + " " + nm("l", j, NR))
                    main.add("act", f"i{q}.{j}", lambda eng, i: eng.activation(h_hi[r][:], HB[j % nb][:], ACT.Relu, bias=b), nm("y", j, NR))
                main.add("dve", f"l{q}.{j}", lambda eng, i: eng.tensor_tensor(h_lo[r][:], hf[r][:], h_hi[r][:].bitcast(F32), ALU.subtract), f"i{q}.{j} f{q}.{j} " + nm("y", j, NR))

            def rd(j, nb):
                return nm("f" if gated else "i", j, nb)

            def down(j, q=q):
                e, c = jobs[j]
                r = j % NR
                Y = YB[e % 2]
                def emit(eng, i):
                    for k in range(NT):
                        t = slice(k * P, (k + 1) * P)
                        x = three(eng, Y[:, t], h_hi[r][:, t], h_lo[r][:, t], dn_hi[:, e, c, :], dn_lo[:, e, c, :],
                                  c == 0 and k == 0, c == HC - 1 and k == NT - 1, skip=True)
                    return x
                free = ""
                if c == 0:
                    ee = e - 2
                    if ee >= 0:
                        free = f"a{q}.{ee}"
                    else:
                        ee = NE + ee
                        if NE % 2:
                            ee = NE - 1 if e % 2 == 0 else NE - 2
                        free = (f"acc{1 - q}.last" if ee == NE - 1 else f"a{1 - q}.{ee}") + ("@1" if q == 0 else "")
                main.add("pe", f"y{q}.{j}", emit, f"l{q}.{j} i{q}.{j} " + free)
                if c == HC - 1:
                    def accum(eng, i):
                        for k in range(NT):
                            x = eng.scalar_tensor_tensor(acc[q][:, k, :], Y[:, k * P:(k + 1) * P], mk[q][:, k, e:e + 1], acc[q][:, k, :], ALU.mult, ALU.add)
                        return x
                    prev = (f"acc{q}.x" + ("" if gated else f" b{q}.acc")) if e == 0 else f"a{q}.{e - 1}"
                    main.add("dve", f"acc{q}.last" if e == NE - 1 else f"a{q}.{e}", accum, f"y{q}.{j} {pn} " + prev)

            LEAD = 2
            for j in range(len(jobs) + LEAD):
                if j < len(jobs):
                    up(j)
                if j >= LEAD:
                    down(j - LEAD)
            main.dma(f"out{q}", lambda eng, i, q=q: eng.dma_start(tokens(xout, group_of(i, q)), acc[q][:]), f"acc{q}.last")
            prep(side, q, 1, 1 - q)
            cut = len(main.steps) * 3 // 4
            head, tail = Steps(), main.steps[cut:]
            k0 = 12
            head.steps = main.steps[k0:cut]
            loop.steps += main.steps[:k0] + merge(head, side).steps + tail
        loop.run(nc, sems, count=NSEQ // 2)


def consts(nc, sems, sb):
    C = dict(ident=sb("ident", [P, P]), eps=sb("eps", [P, 1]), one=sb("one", [P, 1]), pow2=sb("pow2", [P, E]))
    st = Steps()
    st.add("pool", "c.id0", lambda eng, i: eng.memset(C["ident"][:], 0.0))
    st.add("pool", "c.id", lambda eng, i: eng.affine_select(out=C["ident"][:], in_=C["ident"][:], compare_op=ALU.not_equal, fill=1.0,
                                                          base=0, pattern=[[-1, P]], channel_multiplier=1), "c.id0")
    st.add("pool", "c.one", lambda eng, i: eng.memset(C["one"][:], 1.0))
    st.add("pool", "c.eps", lambda eng, i: eng.memset(C["eps"][:], EPS))

    def powers(eng, i):
        for e in range(E):
            x = eng.memset(C["pow2"][:, e:e + 1], float(1 << (E - 1 - e)))
        return x
    st.add("pool", "c.pow2", powers)
    st.run(nc, sems)
    return C


def ffn0_weights(a):
    return dict(tag="_f0", up=[lambda e: a["L0_ffn_W1"][e]], down=lambda e: a["L0_ffn_W2"][e].rearrange("(c p) d -> p c d", p=P),
                gate=a["L0_ffn_W_gate"], b1=a["L0_ffn_b1"].rearrange("e (c p) -> (e c) p", p=P), b2=a["L0_ffn_b2"])


def ffn1_weights(a):
    def pick(shared, routed):
        return lambda e: a[routed][e] if e < E else a[shared]
    return dict(tag="_f1", up=[pick("L1_ffn_w1s", "L1_ffn_W1"), pick("L1_ffn_w2s", "L1_ffn_W2")],
                down=lambda e: pick("L1_ffn_w3s", "L1_ffn_W3")(e).rearrange("(c p) d -> p c d", p=P), gate=a["L1_ffn_Wg"])


def mamba(nc, sems, C, bank, xin, xout, a):
    with ExitStack() as ctx:
        def sb(name, shape, dt=F32):
            return ctx.enter_context(nc.sbuf_tensor(name + "_m", shape, dt))

        def two(name, shape, dt=F32):
            return [sb(name + str(p), shape, dt) for p in range(2)]

        T = ln_tiles(sb)
        T["eps"] = C["eps"]
        w_in = sb("w_in", [P, 2 * INNER])
        w_b = sb("w_b", [P, NH, 64])
        w_c = sb("w_c", [P, NH, 64])
        w_dt = sb("w_dt", [P, NH, RANK])
        w_dt2 = sb("w_dt2", [RANK, INNER])
        w_out = sb("w_out", [P, NH, D])
        w_glu = sb("w_glu", [P, 2 * D])
        b_glu = sb("b_glu", [1, 2 * D])
        ones = sb("ones", [1, P])
        rows = sb("rows", [64, P])
        cols = sb("cols", [P, 64])
        a_log = sb("a_log", [P, NH, NST])
        a_neg = sb("a_neg", [P, NH, NST])
        conv_w = sb("conv_w", [P, NH, TAPS])
        diag = sb("diag", [P, NH, TAPS, P])
        sel = sb("sel", [64, NST, P], F32R)
        sel_f = sb("sel_f", [64, NST, P])
        xp = sb("xp", [P, NT, D])
        xn = sb("xn", [P, NT, D])
        xm = sb("xm", [P, NT, D])
        skip = two("skip", [P, NT, D])
        hT = sb("hT", [P, SEQ])
        xi = sb("xi", [P, NH, TAPS - 1 + SEQ])
        u = two("u", [P, NH, SEQ])
        sz = two("sz", [P, NH, SEQ])
        bp = two("bp", [64, SEQ], F32R)
        cp = two("cp", [64, SEQ], F32R)
        dtr = sb("dtr", [RANK, SEQ])
        v = sb("v", [P, SEQ])
        ab = sb("ab", [P, SEQ])
        dt = two("dt", [P, NH, SEQ])
        du = two("du", [P, NH, SEQ])
        RA = 3
        da = [sb(f"da{r}", [P, SEQ]) for r in range(RA)]
        db = [sb(f"db{r}", [P, SEQ]) for r in range(2)]
        hs = [sb(f"hs{r}", [P, SEQ]) for r in range(2)]
        ph = [sb(f"ph{r}", [P, SEQ]) for r in range(3)]
        y2 = [sb(f"y2{r}", [P, SEQ]) for r in range(2)]
        gT = sb("gT", [P, SEQ])
        sg = sb("sg", [P, NT, D])
        o = two("o", [P, NT, D])
        SB, SC, SY, SX = bank[0:2], bank[2:4], bank[4:6], bank[6:8]
        GAM, BET, CB, DV, DB, = 0, 1, 2, 4, 6

        st = Steps()
        row = lambda ap: ap.rearrange("(h p) -> h p", p=P)
        for k, (nm, ap, n) in enumerate([("L0_attn_ln_gamma", GAM, 1), ("L0_attn_ln_beta", BET, 1), ("L0_attn_conv_b", CB, 2),
                                         ("L0_attn_D", DV, 2), ("L0_attn_dt_proj_b", DB, 2)]):
            st.dma(f"mv{k}", lambda eng, i, nm=nm, ap=ap, n=n: eng.dma_start(rows[ap:ap + n, :], row(a[nm])))
        st.add("pe", "rowsT", lambda eng, i: eng.transpose(SX[0][:, 0:8], rows[0:8, :], C["ident"][0:8, 0:8]), "mv0 mv1 mv2 mv3 mv4")
        st.add("dve", "cols", lambda eng, i: eng.tensor_copy(cols[:, 0:8], SX[0][:, 0:8]), "rowsT")
        st.dma("mw0", lambda eng, i: eng.dma_start(w_in[:], a["L0_attn_in_proj_w"]))
        xw = a["L0_attn_x_proj_w"].rearrange("(h p) n -> p h n", p=P)
        st.add("pool", "z0", lambda eng, i: eng.memset(w_b[:], 0.0))
        st.add("pool", "z1", lambda eng, i: eng.memset(w_c[:], 0.0))
        st.dma("mw1", lambda eng, i: eng.dma_start(w_dt[:], xw[:, :, 0:RANK]))
        for k, (w, at, o0) in enumerate([(w_b, 0, RANK), (w_b, 32, RANK), (w_c, 0, RANK + NST), (w_c, 32, RANK + NST)]):
            st.dma(f"mx{k}", lambda eng, i, w=w, at=at, o0=o0: eng.dma_start(w[:, :, at:at + NST], xw[:, :, o0:o0 + NST]), "z0 z1")
        st.dma("mw2", lambda eng, i: eng.dma_start(w_dt2[:], a["L0_attn_dt_proj_w"]))
        st.dma("mw3", lambda eng, i: eng.dma_start(w_out[:], a["L0_attn_out_proj_w"].rearrange("(h p) n -> p h n", p=P)))
        st.dma("mw4", lambda eng, i: eng.dma_start(w_glu[:], a["L0_attn_glu_w"]))
        st.dma("mw5", lambda eng, i: eng.dma_start(b_glu[:], a["L0_attn_glu_b"].rearrange("(o n) -> o n", o=1)))
        st.dma("mw6", lambda eng, i: eng.dma_start(a_log[:], a["L0_attn_A_log"].rearrange("(h p) n -> p h n", p=P)))
        st.dma("mw7", lambda eng, i: eng.dma_start(conv_w[:], a["L0_attn_conv_w"].rearrange("(h p) n -> p h n", p=P)))
        st.add("pool", "z2", lambda eng, i: eng.memset(ones[:], 1.0))
        st.add("pool", "z3", lambda eng, i: eng.memset(xi[:, :, 0:TAPS - 1], 0.0))
        st.add("pool", "z4", lambda eng, i: eng.memset(sel_f[:], 0.0))
        for k, off in enumerate((0, 32)):
            st.add("pool", f"z5{k}", lambda eng, i, off=off: eng.affine_select(
                out=sel_f[:], in_=sel_f[:], compare_op=ALU.not_equal, fill=1.0, base=-off, pattern=[[-1, NST], [0, P]],
                channel_multiplier=1), "z4" if k == 0 else "z50")
        st.add("dve", "sel", lambda eng, i: eng.tensor_copy(sel[:], sel_f[:]), "z51")
        st.add("act", "a.exp", lambda eng, i: eng.activation(a_neg[:], a_log[:], ACT.Exp), "mw6")
        st.add("dve", "a.neg", lambda eng, i: eng.tensor_scalar(a_neg[:], a_neg[:], -1.0, None, ALU.mult), "a.exp")

        def taps(eng, i):
            for h in range(NH):
                for k in range(TAPS):
                    x = eng.tensor_scalar(diag[:, h, k, :], C["ident"][:], conv_w[:, h, k:k + 1], None, ALU.mult)
            return x
        st.add("dve", "diag", taps, "mw7")

        def prep(st, par, ahead, q):
            n = f"p{q}"
            last = lambda name: "" if ahead == 0 else name
            back = "@1" if q == 1 else ""
            prev = f"p{1 - q}"
            g = lambda i: group_of(i, par, ahead)
            free = last(f"fin{q}" + back)
            st.dma(n + ".x", lambda eng, i: eng.dma_start(xp[:], tokens(xin, g(i))), last(f"{prev}.skip{back}"))
            layernorm(st, n + ".ln", xp, xn, T, n + ".x", last(f"{prev}.skip{back}"))
            st.add("dve", n + ".skip", lambda eng, i: eng.tensor_tensor(skip[q][:], xp[:], xn[:], ALU.add), n + ".ln.out " + free)
            layernorm(st, n + ".l2", xn, xm, T, n + ".ln.out", last(f"{prev}.T{back}"))
            st.add("pe", n + ".T", transposes(SX[0], xm, C["ident"]), n + ".l2.out " + last(f"{prev}.spl1{back}"))
            st.add("dve", n + ".h", lambda eng, i: eng.tensor_scalar(hT[:], SX[0][:], cols[:, GAM:GAM + 1], cols[:, BET:BET + 1], ALU.mult, ALU.add),
                   n + ".T " + last(f"{prev}.z1{back}"))
            for c in range(2 * NH):
                nm = f"{n}.in{c}"
                X = SX[(c + 1) % 2]
                before = f"{n}.h" if c < 2 else f"{n}.e{c - 2}"
                st.add("pe", nm, lambda eng, i, X=X, c=c: eng.matmul(X[:], w_in[:, c * P:(c + 1) * P], hT[:], start=True, stop=True),
                       before + f" {n}.h" + ("" if c else last(f" {prev}.v1{back}")))
                if c < NH:
                    st.add("act", f"{n}.e{c}", lambda eng, i, X=X, c=c: eng.copy(xi[:, c, TAPS - 1:], X[:]), nm + last(f" {prev}.conv{c}{back}"))
                else:
                    st.add("act", f"{n}.e{c}", lambda eng, i, X=X, c=c: eng.activation(sz[q][:, c - NH, :], X[:], ACT.Silu), nm + " " + free)
            st.steps[-1] = (st.steps[-1][0], st.steps[-1][1]) + st.steps[-1][2:]
            st.add("act", n + ".z1", lambda eng, i: eng.copy(T["actick"][:], C["eps"][:]), f"{n}.in3")
            for h in range(NH):
                X = SX[(h + 1) % 2]

                def conv(eng, i, h=h, X=X):
                    for k in range(TAPS):
                        x = eng.matmul(X[:], diag[:, h, k, :], xi[:, h, k:k + SEQ], start=k == 0, stop=k == TAPS - 1)
                    return x
                st.add("pe", f"{n}.conv{h}", conv, f"{n}.e{h} {n}.e{h + 2}")
                st.add("act", f"{n}.u{h}", lambda eng, i, h=h, X=X: eng.activation(u[q][:, h, :], X[:], ACT.Silu, bias=cols[:, CB + h:CB + h + 1]),
                       f"{n}.conv{h} " + free)

            def proj(X, w, m):
                def emit(eng, i):
                    for h in range(NH):
                        x = eng.matmul(X[0:m, :], w[:, h, :], u[q][:, h, :], start=h == 0, stop=h == NH - 1)
                    return x
                return emit
            st.add("pe", n + ".dtr", proj(SX[0], w_dt, RANK), f"{n}.u0 {n}.u1")
            st.add("act", n + ".dtr.s", lambda eng, i: eng.copy(dtr[:], SX[0][0:RANK, :]), n + ".dtr " + last(f"{prev}.dt1{back}"))
            for k, (w, dst) in enumerate(((w_b, bp), (w_c, cp))):
                X = SX[(k + 1) % 2]
                st.add("pe", f"{n}.bc{k}", proj(X, w, 64), f"{n}.u0 {n}.u1" + (f" {n}.dtr.s" if k else ""))
                st.add("act", f"{n}.sph{k}", lambda eng, i, X=X, dst=dst: eng.copy(dst[q][:], X[0:64, :]), f"{n}.bc{k} " + free)
                st.add("dve", f"{n}.spl{k}", lambda eng, i, X=X, dst=dst: eng.tensor_tensor(dst[q][32:64, :], X[32:64, :], dst[q][32:64, :].bitcast(F32), ALU.subtract),
                       f"{n}.sph{k}")
            for h in range(NH):
                X = SX[(h + 1) % 2]
                bias = cols[:, DB + h:DB + h + 1]
                st.add("pe", f"{n}.dt{h}", lambda eng, i, h=h, X=X: eng.matmul(X[:], w_dt2[:, h * P:(h + 1) * P], dtr[:], start=True, stop=True),
                       f"{n}.dtr.s {n}.spl0 {n}.spl1")
                vold = f" {n}.sp{h - 1}" if h else last(f" {prev}.sp1{back}")
                st.add("act", f"{n}.v{h}", lambda eng, i, X=X, bias=bias: eng.activation(v[:], X[:], ACT.Identity, bias=bias), f"{n}.dt{h}" + vold)
                st.add("act", f"{n}.a{h}", lambda eng, i: eng.activation(ab[:], v[:], ACT.Abs), f"{n}.v{h}")
                st.add("act", f"{n}.x{h}", lambda eng, i: eng.activation(ab[:], ab[:], ACT.Exp, scale=-1.0), f"{n}.a{h}")
                st.add("act", f"{n}.l{h}", lambda eng, i: eng.activation(ab[:], ab[:], ACT.Ln, bias=C["one"][:, 0:1]), f"{n}.x{h}")
                st.add("dve", f"{n}.sp{h}", lambda eng, i, h=h: eng.scalar_tensor_tensor(dt[q][:, h, :], v[:], 0.0, ab[:], ALU.max, ALU.add), f"{n}.l{h} " + free)
                st.add("dve", f"{n}.du{h}", lambda eng, i, h=h: eng.tensor_tensor(du[q][:, h, :], dt[q][:, h, :], u[q][:, h, :], ALU.mult), f"{n}.sp{h}")

        T["actick"] = sb("actick", [P, 1])
        pre = Steps()
        prep(pre, 0, 0, 0)
        needs = {"p0.h": ["cols"], "p0.in0": ["mw0"], "p0.u0": ["cols"], "p0.e0": ["z3"], "p0.conv0": ["diag"], "p0.dtr": ["mw1"],
                 "p0.bc0": ["mx0", "mx1", "mx2", "mx3"], "p0.dt0": ["mw2"], "p0.T": ["cols"], "p0.v0": ["cols"]}
        st.steps += [(e, nm, f, list(af) + needs.get(nm, []), d) for e, nm, f, af, d in pre.steps]
        st.run(nc, sems)

        loop = Steps()
        for q in range(2):
            main, side = Steps(), Steps()
            ready = f"p{q}.du1 p{q}.spl1 p{q}.spl0" if q else "p0.du1@1 p0.spl1@1 p0.spl0@1"
            jobs = [(n, h) for n in range(NST) for h in range(NH)]
            NJ = len(jobs)

            def nm(kind, j, dj, total):
                k = j - dj
                return f"{kind}{q}.{k}" if k >= 0 else f"{kind}{1 - q}.{k + total}" + ("@1" if q == 0 else "")

            def bcast(n, q=q):
                def emit(eng, i):
                    eng.matmul(SB[n % 2][:], sel[:, n, :], bp[q][:], start=True, stop=True)
                    return eng.matmul(SC[n % 2][:], sel[:, n, :], cp[q][:], start=True, stop=True)
                main.add("pe", f"bc{q}.{n}", emit, ready + " " + nm("ph", 2 * n + 1, 4, NJ))

            def ysum(j, q=q):
                n, h = jobs[j]
                y_free = "" if n else (f"yd{1 - q}.{h}" + ("@1" if q == 0 else ""))
                main.add("pe", f"ys{q}.{j}", lambda eng, i: eng.matmul(SY[h][:], C["ident"][:], ph[j % 3][:], start=n == 0, stop=n == NST - 1,
                                                                    skip_group_check=True),
                         f"ph{q}.{j} " + y_free)

            for j, (n, h) in enumerate(jobs):
                if j == 0:
                    bcast(0)
                if h == 0 and n + 1 < NST:
                    bcast(n + 1)
                main.add("act", f"da{q}.{j}", lambda eng, i, n=n, h=h, j=j: eng.activation(da[j % RA][:], dt[q][:, h, :], ACT.Exp, scale=a_neg[:, h, n:n + 1]),
                         ready + " " + nm("hs", j, RA, NJ)) if False else main.add(
                             "act", f"da{q}.{j}", (lambda n, h, j, q: lambda eng, i: eng.activation(da[j % RA][:], dt[q][:, h, :], ACT.Exp, scale=a_neg[:, h, n:n + 1]))(n, h, j, q),
                             ready + " " + nm("hs", j, RA, NJ))
                main.add("dve", f"db{q}.{j}", (lambda n, h, j, q: lambda eng, i: eng.tensor_tensor(db[j % 2][:], du[q][:, h, :], SB[n % 2][:], ALU.mult))(n, h, j, q),
                         f"bc{q}.{n}")
                main.add("dve", f"hs{q}.{j}", (lambda j: lambda eng, i: eng.tensor_tensor_scan(hs[j % 2][:], da[j % RA][:], db[j % 2][:], 0.0, ALU.mult, ALU.add))(j),
                         f"da{q}.{j} db{q}.{j}")
                main.add("dve", f"ph{q}.{j}", (lambda n, j: lambda eng, i: eng.tensor_tensor(ph[j % 3][:], hs[j % 2][:], SC[n % 2][:], ALU.mult))(n, j),
                         f"hs{q}.{j} " + nm("ys", j, 3, NJ))
                if j >= 1:
                    ysum(j - 1)
            ysum(NJ - 1)
            other = "@1" if q == 0 else ""
            for h in range(NH):
                main.add("dve", f"yd{q}.{h}", (lambda h, q: lambda eng, i: eng.scalar_tensor_tensor(y2[h][:], u[q][:, h, :], cols[:, DV + h:DV + h + 1], SY[h][:], ALU.mult, ALU.add))(h, q),
                         f"ys{q}.{NJ - NH + h} op{1 - q}{other}")
                main.add("dve", f"y2{q}.{h}", (lambda h, q: lambda eng, i: eng.tensor_tensor(y2[h][:], y2[h][:], sz[q][:, h, :], ALU.mult))(h, q), f"yd{q}.{h}")

            def outp(eng, i):
                for h in range(NH):
                    x = eng.matmul(SB[0][:], w_out[:, h, :], y2[h][:], start=h == 0, stop=h == NH - 1)
                return x
            main.add("pe", f"op{q}", outp, f"y2{q}.0 y2{q}.1 ph{q}.{NJ - 1}")
            main.add("act", f"gT{q}", lambda eng, i: eng.activation(gT[:], SB[0][:], ACT.Gelu), f"op{q} gl{1 - q}{other}")

            def glu(eng, i):
                for k in range(NT):
                    dst = (SC[0] if k < 2 else SC[1])[:, (k % 2) * 2 * D:(k % 2 + 1) * 2 * D]
                    eng.matmul(dst, gT[:, k * P:(k + 1) * P], w_glu[:], start=True, stop=False)
                    x = eng.matmul(dst, ones[:], b_glu[:], start=False, stop=True)
                return x
            main.add("pe", f"gl{q}", glu, f"gT{q}")
            for k2 in range(2):
                G = SC[k2][:].rearrange("p (k c) -> p k c", k=2)
                main.add("act", f"sg{q}.{k2}", (lambda G, k2: lambda eng, i: eng.activation(sg[:, 2 * k2:2 * k2 + 2, :], G[:, :, D:2 * D], ACT.Sigmoid))(G, k2),
                         f"gl{q} go{1 - q}.1{other}")
                main.add("dve", f"go{q}.{k2}", (lambda G, k2, q: lambda eng, i: eng.tensor_tensor(o[q][:, 2 * k2:2 * k2 + 2, :], G[:, :, 0:D], sg[:, 2 * k2:2 * k2 + 2, :], ALU.mult))(G, k2, q),
                         f"sg{q}.{k2} st{q}@1")
            main.add("dve", f"fin{q}", (lambda q: lambda eng, i: eng.tensor_tensor(o[q][:], o[q][:], skip[q][:], ALU.add))(q), f"go{q}.0 go{q}.1")
            main.dma(f"st{q}", (lambda q: lambda eng, i: eng.dma_start(tokens(xout, group_of(i, q)), o[q][:]))(q), f"fin{q}")
            prep(side, q, 1, 1 - q)
            cut = len(main.steps) * 3 // 4
            head = Steps()
            head.steps = main.steps[4:cut]
            loop.steps += main.steps[:4] + merge(head, side).steps + main.steps[cut:]
        fix = {"bc0.0": ["fin1@1", "gT1@1"], "bc1.0": ["fin0", "gT0"], "bc0.1": ["fin1@1"], "bc1.1": ["fin0"]}
        loop.steps = [(e, nm, f, list(af) + fix.get(nm, []), d) for e, nm, f, af, d in loop.steps]
        loop.run(nc, sems, count=NSEQ // 2)


def attention(nc, sems, C, bank, xin, xout, a):
    NB = SEQ // QB
    KP = SEQ + 2 * PAD
    BB = 4
    HB = NB // 2
    VW = HG * HD + 1
    with ExitStack() as ctx:
        def sb(name, shape, dt=F32):
            return ctx.enter_context(nc.sbuf_tensor(name + "_a", shape, dt))

        T = ln_tiles(sb)
        T["eps"] = C["eps"]
        w_q, w_k = sb("w_q", [P, HG, P]), sb("w_k", [P, HG, P])
        w_v, w_o = sb("w_v", [P, D]), sb("w_o", [P, D])
        b_rows, b_cols = sb("b_rows", [2 * HG, P]), sb("b_cols", [P, 2 * HG])
        b_v, b_o = sb("b_v", [1, D]), sb("b_o", [1, D])
        ones, valid = sb("ones", [1, P]), sb("valid", [1, KP])
        band = sb("band", [P, KW])
        own = sb("own", [P, HG * HD])
        fold = sb("fold", [P, QB])
        xp, xn = sb("xp", [P, NT, D]), sb("xn", [P, NT, D])
        xT = sb("xT", [P, KP])
        two = lambda name, shape: [sb(name + str(p), shape) for p in range(2)]
        qd = [[sb(f"qd{p}{g}", [P, NB, HG, QB]) for g in range(HG)] for p in range(2)]
        kT = [[sb(f"kT{p}{g}", [P, KP]) for g in range(HG)] for p in range(2)]
        vb = two("vb", [KW, NB, HG, VW])
        s = two("s", [P, NB, KW])
        mx = two("mx", [P, NB])
        pT = [sb(f"pT{r}", [KW, BB, P]) for r in range(3)]
        rc = two("rc", [P, HB])
        o1 = two("o1", [P, HB, HG * HD])
        oT = sb("oT", [P, SEQ])
        o = two("o", [P, NT, D])
        BS, BT, BO, BZ, BX = bank[0:2], bank[2:4], bank[4], bank[5], bank[6:8]

        st = Steps()
        wT = a["L1_attn_Wqkv"]
        heads = lambda w: w[:].rearrange("p g (r c) -> p (g r) c", r=HG)[:, :, 0:HD]
        st.add("pool", "z0", lambda eng, i: eng.memset(w_q[:], 0.0))
        st.add("pool", "z1", lambda eng, i: eng.memset(w_k[:], 0.0))
        st.add("pool", "z2", lambda eng, i: eng.memset(b_rows[:], 0.0))
        for k, w in enumerate((w_q, w_k)):
            st.dma(f"mx{k}", lambda eng, i, k=k, w=w: eng.dma_start(heads(w), wT[:, k * D:(k + 1) * D].rearrange("p (h c) -> p h c", c=HD)), f"z{k}")
            st.dma(f"mv{k}", lambda eng, i, k=k: eng.dma_start(b_rows[k * HG:(k + 1) * HG, :].rearrange("g (r c) -> g r c", r=HG)[:, :, 0:HD],
                                                             a["L1_attn_bqkv"][k * D:(k + 1) * D].rearrange("(g r c) -> g r c", g=HG, r=HG)), "z2")
        st.dma("mw0", lambda eng, i: eng.dma_start(w_v[:], wT[:, 2 * D:3 * D]))
        st.dma("mw1", lambda eng, i: eng.dma_start(w_o[:], a["L1_attn_Wout"]))
        st.dma("mw2", lambda eng, i: eng.dma_start(b_v[:], a["L1_attn_bqkv"][2 * D:3 * D].rearrange("(o n) -> o n", o=1)))
        st.dma("mw3", lambda eng, i: eng.dma_start(b_o[:], a["L1_attn_bout"].rearrange("(o n) -> o n", o=1)))
        st.add("pe", "bT", lambda eng, i: eng.transpose(BX[0][:, 0:2 * HG], b_rows[:], C["ident"][0:2 * HG, 0:2 * HG]), "mv0 mv1")
        st.add("dve", "b_cols", lambda eng, i: eng.tensor_copy(b_cols[:], BX[0][:, 0:2 * HG]), "bT")
        st.add("pool", "ones", lambda eng, i: eng.memset(ones[:], 1.0))
        st.add("pool", "v0", lambda eng, i: eng.memset(valid[:], 0.0))
        st.add("pool", "v1", lambda eng, i: eng.memset(valid[:, PAD:PAD + SEQ], 1.0), "v0")
        st.add("pool", "m0", lambda eng, i: eng.memset(band[:], 0.0))
        st.add("pool", "m1", lambda eng, i: eng.memset(own[:], 0.0))
        st.add("pool", "m2", lambda eng, i: eng.memset(fold[:], 0.0))

        def quadrants(name, emit, after):
            for r in range(HG):
                last = r == HG - 1
                st.add("pool", name if last else f"{name}.{r}", lambda eng, i, r=r: emit(eng, r, slice(32 * r, 32 * r + 32)), after if r == 0 else f"{name}.{r - 1}")
        quadrants("m3", lambda eng, r, p: eng.affine_select(out=band[p, :], in_=band[p, :], compare_op=ALU.is_ge, fill=-1e30, base=0,
                                                          pattern=[[1, KW]], channel_multiplier=-1), "m2")
        quadrants("m4", lambda eng, r, p: eng.affine_select(out=band[p, :], in_=band[p, :], compare_op=ALU.is_ge, fill=-1e30, base=WIN - 1,
                                                          pattern=[[-1, KW]], channel_multiplier=1), "m3")
        quadrants("m5", lambda eng, r, p: eng.memset(own[p, HD * r:HD * r + HD], 1.0), "m4")
        quadrants("m6", lambda eng, r, p: eng.affine_select(out=fold[p, :], in_=fold[p, :], compare_op=ALU.not_equal, fill=1.0, base=0,
                                                          pattern=[[-1, QB]], channel_multiplier=1), "m5")
        st.add("pool", "m7", lambda eng, i: eng.memset(xT[:, 0:PAD], 0.0), "m6")
        st.add("pool", "m8", lambda eng, i: eng.memset(xT[:, PAD + SEQ:], 0.0))

        def zeros(eng, i):
            for p in range(2):
                for g in range(HG):
                    eng.memset(kT[p][g][:, 0:PAD], 0.0)
                    eng.memset(kT[p][g][:, PAD + SEQ:], 0.0)
                x = eng.memset(vb[p][:, :, :, VW - 1:VW], 1.0)
            return x
        st.add("pool", "m9", zeros, "m8")

        def qzeros(eng, i):
            for p in range(2):
                for g in range(HG):
                    x = eng.memset(qd[p][g][:], 0.0)
            return x
        st.add("dve", "mq", qzeros)

        def prep(st, par, ahead, q):
            n = f"p{q}"
            last = lambda name: "" if ahead == 0 else name
            back = "@1" if q == 1 else ""
            prev = f"p{1 - q}"
            free = last(f"s.last{q}" + back)
            vfree = last(f"ot{q}.{HG - 1}.1" + back)
            st.dma(n + ".x", lambda eng, i: eng.dma_start(xp[:], tokens(xin, group_of(i, par, ahead))), last(f"{prev}.ln.out{back}"))
            layernorm(st, n + ".ln", xp, xn, T, n + ".x", last(f"{prev}.T{back}"))
            st.add("pe", n + ".T", transposes(BX[0], xn, C["ident"]), n + ".ln.out " + last(f"{prev}.v2{back}"))
            st.add("act", n + ".xT", lambda eng, i: eng.copy(xT[:, PAD:PAD + SEQ], BX[0][:]), n + ".T " + last(f"{prev}.vm3{back}"))
            units = [(w, g) for g in range(HG) for w in (0, 1)]
            readers = [n + ".xT", last(f"{prev}.v3{back}")]
            for k, (w, g) in enumerate(units):
                X = BX[k % 2]
                W = (w_q, w_k)[w]
                st.add("pe", f"{n}.m{k}", lambda eng, i, X=X, W=W, g=g: eng.matmul(X[:], W[:, g, :], xT[:, PAD:PAD + SEQ], start=True, stop=True),
                       f"{n}.xT {readers[k % 2]}")
                bias = b_cols[:, w * HG + g:w * HG + g + 1]
                if w == 0:
                    def evac(eng, i, X=X, g=g):
                        for r in range(HG):
                            p = slice(32 * r, 32 * r + 32)
                            x = eng.activation(qd[q][g][p, :, r, :], X[p, :].rearrange("p (b q) -> p b q", q=QB), ACT.Identity, bias=b_cols[p, g:g + 1])
                        return x
                    st.add("act", f"{n}.e{k}", evac, f"{n}.m{k} " + free)
                else:
                    st.add("dve", f"{n}.e{k}", lambda eng, i, X=X, g=g, bias=bias: eng.tensor_scalar(kT[q][g][:, PAD:PAD + SEQ], X[:], bias, None, ALU.add),
                           f"{n}.m{k} " + free)
                readers[k % 2] = f"{n}.e{k}"
            for k in range(NB // 4):
                X = BX[k % 2]

                def vals(eng, i, X=X, k=k):
                    for j in range(4):
                        b = 4 * k + j
                        keys = slice(b * QB, b * QB + KW)
                        eng.matmul(X[0:KW, j * D:(j + 1) * D], xT[:, keys], w_v[:], start=True, stop=False)
                        x = eng.matmul(X[0:KW, j * D:(j + 1) * D], valid[:, keys], b_v[:], start=False, stop=True)
                    return x
                st.add("pe", f"{n}.vm{k}", vals, readers[k % 2])
                st.add("act", f"{n}.v{k}", lambda eng, i, X=X, k=k: eng.copy(vb[q][:, 4 * k:4 * k + 4, :, 0:VW - 1], X[0:KW, :].rearrange("p (b g c) -> p b g c", b=4, g=HG)),
                       f"{n}.vm{k} " + vfree)
                readers[k % 2] = f"{n}.v{k}"

        pre = Steps()
        prep(pre, 0, 0, 0)
        needs = {"p0.m0": ["mx0", "mx1", "m8"], "p0.e0": ["b_cols", "mq"], "p0.e1": ["b_cols", "m9"], "p0.vm0": ["mw0", "mw2", "v1", "m8"], "p0.v0": ["m9"]}
        st.steps += [(e, nm, f, list(af) + needs.get(nm, []), d) for e, nm, f, af, d in pre.steps]
        st.run(nc, sems)

        loop = Steps()
        scale = float(1.0 / np.sqrt(np.float32(HD)))
        for q in range(2):
            main, side = Steps(), Steps()
            w1 = "" if q else "@1"
            ready = f"p{q}.e6{w1} p{q}.e7{w1}"
            main.dma(f"ox{q}", (lambda q: lambda eng, i: eng.dma_start(o[q][:], tokens(xin, group_of(i, q))))(q), f"st{q}@1")

            def before(g, kind):
                return f"{kind.format(q=q, g=g - 1)}" if g else f"{kind.format(q=1 - q, g=HG - 1)}{w1}"

            def before2(g, kind):
                return kind.format(q=q, g=g - 2) if g >= 2 else kind.format(q=1 - q, g=HG + g - 2) + w1

            def scores(g, q=q):
                S, M = s[g % 2], mx[g % 2]
                for c in range(NB // BB):
                    X = BS[c % 2]

                    def mm(eng, i, X=X, c=c):
                        for j in range(BB):
                            b = c * BB + j
                            x = eng.matmul(X[:, j * KW:(j + 1) * KW], qd[q][g][:, b, :, :].rearrange("p r q -> p (r q)"), kT[q][g][:, b * QB:b * QB + KW], start=True, stop=True)
                        return x
                    prev = f"sm{q}.{g}.{c - 2}" if c >= 2 else before(g, "sm{q}.{g}." + str(c + 2))
                    name = f"s.last{q}" if (g, c) == (HG - 1, NB // BB - 1) else f"sc{q}.{g}.{c}"
                    main.add("pe", name, mm, f"{ready} {prev}")
                    main.add("dve", f"sm{q}.{g}.{c}", lambda eng, i, X=X, c=c: eng.scalar_tensor_tensor(
                        S[:, c * BB:(c + 1) * BB, :], X[:, 0:BB * KW].rearrange("p (b k) -> p b k", k=KW), scale, band[:, None, :].to_broadcast([P, BB, KW]), ALU.mult, ALU.add),
                        name + " " + before2(g, "pt{q}.{g}.3"))
                main.add("dve", f"mx{q}.{g}", lambda eng, i: eng.reduce_max(M[:], S[:], AX.X), f"sm{q}.{g}.3")
                main.add("dve", f"sb{q}.{g}", lambda eng, i: eng.tensor_tensor(S[:], S[:], M[:, :, None].to_broadcast([P, NB, KW]), ALU.subtract), f"mx{q}.{g}")
                main.add("act", f"ex{q}.{g}", lambda eng, i: eng.activation(S[:], S[:], ACT.Exp), f"sb{q}.{g}")

            def outputs(g, q=q):
                S = s[g % 2]
                for c in range(NB // BB):
                    k = g * (NB // BB) + c
                    X, W = BT[c % 2], pT[k % 3]

                    def tr(eng, i, X=X, c=c):
                        for j in range(BB):
                            x = eng.transpose(X[0:KW, j * P:(j + 1) * P], S[:, c * BB + j, :], C["ident"][:])
                        return x
                    prev = f"pe{q}.{g}.{c - 2}" if c >= 2 else before(g, "pe{q}.{g}." + str(c + 2))
                    main.add("pe", f"pt{q}.{g}.{c}", tr, f"ex{q}.{g} {prev} op{1 - q}.r{w1}")
                    kk = k - 3
                    old = f"pv{q}.{kk // 4}.{kk % 4}" if kk >= 0 else f"pv{1 - q}.{(kk + 16) // 4}.{(kk + 16) % 4}{w1}"
                    main.add("act", f"pe{q}.{g}.{c}", lambda eng, i, X=X, W=W: eng.copy(W[:].rearrange("p b q -> p (b q)"), X[0:KW, :]), f"pt{q}.{g}.{c} {old}")
                    h = c // 2

                    def pv(eng, i, W=W, c=c):
                        for j in range(BB):
                            b = c * BB + j
                            at = (b % HB) * VW
                            x = eng.matmul(BO[:, at:at + VW], W[:, j, :], vb[q][:, b, g, :], start=True, stop=True)
                        return x
                    bo = (f"on{q}.{g}.0" if h else before(g, "on{q}.{g}.1"))
                    main.add("pe", f"pv{q}.{g}.{c}", pv, f"pe{q}.{g}.{c} {bo}")
                    if c % 2:
                        O = BO[:, 0:HB * VW].rearrange("p (b c) -> p b c", c=VW)
                        R, Z = rc[h], o1[h]
                        zold = before(g, "ot{q}.{g}." + str(h))
                        main.add("dve", f"rc{q}.{g}.{h}", lambda eng, i, O=O, R=R: eng.reciprocal(R[:], O[:, :, VW - 1]), f"pv{q}.{g}.{c}")
                        main.add("dve", f"on{q}.{g}.{h}", lambda eng, i, O=O, R=R, Z=Z: eng.tensor_tensor(Z[:], O[:, :, 0:VW - 1], R[:, :, None].to_broadcast([P, HB, HG * HD]), ALU.mult),
                                 f"rc{q}.{g}.{h} {zold}")
                        main.add("dve", f"om{q}.{g}.{h}", lambda eng, i, Z=Z: eng.tensor_tensor(Z[:], Z[:], own[:, None, :].to_broadcast([P, HB, HG * HD]), ALU.mult),
                                 f"on{q}.{g}.{h}")

                        def ot(eng, i, Z=Z, h=h):
                            for j in range(HB):
                                b = h * HB + j
                                x = eng.matmul(BZ[32 * g:32 * g + 32, b * QB:(b + 1) * QB], Z[:, j, :], fold[:], start=True, stop=True)
                            return x
                        main.add("pe", f"ot{q}.{g}.{h}", ot, f"om{q}.{g}.{h} oc{1 - q}{w1}")

            scores(0)
            for g in range(HG):
                if g + 1 < HG:
                    scores(g + 1)
                outputs(g)
            main.add("act", f"oc{q}", lambda eng, i: eng.copy(oT[:], BZ[:]), f"ot{q}.{HG - 1}.1 op{1 - q}{w1}")

            def proj(eng, i):
                for k in range(NT):
                    t = slice(k * P, (k + 1) * P)
                    eng.matmul(BT[0][:, t], oT[:, t], w_o[:], start=True, stop=False)
                    x = eng.matmul(BT[0][:, t], ones[:], b_o[:], start=False, stop=True)
                return x
            main.add("pe", f"op{q}", proj, f"oc{q} pe{q}.{HG - 1}.2")
            main.add("dve", f"op{q}.r", (lambda q: lambda eng, i: eng.tensor_tensor(o[q][:], o[q][:], BT[0][:].rearrange("p (k d) -> p k d", d=D), ALU.add))(q), f"op{q} ox{q}")
            main.dma(f"st{q}", (lambda q: lambda eng, i: eng.dma_start(tokens(xout, group_of(i, q)), o[q][:]))(q), f"op{q}.r")
            prep(side, q, 1, 1 - q)
            loop.steps += merge(main, side).steps
        loop.run(nc, sems, count=NSEQ // 2)


NAMES = ["L0_attn_x", "L0_attn_ln_gamma", "L0_attn_ln_beta", "L0_attn_in_proj_w", "L0_attn_conv_w", "L0_attn_conv_b",
         "L0_attn_x_proj_w", "L0_attn_dt_proj_w", "L0_attn_dt_proj_b", "L0_attn_A_log", "L0_attn_D", "L0_attn_out_proj_w",
         "L0_attn_glu_w", "L0_attn_glu_b", "L0_ffn_W_gate", "L0_ffn_W1", "L0_ffn_b1", "L0_ffn_W2", "L0_ffn_b2",
         "L1_attn_Wqkv", "L1_attn_bqkv", "L1_attn_Wout", "L1_attn_bout", "L1_ffn_w1s", "L1_ffn_w2s", "L1_ffn_w3s",
         "L1_ffn_W1", "L1_ffn_W2", "L1_ffn_W3", "L1_ffn_Wg"]
TRANSPOSED = ("L1_attn_Wqkv", "L1_attn_Wout")


def program(nc, a, out):
    with ExitStack() as ctx:
        sems = Sems(nc, ctx)
        C = consts(nc, sems, lambda name, shape, dt=F32: ctx.enter_context(nc.sbuf_tensor(name, shape, dt)))
        bank = [ctx.enter_context(nc.psum_tensor(f"bank{b}", [P, SEQ], F32)) for b in range(8)]
        x = [a["L0_attn_x"]] + [nc.dram_tensor(f"x{k}", [NSEQ * SEQ, D], F32, kind="Internal").ap() for k in range(1, 6)] + [out]
        f0, f1 = ffn0_weights(a), ffn1_weights(a)
        ffn(nc, sems, C, bank, x[0], x[1], f0, gated=False)
        mamba(nc, sems, C, bank, x[1], x[2], a)
        ffn(nc, sems, C, bank, x[2], x[3], f0 | {"tag": "_f0b"}, gated=False)
        ffn(nc, sems, C, bank, x[3], x[4], f1, gated=True)
        attention(nc, sems, C, bank, x[4], x[5], a)
        ffn(nc, sems, C, bank, x[5], x[6], f1 | {"tag": "_f1b"}, gated=True)


def kernel(**inputs):
    import concourse.bacc as bacc
    from concourse.bass_utils import run_bass_kernel_spmd

    nc = bacc.Bacc("TRN2", target_bir_lowering=False, num_devices=1)
    arrays, a = {}, {}
    for name in NAMES:
        v = np.asarray(inputs[name])
        if name == "L0_attn_x":
            v = v.reshape(NSEQ * SEQ, D)
        if name in TRANSPOSED:
            v = v.T
        v = np.ascontiguousarray(v)
        arrays["in_" + name] = v
        a[name] = nc.dram_tensor("in_" + name, v.shape, mybir.dt.from_np(v.dtype), kind="ExternalInput").ap()
    out = nc.dram_tensor("out_0", [NSEQ * SEQ, D], F32, kind="ExternalOutput").ap()
    program(nc, a, out)
    r = run_bass_kernel_spmd(nc, [arrays], core_ids=[0])
    return r.results[0]["out_0"].reshape(NSEQ, SEQ, D)
```

```python
from contextlib import ExitStack

import numpy as np
import concourse.bass as bass
from concourse import mybir

F32 = mybir.dt.float32
F32R = mybir.dt.float32r
ALU = mybir.AluOpType
ACT = mybir.ActivationFunctionType
AX = mybir.AxisListType

NSEQ, SEQ, D = 8, 512, 128
P = 128
NT = SEQ // P
EPS = 1e-5
E = 8
HID = 512
HC = HID // P
INNER, NST, RANK, TAPS = 256, 16, 8, 4
NH = INNER // P
HEADS, WIN = 16, 64
HD = D // HEADS
HG = 4
QB = 32
PAD = WIN // 2
KW = 96

ENGINES = ("pe", "act", "dve", "pool", "sp")
HEADROOM = 1 << 14


class Sems:

    def __init__(self, nc, ctx):
        self.nc, self.ctx = nc, ctx
        self.sem = {e: ctx.enter_context(nc.semaphore("done_" + e)) for e in ENGINES}
        self.at = {e: HEADROOM for e in ENGINES}
        self.started = False

    def dma(self, name, start):
        self.sem[name] = self.ctx.enter_context(self.nc.semaphore("dma_" + name))
        self.at[name] = start


class Steps:

    def __init__(self):
        self.steps = []

    def add(self, engine, name, emit, after=()):
        self.steps.append((engine, name, emit, after.split() if isinstance(after, str) else list(after), False))

    def dma(self, name, emit, after="", engine="sp"):
        self.steps.append((engine, name, emit, after.split(), True))


def run(nc, sems, before=None, loop=None, count=0, after=None):
    parts = [(p, n) for p, n in ((before, 1), (loop, count), (after, 1)) if p is not None]
    place, new, at = {}, [], dict(sems.at)
    per_part = []
    for part, n in parts:
        per, base = {}, {}
        looped = part is loop
        for engine, name, _, _, is_dma in part.steps:
            assert name not in place, name
            if is_dma:
                if name not in sems.sem:
                    sems.dma(name, 0 if engine == "pool" else HEADROOM)
                    at[name] = sems.at[name]
                    if engine != "pool":
                        new.append(name)
                s, k = name, 16
                per[s] = 16
            else:
                s = engine
                k = per[s] = per.get(s, 0) + 1
            base.setdefault(s, at[s])
            place[name] = (s, k, looped, base)
        for s in per:
            at[s] += per[s] * n
        per_part.append(per)
    new_engines, sems.started = not sems.started, True

    def emit_all(part, n, per, engine, eng, i):
        waited = {}
        for who, name, emit, after_, is_dma in part.steps:
            if who != engine:
                continue
            for a in after_:
                what, _, lag = a.partition("@")
                s, k, looped, base = place[what]
                inside = looped and part is loop
                if inside:
                    rel = k - int(lag or 0) * per[s]
                else:
                    rel = k + (per_part[parts.index((loop, count))][s] * (count - 1) if looped else 0)
                key, value = (s, inside), base[s] + rel
                if waited.get(key, -HEADROOM) >= value:
                    continue
                waited[key] = value
                eng.wait_ge(sems.sem[s], i * per[s] + value if inside else value)
            emit(eng, i).then_inc(sems.sem[name if is_dma else engine], 16 if is_dma else 1)

    def stream(engine):
        def body(eng):
            if new_engines:
                eng.sem_inc(sems.sem[engine], HEADROOM)
            if engine == "sp":
                for n in new:
                    eng.sem_inc(sems.sem[n], HEADROOM)
            for (part, n), per in zip(parts, per_part):
                if part is not loop:
                    emit_all(part, n, per, engine, eng, None)
                elif any(s[0] == engine for s in part.steps):
                    with eng.Fori(0, count) as i:
                        emit_all(part, n, per, engine, eng, i)
            if engine == "sp":
                for part, _ in parts:
                    for s in part.steps:
                        if s[4]:
                            eng.wait_ge(sems.sem[s[1]], at[s[1]])
        return body

    with nc.Block() as block:
        block.sync(stream("sp"))
        block.gpsimd(stream("pool"))
        block.scalar(stream("act"))
        block.vector(stream("dve"))
        block.tensor(stream("pe"))
    sems.at.update(at)


def merge(main, side):
    out, n, m = [], len(main.steps), len(side.steps)
    j = 0
    for k, s in enumerate(main.steps):
        out.append(s)
        while j < m and (j + 1) * n <= (k + 1) * m:
            out.append(side.steps[j])
            j += 1
    out += side.steps[j:]
    main.steps = out
    return main


def tokens(dram, g):
    return dram[bass.ds(g * SEQ, SEQ), :].rearrange("(k p) d -> p k d", p=P)


def group_of(i, par, ahead=0):
    if i is None:
        return par
    g = i * 2 + (par + ahead)
    if par + ahead >= 2:
        g = (i * 2 + 2) % NSEQ
    return g


def layernorm(st, n, src, dst, T, after, write_after=""):
    stats, mv, sd, rs = T["stats"], T["mv"], T["sd"], T["rs"]

    def bn(eng, i):
        for k in range(NT):
            x = eng.bn_stats(stats[:, k, :], src[:, k, :])
        return x

    def agg(eng, i):
        eng.memset(T["tick"][:], 0.0)
        for k in range(NT):
            x = eng.bn_aggr(mv[:, k, :], stats[:, k, :])
        return x

    def norm(eng, i):
        for k in range(NT):
            x = eng.tensor_scalar(dst[:, k, :], src[:, k, :], mv[:, k, 0:1], rs[:, k:k + 1], ALU.subtract, ALU.mult)
        return x

    st.add("dve", n + ".stats", bn, after)
    st.add("dve", n + ".mv", agg, n + ".stats")
    st.add("act", n + ".sd", lambda eng, i: eng.activation(sd[:], mv[:, :, 1], ACT.Sqrt, bias=T["eps"][:, 0:1]), n + ".mv")
    st.add("dve", n + ".rs", lambda eng, i: eng.reciprocal(rs[:], sd[:]), n + ".sd")
    st.add("dve", n + ".out", norm, n + ".rs " + write_after)


def ln_tiles(sb):
    return dict(stats=sb("stats", [P, NT, 6]), mv=sb("mv", [P, NT, 2]), sd=sb("sd", [P, NT]), rs=sb("rs", [P, NT]), tick=sb("tick", [P, 1]))


def transposes(out, src, ident, n=NT):
    def emit(eng, i):
        for k in range(n):
            x = eng.transpose(out[:, k * P:(k + 1) * P], src[:, k, :], ident[:])
        return x
    return emit


def split_weight(st, name, dram, raw, hi, lo, free=""):
    st.dma(name, lambda eng, i: eng.dma_start(raw, dram), free)
    st.add("pool", name + ".hi", lambda eng, i: eng.tensor_copy(hi, raw), name)
    st.add("pool", name + ".lo", lambda eng, i: eng.tensor_tensor(lo, raw, hi.bitcast(F32), ALU.subtract), name + ".hi")


def three(eng, out, ahi, alo, bhi, blo, start, stop, skip=False):
    eng.matmul(out, ahi, bhi, start=start, stop=False, skip_group_check=skip)
    eng.matmul(out, ahi, blo, start=False, stop=False, skip_group_check=skip)
    return eng.matmul(out, alo, bhi, start=False, stop=stop, skip_group_check=skip)


def before_first(names):
    return " ".join(n + (" s" + n[1:-2] if n.startswith("p0.") and n.endswith("@1") else "") for n in names.split())


def ffn0(nc, sems, C, bank, xin, xout, w):
    with ExitStack() as ctx:
        def sb(name, shape, dt=F32):
            return ctx.enter_context(nc.sbuf_tensor(name + w["tag"], shape, dt))

        T = ln_tiles(sb)
        T["eps"] = C["eps"]
        up_hi, up_lo = sb("up_hi", [P, E, HID], F32R), sb("up_lo", [P, E, HID], F32R)
        dn = sb("dn", [P, E, HC, D])
        wg = sb("wg", [P, E])
        b1, b1_rows = sb("b1", [P, E, HC]), sb("b1_rows", [E * HC, P])
        b2 = sb("b2", [E, D])
        raw = [sb(f"raw{r}", [P, HID]) for r in range(4)]
        xp, xn = sb("xp", [P, NT, D]), sb("xn", [P, NT, D])
        xT = [sb(f"xT{p}", [P, SEQ]) for p in range(2)]
        xT_hi = [sb(f"xT_hi{p}", [P, SEQ], F32R) for p in range(2)]
        xT_lo = [sb(f"xT_lo{p}", [P, SEQ], F32R) for p in range(2)]
        lg = sb("lg", [P, NT, E])
        top = sb("top", [P, NT, 8])
        sel, ex, den = sb("sel", [P, NT, E]), sb("ex", [P, NT, E]), sb("den", [P, NT])
        mk = [sb(f"mk{p}", [P, NT, E]) for p in range(2)]
        mkT = sb("mkT", [E, SEQ])
        acc = [sb(f"acc{p}", [P, NT, D]) for p in range(2)]
        NR = 4
        hf = [sb(f"hf{r}", [P, SEQ]) for r in range(NR)]
        HB, YB = bank[0:4], bank[4:6]
        TB, GB = bank[6], bank[7]

        st = Steps()
        st.dma("wg", lambda eng, i: eng.dma_start(wg[:], w["gate"]))
        st.dma("b1.ld", lambda eng, i: eng.dma_start(b1_rows[:], w["b1"]))
        st.dma("b2.ld", lambda eng, i: eng.dma_start(b2[:], w["b2"]))
        st.add("pe", "b1.T", lambda eng, i: eng.transpose(GB[:, 0:E * HC], b1_rows[:], C["ident"][0:E * HC, 0:E * HC]), "b1.ld")
        st.add("dve", "b1", lambda eng, i: eng.tensor_copy(b1[:].rearrange("p e c -> p (e c)"), GB[:, 0:E * HC]), "b1.T")
        wl = Steps()
        for e in range(E):
            split_weight(wl, f"w{e}", w["up"](e), raw[e % 4][:], up_hi[:, e, :], up_lo[:, e, :], f"w{e - 4}.lo" if e >= 4 else "")
            wl.dma(f"wd{e}", (lambda e: lambda eng, i: eng.dma_start(dn[:, e, :, :], w["down"](e)))(e))

        def prep(st, par, ahead, q):
            n = f"p{q}" if ahead else f"s{q}"
            last = lambda names: before_first(names) if ahead else ""
            back = "@1" if q == 1 else ""
            prev = f"p{1 - q}"
            st.dma(f"{n}.x", lambda eng, i: eng.dma_start(xp[:], tokens(xin, group_of(i, par, ahead))), last(f"{prev}.ln.out{back}"))
            layernorm(st, n + ".ln", xp, xn, T, f"{n}.x", last(f"{prev}.T{back}"))
            st.add("pe", n + ".T", transposes(TB, xn, C["ident"]), n + ".ln.out " + last(f"{prev}.xlo{back}"))
            free = last(f"h{q}.last{back}")
            st.add("act", n + ".xT", lambda eng, i: eng.copy(xT[q][:], TB[:]), n + ".T " + last(f"{n}.gate@1"))
            st.add("act", n + ".xhi", lambda eng, i: eng.copy(xT_hi[q][:], TB[:]), free)
            st.add("dve", n + ".xlo", lambda eng, i: eng.tensor_tensor(xT_lo[q][:], TB[:], xT_hi[q][:].bitcast(F32), ALU.subtract), n + ".xhi")

            def gate(eng, i):
                for k in range(NT):
                    x = eng.matmul(GB[:, k * E:(k + 1) * E], xT[q][:, k * P:(k + 1) * P], wg[:], start=True, stop=True)
                return x
            st.add("pe", n + ".gate", gate, n + ".xT " + last(f"{prev}.lg{back} c{1 - q}.acc"))
            st.add("dve", n + ".lg", lambda eng, i: eng.tensor_copy(lg[:], GB[:, 0:NT * E].rearrange("p (k e) -> p k e", e=E)), n + ".gate")

            def top8(eng, i):
                eng.memset(T["tick"][:], 0.0)
                for k in range(NT):
                    x = eng.max(top[:, k, :], lg[:, k, :])
                return x
            st.add("dve", n + ".top", top8, n + ".lg")
            second, first = top[:, :, 1:2].to_broadcast([P, NT, E]), top[:, :, 0:1].to_broadcast([P, NT, E])
            st.add("dve", n + ".sel", lambda eng, i: eng.tensor_tensor(sel[:], lg[:], second, ALU.is_ge), n + ".top")
            st.add("dve", n + ".sub", lambda eng, i: eng.tensor_tensor(lg[:], lg[:], first, ALU.subtract), n + ".sel")
            st.add("act", n + ".exp", lambda eng, i: eng.activation(ex[:], lg[:], ACT.Exp), n + ".sub")
            st.add("dve", n + ".pick", lambda eng, i: eng.tensor_tensor(ex[:], ex[:], sel[:], ALU.mult), n + ".exp")
            st.add("dve", n + ".sum", lambda eng, i: eng.reduce_sum(den[:], ex[:], AX.X), n + ".pick")
            st.add("dve", n + ".rec", lambda eng, i: eng.reciprocal(den[:], den[:]), n + ".sum")
            st.add("dve", n + ".wsum", lambda eng, i: eng.tensor_tensor(ex[:], ex[:], den[:, :, None].to_broadcast([P, NT, E]), ALU.mult), n + ".rec")
            st.add("dve", n + ".mk", lambda eng, i: eng.tensor_scalar(mk[q][:], ex[:], 0.5 / E, None, ALU.mult), n + ".wsum " + last(f"acc{q}.last{back}"))

        pre = Steps()
        prep(pre, 0, 0, 0)
        needs = {"s0.gate": ["wg", "b1"]}
        st.steps += [(a, b, c, d + needs.get(b, []), f) for a, b, c, d, f in pre.steps] + wl.steps

        loop = Steps()
        for q in range(2):
            main, side = Steps(), Steps()
            jobs = [(e, c) for e in range(E) for c in range(HC)]
            back = "" if q else "@1"
            pn, px = before_first(f"p{q}.mk{back}"), before_first(f"p{q}.xlo{back}")

            main.dma(f"acc{q}.x", lambda eng, i, q=q: eng.dma_start(acc[q][:], tokens(xin, group_of(i, q))), f"out{q}@1")

            def mT(eng, i, q=q):
                for k in range(NT):
                    x = eng.transpose(GB[0:E, k * P:(k + 1) * P], mk[q][:, k, :], C["ident"][:])
                return x
            bias = Steps()
            bias.add("pe", f"c{q}.T", mT, before_first(f"p{q}.mk{back} p{q}.lg{back}") + f" c{1 - q}.acc{back}")
            bias.add("act", f"c{q}.mT", lambda eng, i: eng.copy(mkT[:], GB[0:E, :]), f"c{q}.T c{1 - q}.mm{back}")

            def b2mm(eng, i):
                for k in range(NT):
                    x = eng.matmul(GB[:, k * P:(k + 1) * P], mkT[:, k * P:(k + 1) * P], b2[:], start=True, stop=True)
                return x
            bias.add("pe", f"c{q}.mm", b2mm, f"c{q}.mT b2.ld")
            bias.add("dve", f"c{q}.acc", lambda eng, i, q=q: eng.tensor_tensor(acc[q][:], acc[q][:], GB[:].rearrange("p (k d) -> p k d", d=D), ALU.add), f"c{q}.mm a{q}.2")

            def nm(kind, j, dj=0):
                k = j - dj
                return f"{kind}{q}.{k}" if k >= 0 else f"{kind}{1 - q}.{k + len(jobs)}{back}"

            def up(j, q=q):
                e, c = jobs[j]
                s, r = slice(c * P, (c + 1) * P), j % NR
                name = f"h{q}.last" if j == len(jobs) - 1 else f"h{q}.{j}"
                weight = f" w{e}.lo" if c == 0 else ""
                main.add("pe", name, lambda eng, i: three(eng, HB[j % 4][:], up_hi[:, e, s], up_lo[:, e, s], xT_hi[q][:], xT_lo[q][:], True, True),
                         px + " " + nm("f", j, 4) + weight)
                b = b1[:, e, c:c + 1]
                if j % 5 in (1, 3):
                    main.add("dve", f"f{q}.{j}", lambda eng, i: eng.tensor_scalar(hf[r][:], HB[j % 4][:], b, 0.0, ALU.add, ALU.max), name + " " + nm("y", j, NR) + " b1")
                else:
                    main.add("act", f"f{q}.{j}", lambda eng, i: eng.activation(hf[r][:], HB[j % 4][:], ACT.Relu, bias=b), name + " " + nm("y", j, NR) + " b1")

            def down(j, q=q):
                e, c = jobs[j]
                r, Y = j % NR, YB[e % 2]

                def emit(eng, i):
                    for k in range(NT):
                        t = slice(k * P, (k + 1) * P)
                        x = eng.matmul(Y[:, t], hf[r][:, t], dn[:, e, c, :], start=c == 0 and k == 0, stop=c == HC - 1 and k == NT - 1, skip_group_check=True)
                    return x
                free = (f"a{q}.{e - 2}" if e >= 2 else f"a{1 - q}.{E - 2}{back}" if e == 0 else f"acc{1 - q}.last{back}") if c == 0 else ""
                main.add("pe", f"y{q}.{j}", emit, f"f{q}.{j} wd{e} " + free)
                if c == HC - 1:
                    def accum(eng, i):
                        for k in range(NT):
                            x = eng.scalar_tensor_tensor(acc[q][:, k, :], Y[:, k * P:(k + 1) * P], mk[q][:, k, e:e + 1], acc[q][:, k, :], ALU.mult, ALU.add)
                        return x
                    prev = f"acc{q}.x" if e == 0 else f"a{q}.{e - 1}"
                    main.add("dve", f"acc{q}.last" if e == E - 1 else f"a{q}.{e}", accum, f"y{q}.{j} {pn} " + prev + (f" c{q}.acc" if e == 3 else ""))

            LEAD = 2
            for j in range(len(jobs) + LEAD):
                if j < len(jobs):
                    up(j)
                if j >= LEAD:
                    down(j - LEAD)
                if j in (4, 8, 12, 16):
                    main.steps.append(bias.steps[j // 4 - 1])
            main.dma(f"out{q}", lambda eng, i, q=q: eng.dma_start(tokens(xout, group_of(i, q)), acc[q][:]), f"acc{q}.last")
            prep(side, q, 1, 1 - q)
            a, b = len(main.steps) * 3 // 8, len(main.steps) * 7 // 8
            mid = Steps()
            mid.steps = main.steps[a:b]
            loop.steps += main.steps[:a] + merge(mid, side).steps + main.steps[b:]
        run(nc, sems, before=st, loop=loop, count=NSEQ // 2)


def consts(nc, sems, sb):
    C = dict(ident=sb("ident", [P, P]), eps=sb("eps", [P, 1]), one=sb("one", [P, 1]), pow2=sb("pow2", [P, E]))
    st = Steps()
    st.add("pool", "c.id0", lambda eng, i: eng.memset(C["ident"][:], 0.0))
    st.add("pool", "c.id", lambda eng, i: eng.affine_select(out=C["ident"][:], in_=C["ident"][:], compare_op=ALU.not_equal, fill=1.0,
                                                          base=0, pattern=[[-1, P]], channel_multiplier=1), "c.id0")
    st.add("pool", "c.one", lambda eng, i: eng.memset(C["one"][:], 1.0))
    st.add("pool", "c.eps", lambda eng, i: eng.memset(C["eps"][:], EPS))

    def powers(eng, i):
        for e in range(E):
            x = eng.memset(C["pow2"][:, e:e + 1], float(1 << (E - 1 - e)))
        return x
    st.add("pool", "c.pow2", powers)
    run(nc, sems, before=st)
    return C


def ffn0_weights(a):
    return dict(tag="_f0", up=lambda e: a["L0_ffn_W1"][e], down=lambda e: a["L0_ffn_W2"][e].rearrange("(c p) d -> p c d", p=P),
                gate=a["L0_ffn_W_gate"], b1=a["L0_ffn_b1"].rearrange("e (c p) -> (e c) p", p=P), b2=a["L0_ffn_b2"])


def ffn1_weights(a):
    def pick(shared, routed):
        return lambda e: a[routed][e] if e < E else a[shared]
    return dict(tag="_f1", up=[pick("L1_ffn_w1s", "L1_ffn_W1"), pick("L1_ffn_w2s", "L1_ffn_W2")],
                down=lambda e: pick("L1_ffn_w3s", "L1_ffn_W3")(e).rearrange("(c p) d -> p c d", p=P), gate=a["L1_ffn_Wg"])


def mamba(nc, sems, C, bank, xin, xout, a):
    with ExitStack() as ctx:
        def sb(name, shape, dt=F32):
            return ctx.enter_context(nc.sbuf_tensor(name + "_m", shape, dt))

        def two(name, shape, dt=F32):
            return [sb(name + str(p), shape, dt) for p in range(2)]

        T = ln_tiles(sb)
        T["eps"] = C["eps"]
        w_in = sb("w_in", [P, 2 * INNER])
        w_b = sb("w_b", [P, NH, 64])
        w_c = sb("w_c", [P, NH, 64])
        w_dt = sb("w_dt", [P, NH, RANK])
        w_dt2 = sb("w_dt2", [RANK, INNER])
        w_out = sb("w_out", [P, NH, D])
        w_glu = sb("w_glu", [P, 2 * D])
        b_glu = sb("b_glu", [1, 2 * D])
        ones = sb("ones", [1, P])
        rows = sb("rows", [64, P])
        cols = sb("cols", [P, 64])
        a_log = sb("a_log", [P, NH, NST])
        a_neg = sb("a_neg", [P, NH, NST])
        conv_w = sb("conv_w", [P, NH, TAPS])
        diag = sb("diag", [P, NH, TAPS, P])
        sel = sb("sel", [64, NST, P], F32R)
        sel_f = sb("sel_f", [64, NST, P])
        xp = sb("xp", [P, NT, D])
        xn = sb("xn", [P, NT, D])
        xm = sb("xm", [P, NT, D])
        skip = two("skip", [P, NT, D])
        hT = sb("hT", [P, SEQ])
        xi = sb("xi", [P, NH, TAPS - 1 + SEQ])
        u = two("u", [P, NH, SEQ])
        sz = two("sz", [P, NH, SEQ])
        bp = two("bp", [64, SEQ], F32R)
        cp = two("cp", [64, SEQ], F32R)
        dtr = sb("dtr", [RANK, SEQ])
        v = sb("v", [P, SEQ])
        ab = sb("ab", [P, SEQ])
        dt = two("dt", [P, NH, SEQ])
        du = two("du", [P, NH, SEQ])
        RA = 3
        da = [sb(f"da{r}", [P, SEQ]) for r in range(RA)]
        db = [sb(f"db{r}", [P, SEQ]) for r in range(2)]
        hs = [sb(f"hs{r}", [P, SEQ]) for r in range(2)]
        ph = [sb(f"ph{r}", [P, SEQ]) for r in range(3)]
        y2 = [sb(f"y2{r}", [P, SEQ]) for r in range(2)]
        gT = sb("gT", [P, SEQ])
        sg = sb("sg", [P, NT, D])
        o = two("o", [P, NT, D])
        SB, SC, SY, SX = bank[0:2], bank[2:4], bank[4:6], bank[6:8]
        GAM, BET, CB, DV, DB, = 0, 1, 2, 4, 6

        st = Steps()
        row = lambda ap: ap.rearrange("(h p) -> h p", p=P)
        for k, (nm, ap, n) in enumerate([("L0_attn_ln_gamma", GAM, 1), ("L0_attn_ln_beta", BET, 1), ("L0_attn_conv_b", CB, 2),
                                         ("L0_attn_D", DV, 2), ("L0_attn_dt_proj_b", DB, 2)]):
            st.dma(f"mv{k}", lambda eng, i, nm=nm, ap=ap, n=n: eng.dma_start(rows[ap:ap + n, :], row(a[nm])))
        st.add("pe", "rowsT", lambda eng, i: eng.transpose(SX[0][:, 0:8], rows[0:8, :], C["ident"][0:8, 0:8]), "mv0 mv1 mv2 mv3 mv4")
        st.add("dve", "cols", lambda eng, i: eng.tensor_copy(cols[:, 0:8], SX[0][:, 0:8]), "rowsT")
        st.dma("mw0", lambda eng, i: eng.dma_start(w_in[:], a["L0_attn_in_proj_w"]))
        xw = a["L0_attn_x_proj_w"].rearrange("(h p) n -> p h n", p=P)
        st.add("pool", "z0", lambda eng, i: eng.memset(w_b[:], 0.0))
        st.add("pool", "z1", lambda eng, i: eng.memset(w_c[:], 0.0))
        st.dma("mw1", lambda eng, i: eng.dma_start(w_dt[:], xw[:, :, 0:RANK]))
        for k, (w, at, o0) in enumerate([(w_b, 0, RANK), (w_b, 32, RANK), (w_c, 0, RANK + NST), (w_c, 32, RANK + NST)]):
            st.dma(f"mx{k}", lambda eng, i, w=w, at=at, o0=o0: eng.dma_start(w[:, :, at:at + NST], xw[:, :, o0:o0 + NST]), "z0 z1")
        st.dma("mw2", lambda eng, i: eng.dma_start(w_dt2[:], a["L0_attn_dt_proj_w"]))
        st.dma("mw3", lambda eng, i: eng.dma_start(w_out[:], a["L0_attn_out_proj_w"].rearrange("(h p) n -> p h n", p=P)))
        st.dma("mw4", lambda eng, i: eng.dma_start(w_glu[:], a["L0_attn_glu_w"]))
        st.dma("mw5", lambda eng, i: eng.dma_start(b_glu[:], a["L0_attn_glu_b"].rearrange("(o n) -> o n", o=1)))
        st.dma("mw6", lambda eng, i: eng.dma_start(a_log[:], a["L0_attn_A_log"].rearrange("(h p) n -> p h n", p=P)))
        st.dma("mw7", lambda eng, i: eng.dma_start(conv_w[:], a["L0_attn_conv_w"].rearrange("(h p) n -> p h n", p=P)))
        st.add("pool", "z2", lambda eng, i: eng.memset(ones[:], 1.0))
        st.add("pool", "z3", lambda eng, i: eng.memset(xi[:, :, 0:TAPS - 1], 0.0))
        st.add("pool", "z4", lambda eng, i: eng.memset(sel_f[:], 0.0))
        for k, off in enumerate((0, 32)):
            st.add("pool", f"z5{k}", lambda eng, i, off=off: eng.affine_select(
                out=sel_f[:], in_=sel_f[:], compare_op=ALU.not_equal, fill=1.0, base=-off, pattern=[[-1, NST], [0, P]],
                channel_multiplier=1), "z4" if k == 0 else "z50")
        st.add("dve", "sel", lambda eng, i: eng.tensor_copy(sel[:], sel_f[:]), "z51")
        st.add("act", "a.exp", lambda eng, i: eng.activation(a_neg[:], a_log[:], ACT.Exp), "mw6")
        st.add("dve", "a.neg", lambda eng, i: eng.tensor_scalar(a_neg[:], a_neg[:], -1.0, None, ALU.mult), "a.exp")

        def taps(eng, i):
            for h in range(NH):
                for k in range(TAPS):
                    x = eng.tensor_scalar(diag[:, h, k, :], C["ident"][:], conv_w[:, h, k:k + 1], None, ALU.mult)
            return x
        st.add("dve", "diag", taps, "mw7")

        def prep(st, par, ahead, q):
            n = f"p{q}"
            last = lambda name: "" if ahead == 0 else name
            back = "@1" if q == 1 else ""
            prev = f"p{1 - q}"
            g = lambda i: group_of(i, par, ahead)
            free = last(f"fin{q}" + back)
            st.dma(n + ".x", lambda eng, i: eng.dma_start(xp[:], tokens(xin, g(i))), last(f"{prev}.skip{back}"))
            layernorm(st, n + ".ln", xp, xn, T, n + ".x", last(f"{prev}.skip{back}"))
            st.add("dve", n + ".skip", lambda eng, i: eng.tensor_tensor(skip[q][:], xp[:], xn[:], ALU.add), n + ".ln.out " + free)
            layernorm(st, n + ".l2", xn, xm, T, n + ".ln.out", last(f"{prev}.T{back}"))
            st.add("pe", n + ".T", transposes(SX[0], xm, C["ident"]), n + ".l2.out " + last(f"{prev}.spl1{back}"))
            st.add("dve", n + ".h", lambda eng, i: eng.tensor_scalar(hT[:], SX[0][:], cols[:, GAM:GAM + 1], cols[:, BET:BET + 1], ALU.mult, ALU.add),
                   n + ".T " + last(f"{prev}.z1{back}"))
            for c in range(2 * NH):
                nm = f"{n}.in{c}"
                X = SX[(c + 1) % 2]
                before = f"{n}.h" if c < 2 else f"{n}.e{c - 2}"
                st.add("pe", nm, lambda eng, i, X=X, c=c: eng.matmul(X[:], w_in[:, c * P:(c + 1) * P], hT[:], start=True, stop=True),
                       before + f" {n}.h" + ("" if c else last(f" {prev}.v1{back}")))
                if c < NH:
                    st.add("act", f"{n}.e{c}", lambda eng, i, X=X, c=c: eng.copy(xi[:, c, TAPS - 1:], X[:]), nm + last(f" {prev}.conv{c}{back}"))
                else:
                    st.add("act", f"{n}.e{c}", lambda eng, i, X=X, c=c: eng.activation(sz[q][:, c - NH, :], X[:], ACT.Silu), nm + " " + free)
            st.steps[-1] = (st.steps[-1][0], st.steps[-1][1]) + st.steps[-1][2:]
            st.add("act", n + ".z1", lambda eng, i: eng.copy(T["actick"][:], C["eps"][:]), f"{n}.in3")
            for h in range(NH):
                X = SX[(h + 1) % 2]

                def conv(eng, i, h=h, X=X):
                    for k in range(TAPS):
                        x = eng.matmul(X[:], diag[:, h, k, :], xi[:, h, k:k + SEQ], start=k == 0, stop=k == TAPS - 1)
                    return x
                st.add("pe", f"{n}.conv{h}", conv, f"{n}.e{h} {n}.e{h + 2}")
                st.add("act", f"{n}.u{h}", lambda eng, i, h=h, X=X: eng.activation(u[q][:, h, :], X[:], ACT.Silu, bias=cols[:, CB + h:CB + h + 1]),
                       f"{n}.conv{h} " + free)

            def proj(X, w, m):
                def emit(eng, i):
                    for h in range(NH):
                        x = eng.matmul(X[0:m, :], w[:, h, :], u[q][:, h, :], start=h == 0, stop=h == NH - 1)
                    return x
                return emit
            st.add("pe", n + ".dtr", proj(SX[0], w_dt, RANK), f"{n}.u0 {n}.u1")
            st.add("act", n + ".dtr.s", lambda eng, i: eng.copy(dtr[:], SX[0][0:RANK, :]), n + ".dtr " + last(f"{prev}.dt1{back}"))
            for k, (w, dst) in enumerate(((w_b, bp), (w_c, cp))):
                X = SX[(k + 1) % 2]
                st.add("pe", f"{n}.bc{k}", proj(X, w, 64), f"{n}.u0 {n}.u1" + (f" {n}.dtr.s" if k else ""))
                st.add("act", f"{n}.sph{k}", lambda eng, i, X=X, dst=dst: eng.copy(dst[q][:], X[0:64, :]), f"{n}.bc{k} " + free)
                st.add("dve", f"{n}.spl{k}", lambda eng, i, X=X, dst=dst: eng.tensor_tensor(dst[q][32:64, :], X[32:64, :], dst[q][32:64, :].bitcast(F32), ALU.subtract),
                       f"{n}.sph{k}")
            for h in range(NH):
                X = SX[(h + 1) % 2]
                bias = cols[:, DB + h:DB + h + 1]
                st.add("pe", f"{n}.dt{h}", lambda eng, i, h=h, X=X: eng.matmul(X[:], w_dt2[:, h * P:(h + 1) * P], dtr[:], start=True, stop=True),
                       f"{n}.dtr.s {n}.spl0 {n}.spl1")
                vold = f" {n}.sp{h - 1}" if h else last(f" {prev}.sp1{back}")
                st.add("act", f"{n}.v{h}", lambda eng, i, X=X, bias=bias: eng.activation(v[:], X[:], ACT.Identity, bias=bias), f"{n}.dt{h}" + vold)
                st.add("act", f"{n}.a{h}", lambda eng, i: eng.activation(ab[:], v[:], ACT.Abs), f"{n}.v{h}")
                st.add("act", f"{n}.x{h}", lambda eng, i: eng.activation(ab[:], ab[:], ACT.Exp, scale=-1.0), f"{n}.a{h}")
                st.add("act", f"{n}.l{h}", lambda eng, i: eng.activation(ab[:], ab[:], ACT.Ln, bias=C["one"][:, 0:1]), f"{n}.x{h}")
                st.add("dve", f"{n}.sp{h}", lambda eng, i, h=h: eng.scalar_tensor_tensor(dt[q][:, h, :], v[:], 0.0, ab[:], ALU.max, ALU.add), f"{n}.l{h} " + free)
                st.add("dve", f"{n}.du{h}", lambda eng, i, h=h: eng.tensor_tensor(du[q][:, h, :], dt[q][:, h, :], u[q][:, h, :], ALU.mult), f"{n}.sp{h}")

        T["actick"] = sb("actick", [P, 1])
        pre = Steps()
        prep(pre, 0, 0, 0)
        needs = {"p0.h": ["cols"], "p0.in0": ["mw0"], "p0.u0": ["cols"], "p0.e0": ["z3"], "p0.conv0": ["diag"], "p0.dtr": ["mw1"],
                 "p0.bc0": ["mx0", "mx1", "mx2", "mx3"], "p0.dt0": ["mw2"], "p0.T": ["cols"], "p0.v0": ["cols"]}
        st.steps += [(e, nm, f, list(af) + needs.get(nm, []), d) for e, nm, f, af, d in pre.steps]
        run(nc, sems, before=st)

        loop = Steps()
        for q in range(2):
            main, side = Steps(), Steps()
            ready = f"p{q}.du1 p{q}.spl1 p{q}.spl0" if q else "p0.du1@1 p0.spl1@1 p0.spl0@1"
            jobs = [(n, h) for n in range(NST) for h in range(NH)]
            NJ = len(jobs)

            def nm(kind, j, dj, total):
                k = j - dj
                return f"{kind}{q}.{k}" if k >= 0 else f"{kind}{1 - q}.{k + total}" + ("@1" if q == 0 else "")

            def bcast(n, q=q):
                def emit(eng, i):
                    eng.matmul(SB[n % 2][:], sel[:, n, :], bp[q][:], start=True, stop=True)
                    return eng.matmul(SC[n % 2][:], sel[:, n, :], cp[q][:], start=True, stop=True)
                main.add("pe", f"bc{q}.{n}", emit, ready + " " + nm("ph", 2 * n + 1, 4, NJ))

            def ysum(j, q=q):
                n, h = jobs[j]
                y_free = "" if n else (f"yd{1 - q}.{h}" + ("@1" if q == 0 else ""))
                main.add("pe", f"ys{q}.{j}", lambda eng, i: eng.matmul(SY[h][:], C["ident"][:], ph[j % 3][:], start=n == 0, stop=n == NST - 1,
                                                                    skip_group_check=True),
                         f"ph{q}.{j} " + y_free)

            for j, (n, h) in enumerate(jobs):
                if j == 0:
                    bcast(0)
                if h == 0 and n + 1 < NST:
                    bcast(n + 1)
                main.add("act", f"da{q}.{j}", lambda eng, i, n=n, h=h, j=j: eng.activation(da[j % RA][:], dt[q][:, h, :], ACT.Exp, scale=a_neg[:, h, n:n + 1]),
                         ready + " " + nm("hs", j, RA, NJ)) if False else main.add(
                             "act", f"da{q}.{j}", (lambda n, h, j, q: lambda eng, i: eng.activation(da[j % RA][:], dt[q][:, h, :], ACT.Exp, scale=a_neg[:, h, n:n + 1]))(n, h, j, q),
                             ready + " " + nm("hs", j, RA, NJ))
                main.add("dve", f"db{q}.{j}", (lambda n, h, j, q: lambda eng, i: eng.tensor_tensor(db[j % 2][:], du[q][:, h, :], SB[n % 2][:], ALU.mult))(n, h, j, q),
                         f"bc{q}.{n}")
                main.add("dve", f"hs{q}.{j}", (lambda j: lambda eng, i: eng.tensor_tensor_scan(hs[j % 2][:], da[j % RA][:], db[j % 2][:], 0.0, ALU.mult, ALU.add))(j),
                         f"da{q}.{j} db{q}.{j}")
                main.add("dve", f"ph{q}.{j}", (lambda n, j: lambda eng, i: eng.tensor_tensor(ph[j % 3][:], hs[j % 2][:], SC[n % 2][:], ALU.mult))(n, j),
                         f"hs{q}.{j} " + nm("ys", j, 3, NJ))
                if j >= 1:
                    ysum(j - 1)
            ysum(NJ - 1)
            other = "@1" if q == 0 else ""
            for h in range(NH):
                main.add("dve", f"yd{q}.{h}", (lambda h, q: lambda eng, i: eng.scalar_tensor_tensor(y2[h][:], u[q][:, h, :], cols[:, DV + h:DV + h + 1], SY[h][:], ALU.mult, ALU.add))(h, q),
                         f"ys{q}.{NJ - NH + h} op{1 - q}{other}")
                main.add("dve", f"y2{q}.{h}", (lambda h, q: lambda eng, i: eng.tensor_tensor(y2[h][:], y2[h][:], sz[q][:, h, :], ALU.mult))(h, q), f"yd{q}.{h}")

            def outp(eng, i):
                for h in range(NH):
                    x = eng.matmul(SB[0][:], w_out[:, h, :], y2[h][:], start=h == 0, stop=h == NH - 1)
                return x
            main.add("pe", f"op{q}", outp, f"y2{q}.0 y2{q}.1 ph{q}.{NJ - 1}")
            main.add("act", f"gT{q}", lambda eng, i: eng.activation(gT[:], SB[0][:], ACT.Gelu), f"op{q} gl{1 - q}{other}")

            def glu(eng, i):
                for k in range(NT):
                    dst = (SC[0] if k < 2 else SC[1])[:, (k % 2) * 2 * D:(k % 2 + 1) * 2 * D]
                    eng.matmul(dst, gT[:, k * P:(k + 1) * P], w_glu[:], start=True, stop=False)
                    x = eng.matmul(dst, ones[:], b_glu[:], start=False, stop=True)
                return x
            main.add("pe", f"gl{q}", glu, f"gT{q}")
            for k2 in range(2):
                G = SC[k2][:].rearrange("p (k c) -> p k c", k=2)
                main.add("act", f"sg{q}.{k2}", (lambda G, k2: lambda eng, i: eng.activation(sg[:, 2 * k2:2 * k2 + 2, :], G[:, :, D:2 * D], ACT.Sigmoid))(G, k2),
                         f"gl{q} go{1 - q}.1{other}")
                main.add("dve", f"go{q}.{k2}", (lambda G, k2, q: lambda eng, i: eng.tensor_tensor(o[q][:, 2 * k2:2 * k2 + 2, :], G[:, :, 0:D], sg[:, 2 * k2:2 * k2 + 2, :], ALU.mult))(G, k2, q),
                         f"sg{q}.{k2} st{q}@1")
            main.add("dve", f"fin{q}", (lambda q: lambda eng, i: eng.tensor_tensor(o[q][:], o[q][:], skip[q][:], ALU.add))(q), f"go{q}.0 go{q}.1")
            main.dma(f"st{q}", (lambda q: lambda eng, i: eng.dma_start(tokens(xout, group_of(i, q)), o[q][:]))(q), f"fin{q}")
            prep(side, q, 1, 1 - q)
            cut = len(main.steps) * 3 // 4
            head = Steps()
            head.steps = main.steps[4:cut]
            loop.steps += main.steps[:4] + merge(head, side).steps + main.steps[cut:]
        fix = {"bc0.0": ["fin1@1", "gT1@1"], "bc1.0": ["fin0", "gT0"], "bc0.1": ["fin1@1"], "bc1.1": ["fin0"]}
        loop.steps = [(e, nm, f, list(af) + fix.get(nm, []), d) for e, nm, f, af, d in loop.steps]
        run(nc, sems, loop=loop, count=NSEQ // 2)


def attention(nc, sems, C, bank, xin, xout, a):
    NB = SEQ // QB
    KP = SEQ + 2 * PAD
    BB = 4
    HB = NB // 2
    VW = HG * HD + 1
    with ExitStack() as ctx:
        def sb(name, shape, dt=F32):
            return ctx.enter_context(nc.sbuf_tensor(name + "_a", shape, dt))

        T = ln_tiles(sb)
        T["eps"] = C["eps"]
        w_q, w_k = sb("w_q", [P, HG, P]), sb("w_k", [P, HG, P])
        w_v, w_o = sb("w_v", [P, D]), sb("w_o", [P, D])
        b_rows, b_cols = sb("b_rows", [2 * HG, P]), sb("b_cols", [P, 2 * HG])
        b_v, b_o = sb("b_v", [1, D]), sb("b_o", [1, D])
        ones, valid = sb("ones", [1, P]), sb("valid", [1, KP])
        band = sb("band", [P, KW])
        own = sb("own", [P, HG * HD])
        fold = sb("fold", [P, QB])
        xp, xn = sb("xp", [P, NT, D]), sb("xn", [P, NT, D])
        xT = sb("xT", [P, KP])
        two = lambda name, shape: [sb(name + str(p), shape) for p in range(2)]
        qd = [[sb(f"qd{p}{g}", [P, NB, HG, QB]) for g in range(HG)] for p in range(2)]
        kT = [[sb(f"kT{p}{g}", [P, KP]) for g in range(HG)] for p in range(2)]
        vb = two("vb", [KW, NB, HG, VW])
        s = two("s", [P, NB, KW])
        mx = two("mx", [P, NB])
        pT = [sb(f"pT{r}", [KW, BB, P]) for r in range(3)]
        rc = two("rc", [P, HB])
        o1 = two("o1", [P, HB, HG * HD])
        oT = sb("oT", [P, SEQ])
        o = two("o", [P, NT, D])
        BS, BT, BO, BZ, BX = bank[0:2], bank[2:4], bank[4], bank[5], bank[6:8]

        st = Steps()
        wT = a["L1_attn_Wqkv"]
        heads = lambda w: w[:].rearrange("p g (r c) -> p (g r) c", r=HG)[:, :, 0:HD]
        st.add("pool", "z0", lambda eng, i: eng.memset(w_q[:], 0.0))
        st.add("pool", "z1", lambda eng, i: eng.memset(w_k[:], 0.0))
        st.add("pool", "z2", lambda eng, i: eng.memset(b_rows[:], 0.0))
        for k, w in enumerate((w_q, w_k)):
            st.dma(f"mx{k}", lambda eng, i, k=k, w=w: eng.dma_start(heads(w), wT[:, k * D:(k + 1) * D].rearrange("p (h c) -> p h c", c=HD)), f"z{k}")
            st.dma(f"mv{k}", lambda eng, i, k=k: eng.dma_start(b_rows[k * HG:(k + 1) * HG, :].rearrange("g (r c) -> g r c", r=HG)[:, :, 0:HD],
                                                             a["L1_attn_bqkv"][k * D:(k + 1) * D].rearrange("(g r c) -> g r c", g=HG, r=HG)), "z2")
        st.dma("mw0", lambda eng, i: eng.dma_start(w_v[:], wT[:, 2 * D:3 * D]))
        st.dma("mw1", lambda eng, i: eng.dma_start(w_o[:], a["L1_attn_Wout"]))
        st.dma("mw2", lambda eng, i: eng.dma_start(b_v[:], a["L1_attn_bqkv"][2 * D:3 * D].rearrange("(o n) -> o n", o=1)))
        st.dma("mw3", lambda eng, i: eng.dma_start(b_o[:], a["L1_attn_bout"].rearrange("(o n) -> o n", o=1)))
        st.add("pe", "bT", lambda eng, i: eng.transpose(BX[0][:, 0:2 * HG], b_rows[:], C["ident"][0:2 * HG, 0:2 * HG]), "mv0 mv1")
        st.add("dve", "b_cols", lambda eng, i: eng.tensor_copy(b_cols[:], BX[0][:, 0:2 * HG]), "bT")
        st.add("pool", "ones", lambda eng, i: eng.memset(ones[:], 1.0))
        st.add("pool", "v0", lambda eng, i: eng.memset(valid[:], 0.0))
        st.add("pool", "v1", lambda eng, i: eng.memset(valid[:, PAD:PAD + SEQ], 1.0), "v0")
        st.add("pool", "m0", lambda eng, i: eng.memset(band[:], 0.0))
        st.add("pool", "m1", lambda eng, i: eng.memset(own[:], 0.0))
        st.add("pool", "m2", lambda eng, i: eng.memset(fold[:], 0.0))

        def quadrants(name, emit, after):
            for r in range(HG):
                last = r == HG - 1
                st.add("pool", name if last else f"{name}.{r}", lambda eng, i, r=r: emit(eng, r, slice(32 * r, 32 * r + 32)), after if r == 0 else f"{name}.{r - 1}")
        quadrants("m3", lambda eng, r, p: eng.affine_select(out=band[p, :], in_=band[p, :], compare_op=ALU.is_ge, fill=-1e30, base=0,
                                                          pattern=[[1, KW]], channel_multiplier=-1), "m2")
        quadrants("m4", lambda eng, r, p: eng.affine_select(out=band[p, :], in_=band[p, :], compare_op=ALU.is_ge, fill=-1e30, base=WIN - 1,
                                                          pattern=[[-1, KW]], channel_multiplier=1), "m3")
        quadrants("m5", lambda eng, r, p: eng.memset(own[p, HD * r:HD * r + HD], 1.0), "m4")
        quadrants("m6", lambda eng, r, p: eng.affine_select(out=fold[p, :], in_=fold[p, :], compare_op=ALU.not_equal, fill=1.0, base=0,
                                                          pattern=[[-1, QB]], channel_multiplier=1), "m5")
        st.add("pool", "m7", lambda eng, i: eng.memset(xT[:, 0:PAD], 0.0), "m6")
        st.add("pool", "m8", lambda eng, i: eng.memset(xT[:, PAD + SEQ:], 0.0))

        def zeros(eng, i):
            for p in range(2):
                for g in range(HG):
                    eng.memset(kT[p][g][:, 0:PAD], 0.0)
                    eng.memset(kT[p][g][:, PAD + SEQ:], 0.0)
                x = eng.memset(vb[p][:, :, :, VW - 1:VW], 1.0)
            return x
        st.add("pool", "m9", zeros, "m8")

        def qzeros(eng, i):
            for p in range(2):
                for g in range(HG):
                    x = eng.memset(qd[p][g][:], 0.0)
            return x
        st.add("dve", "mq", qzeros)

        def prep(st, par, ahead, q):
            n = f"p{q}"
            last = lambda name: "" if ahead == 0 else name
            back = "@1" if q == 1 else ""
            prev = f"p{1 - q}"
            free = last(f"s.last{q}" + back)
            vfree = last(f"ot{q}.{HG - 1}.1" + back)
            st.dma(n + ".x", lambda eng, i: eng.dma_start(xp[:], tokens(xin, group_of(i, par, ahead))), last(f"{prev}.ln.out{back}"))
            layernorm(st, n + ".ln", xp, xn, T, n + ".x", last(f"{prev}.T{back}"))
            st.add("pe", n + ".T", transposes(BX[0], xn, C["ident"]), n + ".ln.out " + last(f"{prev}.v2{back}"))
            st.add("act", n + ".xT", lambda eng, i: eng.copy(xT[:, PAD:PAD + SEQ], BX[0][:]), n + ".T " + last(f"{prev}.vm3{back}"))
            units = [(w, g) for g in range(HG) for w in (0, 1)]
            readers = [n + ".xT", last(f"{prev}.v3{back}")]
            for k, (w, g) in enumerate(units):
                X = BX[k % 2]
                W = (w_q, w_k)[w]
                st.add("pe", f"{n}.m{k}", lambda eng, i, X=X, W=W, g=g: eng.matmul(X[:], W[:, g, :], xT[:, PAD:PAD + SEQ], start=True, stop=True),
                       f"{n}.xT {readers[k % 2]}")
                bias = b_cols[:, w * HG + g:w * HG + g + 1]
                if w == 0:
                    def evac(eng, i, X=X, g=g):
                        for r in range(HG):
                            p = slice(32 * r, 32 * r + 32)
                            x = eng.activation(qd[q][g][p, :, r, :], X[p, :].rearrange("p (b q) -> p b q", q=QB), ACT.Identity, bias=b_cols[p, g:g + 1])
                        return x
                    st.add("act", f"{n}.e{k}", evac, f"{n}.m{k} " + free)
                else:
                    st.add("dve", f"{n}.e{k}", lambda eng, i, X=X, g=g, bias=bias: eng.tensor_scalar(kT[q][g][:, PAD:PAD + SEQ], X[:], bias, None, ALU.add),
                           f"{n}.m{k} " + free)
                readers[k % 2] = f"{n}.e{k}"
            for k in range(NB // 4):
                X = BX[k % 2]

                def vals(eng, i, X=X, k=k):
                    for j in range(4):
                        b = 4 * k + j
                        keys = slice(b * QB, b * QB + KW)
                        eng.matmul(X[0:KW, j * D:(j + 1) * D], xT[:, keys], w_v[:], start=True, stop=False)
                        x = eng.matmul(X[0:KW, j * D:(j + 1) * D], valid[:, keys], b_v[:], start=False, stop=True)
                    return x
                st.add("pe", f"{n}.vm{k}", vals, readers[k % 2])
                st.add("act", f"{n}.v{k}", lambda eng, i, X=X, k=k: eng.copy(vb[q][:, 4 * k:4 * k + 4, :, 0:VW - 1], X[0:KW, :].rearrange("p (b g c) -> p b g c", b=4, g=HG)),
                       f"{n}.vm{k} " + vfree)
                readers[k % 2] = f"{n}.v{k}"

        pre = Steps()
        prep(pre, 0, 0, 0)
        needs = {"p0.m0": ["mx0", "mx1", "m8"], "p0.e0": ["b_cols", "mq"], "p0.e1": ["b_cols", "m9"], "p0.vm0": ["mw0", "mw2", "v1", "m8"], "p0.v0": ["m9"]}
        st.steps += [(e, nm, f, list(af) + needs.get(nm, []), d) for e, nm, f, af, d in pre.steps]
        run(nc, sems, before=st)

        loop = Steps()
        scale = float(1.0 / np.sqrt(np.float32(HD)))
        for q in range(2):
            main, side = Steps(), Steps()
            w1 = "" if q else "@1"
            ready = f"p{q}.e6{w1} p{q}.e7{w1}"
            main.dma(f"ox{q}", (lambda q: lambda eng, i: eng.dma_start(o[q][:], tokens(xin, group_of(i, q))))(q), f"st{q}@1")

            def before(g, kind):
                return f"{kind.format(q=q, g=g - 1)}" if g else f"{kind.format(q=1 - q, g=HG - 1)}{w1}"

            def before2(g, kind):
                return kind.format(q=q, g=g - 2) if g >= 2 else kind.format(q=1 - q, g=HG + g - 2) + w1

            def scores(g, q=q):
                S, M = s[g % 2], mx[g % 2]
                for c in range(NB // BB):
                    X = BS[c % 2]

                    def mm(eng, i, X=X, c=c):
                        for j in range(BB):
                            b = c * BB + j
                            x = eng.matmul(X[:, j * KW:(j + 1) * KW], qd[q][g][:, b, :, :].rearrange("p r q -> p (r q)"), kT[q][g][:, b * QB:b * QB + KW], start=True, stop=True)
                        return x
                    prev = f"sm{q}.{g}.{c - 2}" if c >= 2 else before(g, "sm{q}.{g}." + str(c + 2))
                    name = f"s.last{q}" if (g, c) == (HG - 1, NB // BB - 1) else f"sc{q}.{g}.{c}"
                    main.add("pe", name, mm, f"{ready} {prev}")
                    main.add("dve", f"sm{q}.{g}.{c}", lambda eng, i, X=X, c=c: eng.scalar_tensor_tensor(
                        S[:, c * BB:(c + 1) * BB, :], X[:, 0:BB * KW].rearrange("p (b k) -> p b k", k=KW), scale, band[:, None, :].to_broadcast([P, BB, KW]), ALU.mult, ALU.add),
                        name + " " + before2(g, "pt{q}.{g}.3"))
                main.add("dve", f"mx{q}.{g}", lambda eng, i: eng.reduce_max(M[:], S[:], AX.X), f"sm{q}.{g}.3")
                main.add("dve", f"sb{q}.{g}", lambda eng, i: eng.tensor_tensor(S[:], S[:], M[:, :, None].to_broadcast([P, NB, KW]), ALU.subtract), f"mx{q}.{g}")
                main.add("act", f"ex{q}.{g}", lambda eng, i: eng.activation(S[:], S[:], ACT.Exp), f"sb{q}.{g}")

            def outputs(g, q=q):
                S = s[g % 2]
                for c in range(NB // BB):
                    k = g * (NB // BB) + c
                    X, W = BT[c % 2], pT[k % 3]

                    def tr(eng, i, X=X, c=c):
                        for j in range(BB):
                            x = eng.transpose(X[0:KW, j * P:(j + 1) * P], S[:, c * BB + j, :], C["ident"][:])
                        return x
                    prev = f"pe{q}.{g}.{c - 2}" if c >= 2 else before(g, "pe{q}.{g}." + str(c + 2))
                    main.add("pe", f"pt{q}.{g}.{c}", tr, f"ex{q}.{g} {prev} op{1 - q}.r{w1}")
                    kk = k - 3
                    old = f"pv{q}.{kk // 4}.{kk % 4}" if kk >= 0 else f"pv{1 - q}.{(kk + 16) // 4}.{(kk + 16) % 4}{w1}"
                    main.add("act", f"pe{q}.{g}.{c}", lambda eng, i, X=X, W=W: eng.copy(W[:].rearrange("p b q -> p (b q)"), X[0:KW, :]), f"pt{q}.{g}.{c} {old}")
                    h = c // 2

                    def pv(eng, i, W=W, c=c):
                        for j in range(BB):
                            b = c * BB + j
                            at = (b % HB) * VW
                            x = eng.matmul(BO[:, at:at + VW], W[:, j, :], vb[q][:, b, g, :], start=True, stop=True)
                        return x
                    bo = (f"on{q}.{g}.0" if h else before(g, "on{q}.{g}.1"))
                    main.add("pe", f"pv{q}.{g}.{c}", pv, f"pe{q}.{g}.{c} {bo}")
                    if c % 2:
                        O = BO[:, 0:HB * VW].rearrange("p (b c) -> p b c", c=VW)
                        R, Z = rc[h], o1[h]
                        zold = before(g, "ot{q}.{g}." + str(h))
                        main.add("dve", f"rc{q}.{g}.{h}", lambda eng, i, O=O, R=R: eng.reciprocal(R[:], O[:, :, VW - 1]), f"pv{q}.{g}.{c}")
                        main.add("dve", f"on{q}.{g}.{h}", lambda eng, i, O=O, R=R, Z=Z: eng.tensor_tensor(Z[:], O[:, :, 0:VW - 1], R[:, :, None].to_broadcast([P, HB, HG * HD]), ALU.mult),
                                 f"rc{q}.{g}.{h} {zold}")
                        main.add("dve", f"om{q}.{g}.{h}", lambda eng, i, Z=Z: eng.tensor_tensor(Z[:], Z[:], own[:, None, :].to_broadcast([P, HB, HG * HD]), ALU.mult),
                                 f"on{q}.{g}.{h}")

                        def ot(eng, i, Z=Z, h=h):
                            for j in range(HB):
                                b = h * HB + j
                                x = eng.matmul(BZ[32 * g:32 * g + 32, b * QB:(b + 1) * QB], Z[:, j, :], fold[:], start=True, stop=True)
                            return x
                        main.add("pe", f"ot{q}.{g}.{h}", ot, f"om{q}.{g}.{h} oc{1 - q}{w1}")

            scores(0)
            for g in range(HG):
                if g + 1 < HG:
                    scores(g + 1)
                outputs(g)
            main.add("act", f"oc{q}", lambda eng, i: eng.copy(oT[:], BZ[:]), f"ot{q}.{HG - 1}.1 op{1 - q}{w1}")

            def proj(eng, i):
                for k in range(NT):
                    t = slice(k * P, (k + 1) * P)
                    eng.matmul(BT[0][:, t], oT[:, t], w_o[:], start=True, stop=False)
                    x = eng.matmul(BT[0][:, t], ones[:], b_o[:], start=False, stop=True)
                return x
            main.add("pe", f"op{q}", proj, f"oc{q} pe{q}.{HG - 1}.2")
            main.add("dve", f"op{q}.r", (lambda q: lambda eng, i: eng.tensor_tensor(o[q][:], o[q][:], BT[0][:].rearrange("p (k d) -> p k d", d=D), ALU.add))(q), f"op{q} ox{q}")
            main.dma(f"st{q}", (lambda q: lambda eng, i: eng.dma_start(tokens(xout, group_of(i, q)), o[q][:]))(q), f"op{q}.r")
            prep(side, q, 1, 1 - q)
            loop.steps += merge(main, side).steps
        run(nc, sems, loop=loop, count=NSEQ // 2)


RT = NSEQ * NT + E
SPARE = 2
XS_TILES = SPARE + RT
TILES = NSEQ * NT
CLEAR = 6


def clear_rows(nc, sems, xs):
    with ExitStack() as ctx:
        zero = ctx.enter_context(nc.sbuf_tensor("zero", [P, CLEAR, D], F32))
        st = Steps()
        st.add("pool", "c.zero", lambda eng, i: eng.memset(zero[:], 0.0))
        for k in range(XS_TILES // CLEAR):
            st.dma(f"w{k}", (lambda k: lambda eng, i: eng.dma_start(xs[k * CLEAR * P:(k + 1) * CLEAR * P, :].rearrange("(k p) d -> p k d", p=P), zero[:]))(k), "c.zero")
        assert XS_TILES % CLEAR == 0
        run(nc, sems, before=st)


def ffn1(nc, sems, C, bank, xin, xout, w, xs, ys):
    NU, U = 2, 4
    with ExitStack() as ctx:
        def sb(name, shape, dt=F32):
            return ctx.enter_context(nc.sbuf_tensor(name + w["tag"], shape, dt))

        U32, I32 = mybir.dt.uint32, mybir.dt.int32
        two = lambda name, shape, dt=F32: [sb(name + str(p), shape, dt) for p in range(2)]
        T = ln_tiles(sb)
        T["eps"] = C["eps"]
        up_hi = [sb(f"up_hi{u}", [P, E + 1, HID], F32R) for u in range(NU)]
        up_lo = [sb(f"up_lo{u}", [P, E + 1, HID], F32R) for u in range(NU)]
        dn = sb("dn", [P, E + 1, HC, D])
        wg = sb("wg", [P, E])
        raw = [sb(f"raw{r}", [P, HID]) for r in range(3)]
        xp, xn, xT = two("xp", [P, NT, D]), two("xn", [P, NT, D]), two("xT", [P, SEQ])
        xn_all = sb("xn_all", [P, TILES, D])
        xT_hi, xT_lo = sb("xT_hi", [P, NSEQ * SEQ], F32R), sb("xT_lo", [P, NSEQ * SEQ], F32R)
        acc_all = sb("acc_all", [P, TILES, D])
        lg = sb("lg", [P, TILES, E])
        mx, ge, wt, v1 = sb("mx", [P, TILES]), sb("ge", [P, TILES, E]), sb("wt", [P, TILES, E]), sb("v1", [P, TILES])
        oh, ohr = sb("oh", [P, TILES, E]), sb("ohr", [P, TILES * E], F32R)
        tri, one_r = sb("tri", [P, P], F32R), sb("one_r", [P, P], F32R)
        tri_f, one_f = sb("tri_f", [P, P]), sb("one_f", [P, E * TILES])
        tot, cum, exc = sb("tot", [P, E, TILES]), sb("cum", [P, E, TILES]), sb("exc", [P, E, TILES])
        cnt, ntl, tcum, base = sb("cnt", [P, E]), sb("ntl", [P, E]), sb("tcum", [P, E]), sb("base", [P, E])
        steps128 = sb("steps128", [P, TILES])
        tile_no = sb("tile_no", [1, RT])
        many = sb("many", [P, E, TILES])
        slot_f, slot = sb("slot_f", [P, TILES]), sb("slot", [P, TILES], U32)
        te_f, te_c, te = sb("te_f", [1, RT]), sb("te_c", [1, RT, E - 1]), sb("te", [1, RT], I32)
        four = lambda name, shape, dt=F32: [sb(name + str(p), shape, dt) for p in range(U)]
        xg = four("xg", [P, D])
        x_hi, x_lo = four("x_hi", [P, P], F32R), four("x_lo", [P, P], F32R)
        te_tab = sb("te_tab", [1, RT // U + 1, 2 * U], I32)
        gel, hf = two("gel", [P, HID]), four("hf", [P, HID])
        hT, yb = raw[0:2], [raw[2][:, r * D:(r + 1) * D] for r in range(2)]
        HB, HT, XB, YB = bank[0:4], bank[4:6], bank[6], bank[7]

        st, loop = Steps(), Steps()
        ring = [""] * 3

        def weights(st, experts):
            for e in experts:
                for u in range(NU):
                    r, name = (NU * e + u) % 3, f"w{u}.{e}"
                    split_weight(st, name, w["up"][u](e), raw[r][:], up_hi[u][:, e, :], up_lo[u][:, e, :], ring[r])
                    ring[r] = name + ".lo"
                st.dma(f"wd{e}", (lambda e: lambda eng, i: eng.dma_start(dn[:, e, :, :], w["down"](e)))(e))
        first, second = [E] + list(range(5)), list(range(5, E))
        st.dma("wg", lambda eng, i: eng.dma_start(wg[:], w["gate"]))
        for q in range(2):
            st.dma(f"s.x{q}", (lambda q: lambda eng, i: eng.dma_start(xp[q][:], tokens(xin, q)))(q))
        weights(st, first)
        halves = []
        for q in range(2):
            half = Steps()
            halves.append(half)
            Tq = T if q == 0 else T | {k: sb(k + "_b", t.shape) for k, t in T.items() if k != "eps"}
            at = lambda i, q=q: bass.ds((i * 2 + q) * NT, NT)
            cols = lambda i, q=q: bass.ds((i * 2 + q) * SEQ, SEQ)
            layernorm(half, f"ln{q}", xp[q], xn[q], Tq, f"x{q}@1 s.x{q}", f"T{q}@1 keep{q}@1")
            half.add("pe", f"T{q}", transposes(HB[q], xn[q], C["ident"]), f"ln{q}.out xT{q}@1 lo{q}@1")
            half.add("act", f"xT{q}", (lambda q: lambda eng, i: eng.copy(xT[q][:], HB[q][:]))(q), f"T{q} gt{q}@1")
            half.add("act", f"hi{q}", (lambda q, cols: lambda eng, i: eng.copy(xT_hi[:, cols(i)], HB[q][:]))(q, cols))
            half.add("dve", f"lo{q}", (lambda q, cols: lambda eng, i: eng.tensor_tensor(xT_lo[:, cols(i)], HB[q][:], xT_hi[:, cols(i)].bitcast(F32), ALU.subtract))(q, cols), f"hi{q}")
            half.add("act", f"keep{q}", (lambda q, at: lambda eng, i: eng.copy(xn_all[:, at(i), :], xn[q][:]))(q, at))
            half.dma(f"x{q}", (lambda q: lambda eng, i: eng.dma_start(xp[q][:], tokens(xin, (i * 2 + (q + 2)) % NSEQ)))(q), f"ln{q}.out", engine="act")

            def gate(eng, i, q=q):
                for k in range(NT):
                    x = eng.matmul(HT[q][:, k * E:(k + 1) * E], xT[q][:, k * P:(k + 1) * P], wg[:], start=True, stop=True)
                return x
            half.add("pe", f"gt{q}", gate, f"xT{q} lg{q}@1 wg")
            half.add("dve", f"lg{q}", (lambda q, at: lambda eng, i: eng.tensor_copy(lg[:, at(i), :], HT[q][:, 0:NT * E].rearrange("p (k e) -> p k e", e=E)))(q, at), f"gt{q}")
        for pair in zip(*(h.steps for h in halves)):
            loop.steps += pair

        rt = Steps()
        every = lambda ap, n: ap[:, :, None].to_broadcast([P, TILES, n])
        pow2 = C["pow2"][:, None, :].to_broadcast([P, TILES, E])
        chain = [""]

        def dve(name, emit, extra=""):
            rt.add("dve", name, emit, f"{chain[0]} {extra}")
            chain[0] = name
        tt = lambda out, a, b, op: (lambda eng, i: eng.tensor_tensor(out, a, b, op))
        dve("r.max", lambda eng, i: eng.reduce_max(mx[:], lg[:], AX.X), "lg0 lg1")
        dve("r.ge", tt(ge[:], lg[:], every(mx, E), ALU.is_ge))
        dve("r.wt", tt(wt[:], ge[:], pow2, ALU.mult))
        dve("r.v1", lambda eng, i: eng.reduce_sum(v1[:], wt[:], AX.X))
        dve("r.st", tt(wt[:], every(v1, E), pow2, ALU.is_ge))
        dve("r.o0", lambda eng, i: eng.tensor_copy(oh[:, :, 0:1], wt[:, :, 0:1]))
        dve("r.oh", tt(oh[:, :, 1:E], wt[:, :, 1:E], wt[:, :, 0:E - 1], ALU.subtract))
        dve("r.ohr", lambda eng, i: eng.tensor_copy(ohr[:], oh[:].rearrange("p t e -> p (t e)")))
        rt.add("pe", "r.rank", lambda eng, i: eng.matmul(XB[:, 0:TILES * E], tri[:], ohr[:], start=True, stop=True), "r.ohr t.tri")
        rt.add("pe", "r.tot", lambda eng, i: eng.matmul(YB[:, 0:TILES * E], one_r[:], ohr[:], start=True, stop=True), "r.ohr t.one")
        dve("r.t", lambda eng, i: eng.tensor_copy(tot[:], YB[:, 0:TILES * E].rearrange("p (t e) -> p e t", e=E)), "r.tot")
        flat = lambda t: t[:].rearrange("p e t -> p (e t)")
        dve("r.cum", lambda eng, i: eng.tensor_tensor_scan(flat(cum), one_f[:], flat(tot), 0.0, ALU.mult, ALU.add), "t.onef")
        dve("r.exc", tt(exc[:], cum[:], tot[:], ALU.subtract))
        dve("r.cnt", tt(cnt[:], cum[:, :, TILES - 1], exc[:, :, 0], ALU.subtract))
        dve("r.many", tt(many[:], cnt[:, :, None].to_broadcast([P, E, TILES]), steps128[:, None, :].to_broadcast([P, E, TILES]), ALU.is_gt), "t.s128")
        dve("r.ntl", lambda eng, i: eng.reduce_sum(ntl[:], many[:], AX.X))
        dve("r.tc", lambda eng, i: eng.tensor_tensor_scan(tcum[:], one_f[:, 0:E], ntl[:], 0.0, ALU.mult, ALU.add))
        dve("r.b0", tt(base[:], tcum[:], ntl[:], ALU.subtract))
        dve("r.b1", lambda eng, i: eng.tensor_scalar(base[:], base[:], float(P), float(SPARE * P), ALU.mult, ALU.add))
        dve("r.b2", tt(base[:], base[:], exc[:, :, 0], ALU.subtract))
        dve("r.pos", tt(exc[:], exc[:], base[:, :, None].to_broadcast([P, E, TILES]), ALU.add))
        dve("r.row", tt(wt[:], XB[:, 0:TILES * E].rearrange("p (t e) -> p t e", e=E), exc[:].rearrange("p e t -> p t e"), ALU.add), "r.rank")
        dve("r.own", tt(wt[:], wt[:], oh[:], ALU.mult))
        dve("r.sum", lambda eng, i: eng.reduce_sum(slot_f[:], wt[:], AX.X))
        dve("r.slot", lambda eng, i: eng.tensor_copy(slot[:], slot_f[:]))
        dve("r.te", tt(te_c[:], tile_no[:, :, None].to_broadcast([1, RT, E - 1]), tcum[0:1, None, 0:E - 1].to_broadcast([1, RT, E - 1]), ALU.is_ge), "t.no")
        dve("r.tf", lambda eng, i: eng.reduce_sum(te_f[:], te_c[:], AX.X))
        dve("r.ti", lambda eng, i: eng.tensor_copy(te[:], te_f[:]))

        tb = Steps()
        tb.add("pool", "t.0", lambda eng, i: eng.memset(tri_f[:], 1.0))
        tb.add("pool", "t.1", lambda eng, i: eng.affine_select(out=tri_f[:], in_=tri_f[:], compare_op=ALU.is_gt, fill=0.0, base=0, pattern=[[1, P]], channel_multiplier=-1), "t.0")
        tb.add("pool", "t.tri", lambda eng, i: eng.tensor_copy(tri[:], tri_f[:]), "t.1")
        tb.add("pool", "t.onef", lambda eng, i: eng.memset(one_f[:], 1.0))
        tb.add("pool", "t.one", lambda eng, i: eng.tensor_copy(one_r[:], one_f[:, 0:P]), "t.onef")
        tb.add("pool", "t.s128", lambda eng, i: eng.iota(steps128[:], [[P, TILES]], base=0, channel_multiplier=0, allow_small_or_imprecise_dtypes=True), "t.one")
        tb.add("pool", "t.no", lambda eng, i: eng.iota(tile_no[:], [[1, RT]], base=0, channel_multiplier=0, allow_small_or_imprecise_dtypes=True), "t.s128")

        tb.steps += st.steps
        run(nc, sems, before=tb, loop=loop, count=NSEQ // 2, after=rt)

        sc, loop = Steps(), Steps()
        for t in range(TILES):
            sc.dma(f"sc{t}", (lambda t: lambda eng, i: eng.indirect_dma_start(
                xs[:, :], bass.IndirectOffsetOnAxis(slot[:, t:t + 1], 0), xn_all[:, t, :], None))(t), engine="pool")
        ring = [""] * 3
        weights(sc, second)
        by_slot = te[:].rearrange("o (n u) -> o n u", u=U)
        sc.add("dve", "te.0", lambda eng, i: eng.memset(te_tab[:], 0))
        sc.add("dve", "te.1", lambda eng, i: eng.tensor_copy(te_tab[:, 0:RT // U, 0:U], by_slot), "te.0")
        sc.add("dve", "te.2", lambda eng, i: eng.tensor_copy(te_tab[:, 0:RT // U, U + 2:2 * U], by_slot[:, :, 0:2]), "te.1")
        sc.add("dve", "te.3", lambda eng, i: eng.tensor_copy(te_tab[:, 1:RT // U + 1, U:U + 2], by_slot[:, :, 2:4]), "te.2")
        for q in range(2):
            sc.dma(f"s.a{q}", (lambda q: lambda eng, i: eng.dma_start(xp[q][:], tokens(xin, q)))(q), engine="act")
        jobs = [(q, c) for q in range(2) for c in range(HC)]
        nm = lambda kind, j: f"{kind}{j}" if j >= 0 else f"{kind}{j + len(jobs)}@1"

        def up(j):
            q, c = jobs[j]
            s, r = slice(c * P, (c + 1) * P), j % 2

            def emit(eng, i):
                at = bass.ds((i * 2 + q) * SEQ, SEQ)
                for u in range(NU):
                    x = three(eng, HB[2 * r + u][:], up_hi[u][:, E, s], up_lo[u][:, E, s], xT_hi[:, at], xT_lo[:, at], True, True)
                return x
            loop.add("pe", f"up{j}", emit, nm("f", j - 2))
            loop.add("act", f"g{j}", lambda eng, i: eng.activation(gel[r][:], HB[2 * r][:], ACT.Gelu), f"up{j} " + nm("f", j - 2))
            loop.add("dve", f"f{j}", lambda eng, i: eng.tensor_tensor(hf[j % 4][:], gel[r][:], HB[2 * r + 1][:], ALU.mult), f"g{j} " + nm("y", j - 4))

        def shared_down(j):
            q, c = jobs[j]
            Y = HT[q]

            def emit(eng, i):
                for k in range(NT):
                    t = slice(k * P, (k + 1) * P)
                    x = eng.matmul(Y[:, t], hf[j % 4][:, t], dn[:, E, c, :], start=c == 0 and k == 0, stop=c == HC - 1 and k == NT - 1, skip_group_check=True)
                return x
            loop.add("pe", f"y{j}", emit, f"f{j}" + (f" a{q}@1" if c == 0 else ""))
            if c == HC - 1:
                loop.add("dve", f"a{q}", lambda eng, i: eng.scalar_tensor_tensor(
                    acc_all[:, bass.ds((i * 2 + q) * NT, NT), :], Y[:].rearrange("p (k d) -> p k d", d=D), 0.5, xp[q][:], ALU.mult, ALU.add), f"y{j} x{q}@1 s.a{q}")
                loop.dma(f"x{q}", lambda eng, i: eng.dma_start(xp[q][:], tokens(xin, (i * 2 + (q + 2)) % NSEQ)), f"a{q}", engine="act")

        for j in range(len(jobs) + 2):
            if j < len(jobs):
                up(j)
            if j >= 2:
                shared_down(j - 2)
        run(nc, sems, before=sc, loop=loop, count=NSEQ // 2)

        LEAD = dict(ld=-4, T=-2, xh=-2, xl=-2, up=0, g=0, f=0, ht=1, hc=1, dn=2, yc=2, st=2)

        def tile_loop():
            pre, loop, post = Steps(), Steps(), Steps()
            regs = {}

            def ref(h, *wanted):
                out = []
                for kind, d in wanted:
                    back = -((h + d + LEAD[kind]) // U)
                    assert back >= 0
                    out.append(f"{kind}{(h + d) % U}" + (f"@{back}" if back else ""))
                return " ".join(out)

            def turn_in(part, name, t, after):
                part.add("pe", f"{name}T{t}", lambda eng, i: eng.transpose(XB[:, 0:P], xg[t][:], C["ident"][:]), after[0])
                part.add("act", f"{name}xh{t}", lambda eng, i: eng.copy(x_hi[t][:], XB[:, 0:P]), f"{name}T{t} " + after[1])
                part.add("dve", f"{name}xl{t}", lambda eng, i: eng.tensor_tensor(x_lo[t][:], XB[:, 0:P], x_hi[t][:].bitcast(F32), ALU.subtract), f"{name}xh{t}")

            def turn_hidden(part, name, h, after):
                t, r = (h - 1) % U, (h - 1) % 2

                def ht(eng, i):
                    for c in range(HC):
                        x = eng.transpose(HT[r][:, c * P:(c + 1) * P], hf[r][:, c * P:(c + 1) * P], C["ident"][:])
                    return x
                part.add("pe", f"{name}ht{t}", ht, after[0])
                part.add("act", f"{name}hc{t}", lambda eng, i: eng.copy(hT[r][:], HT[r][:]), f"{name}ht{t} " + after[1])

            def down(part, name, h, row, after):
                t, r = (h - 2) % U, h % 2

                def dn_(eng, i):
                    e = regs["down"][h]
                    W = lambda c: dn[:, bass.ds(e, 1), c, :].rearrange("p a n -> p (a n)")
                    for c in range(HC):
                        x = eng.matmul(YB[:, 0:D], hT[r][:, c * P:(c + 1) * P], W(c), start=c == 0, stop=c == HC - 1)
                    return x
                part.add("pe", f"{name}dn{t}", dn_, after[0])
                part.add("dve", f"{name}yc{t}", lambda eng, i: eng.tensor_copy(yb[r], YB[:, 0:D]), f"{name}dn{t} " + after[1])
                part.dma(f"{name}st{t}", lambda eng, i: eng.dma_start(ys[row(i), :], yb[r]), f"{name}yc{t}")

            def experts(eng, at, lo, n):
                _, r = nc.values_load_multi_w_load_instructions(te_tab[0:1, at, lo:lo + n], engines=(mybir.EngineType.PE,), min_val=0, max_val=E - 1)
                return list(r)

            for t in range(U):
                pre.dma(f"p.ld{t}", (lambda t: lambda eng, i: eng.dma_start(xg[t][:], xs[(SPARE + t) * P:(SPARE + t + 1) * P, :]))(t))
            turn_in(pre, "p.", 0, ("p.ld0", ""))
            turn_in(pre, "p.", 1, ("p.ld1 p.xl0", ""))
            pre.add("dve", "p.f", lambda eng, i: eng.memset(hf[1][:], 0.0))
            pre.add("dve", "p.h", lambda eng, i: eng.memset(hT[0][:], 0.0))
            for h in range(U):
                r = h % 2

                def up(eng, i, h=h, r=r):
                    if h == 0:
                        x = experts(eng, i, 0, 2 * U)
                        regs.update(up=x[:U], down=x[U:])
                    e = regs["up"][h]
                    W = lambda t: t[:, bass.ds(e, 1), :].rearrange("p a n -> p (a n)")
                    for u in range(NU):
                        x = three(eng, HB[2 * r + u][:], x_hi[h][:], x_lo[h][:], W(up_hi[u]), W(up_lo[u]), True, True)
                    return x
                loop.add("pe", f"up{h}", up, "p.xl1 " + ref(h, ("xl", 0), ("f", -2)))
                loop.add("act", f"g{h}", (lambda r: lambda eng, i: eng.activation(gel[r][:], HB[2 * r][:], ACT.Gelu))(r), ref(h, ("up", 0), ("f", -2)))
                loop.add("dve", f"f{h}", (lambda r: lambda eng, i: eng.tensor_tensor(hf[r][:], gel[r][:], HB[2 * r + 1][:], ALU.mult))(r), ref(h, ("g", 0), ("ht", -2)))
                turn_in(loop, "", (h + 2) % U, (ref(h, ("ld", 2), ("xl", 1)) + f" p.ld{(h + 2) % U} p.xl1", ref(h, ("up", -2))))
                loop.dma(f"ld{h}", (lambda h: lambda eng, i: eng.dma_start(xg[h][:], xs[bass.ds(((i * U + (h + 4)) % RT) * P + SPARE * P, P), :]))(h),
                         ref(h, ("T", 0)) + " p.T1")
                turn_hidden(loop, "", h, (ref(h, ("f", -1), ("hc", -3)) + " p.f", ref(h, ("dn", -3))))
                down(loop, "", h, (lambda h: lambda i: bass.ds(i * U * P + (h - 2 + SPARE) * P, P))(h), (ref(h, ("hc", -2), ("yc", -3)) + " p.h", ref(h, ("st", -4))))
            end = lambda k: slice((SPARE + RT - k) * P, (SPARE + RT - k + 1) * P)
            turn_hidden(post, "e.", U, ("f3 hc1", "dn1"))

            def last_experts(eng, i):
                regs["down"] = dict(zip((U, U + 1), experts(eng, slice(RT // U, RT // U + 1), U, 2)))
                return eng.transpose(XB[:, 0:P], xg[0][:], C["ident"][:])
            post.add("pe", "e.regs", last_experts, "xl1 ld0")
            down(post, "e.", U, lambda i: end(2), ("hc2 yc1", "st0"))
            down(post, "e.", U + 1, lambda i: end(1), ("e.hc3 e.yc2", "st1"))
            run(nc, sems, before=pre, loop=loop, count=RT // U, after=post)

        tile_loop()
        fin = Steps()
        for g in range(NSEQ):
            t0 = g * NT
            for t in range(t0, t0 + NT):
                fin.dma(f"sc{t}", (lambda t: lambda eng, i: eng.indirect_dma_start(
                    xn_all[:, t, :], None, ys[:, :], bass.IndirectOffsetOnAxis(slot[:, t:t + 1], 0)))(t), engine="pool")
            A, R = acc_all[:, t0:t0 + NT, :], xn_all[:, t0:t0 + NT, :]
            fin.add("dve", f"fb{g}", (lambda A, R: lambda eng, i: eng.scalar_tensor_tensor(A, R, 0.5, A, ALU.mult, ALU.add))(A, R),
                    " ".join(f"sc{t}" for t in range(t0, t0 + NT)))
            fin.dma(f"fo{g}", (lambda g, A: lambda eng, i: eng.dma_start(tokens(xout, g), A))(g, A), f"fb{g}")
        run(nc, sems, before=fin)


NAMES = ["L0_attn_x", "L0_attn_ln_gamma", "L0_attn_ln_beta", "L0_attn_in_proj_w", "L0_attn_conv_w", "L0_attn_conv_b",
         "L0_attn_x_proj_w", "L0_attn_dt_proj_w", "L0_attn_dt_proj_b", "L0_attn_A_log", "L0_attn_D", "L0_attn_out_proj_w",
         "L0_attn_glu_w", "L0_attn_glu_b", "L0_ffn_W_gate", "L0_ffn_W1", "L0_ffn_b1", "L0_ffn_W2", "L0_ffn_b2",
         "L1_attn_Wqkv", "L1_attn_bqkv", "L1_attn_Wout", "L1_attn_bout", "L1_ffn_w1s", "L1_ffn_w2s", "L1_ffn_w3s",
         "L1_ffn_W1", "L1_ffn_W2", "L1_ffn_W3", "L1_ffn_Wg"]
TRANSPOSED = ("L1_attn_Wqkv", "L1_attn_Wout")


def program(nc, a, out):
    with ExitStack() as ctx:
        sems = Sems(nc, ctx)
        C = consts(nc, sems, lambda name, shape, dt=F32: ctx.enter_context(nc.sbuf_tensor(name, shape, dt)))
        bank = [ctx.enter_context(nc.psum_tensor(f"bank{b}", [P, SEQ], F32)) for b in range(8)]
        x = [a["L0_attn_x"]] + [nc.dram_tensor(f"x{k}", [NSEQ * SEQ, D], F32, kind="Internal").ap() for k in range(1, 6)] + [out]
        xs = nc.dram_tensor("xs", [XS_TILES * P, D], F32, kind="Internal").ap()
        ys = nc.dram_tensor("ys", [XS_TILES * P, D], F32, kind="Internal").ap()
        clear_rows(nc, sems, xs)
        f0, f1 = ffn0_weights(a), ffn1_weights(a)
        ffn0(nc, sems, C, bank, x[0], x[1], f0)
        mamba(nc, sems, C, bank, x[1], x[2], a)
        ffn0(nc, sems, C, bank, x[2], x[3], f0 | {"tag": "_f0b"})
        ffn1(nc, sems, C, bank, x[3], x[4], f1, xs, ys)
        attention(nc, sems, C, bank, x[4], x[5], a)
        ffn1(nc, sems, C, bank, x[5], x[6], f1 | {"tag": "_f1b"}, xs, ys)


def kernel(**inputs):
    import concourse.bacc as bacc
    from concourse.bass_utils import run_bass_kernel_spmd

    nc = bacc.Bacc("TRN2", target_bir_lowering=False, num_devices=1)
    arrays, a = {}, {}
    for name in NAMES:
        v = np.asarray(inputs[name])
        if name == "L0_attn_x":
            v = v.reshape(NSEQ * SEQ, D)
        if name in TRANSPOSED:
            v = v.T
        v = np.ascontiguousarray(v)
        arrays["in_" + name] = v
        a[name] = nc.dram_tensor("in_" + name, v.shape, mybir.dt.from_np(v.dtype), kind="ExternalInput").ap()
    out = nc.dram_tensor("out_0", [NSEQ * SEQ, D], F32, kind="ExternalOutput").ap()
    program(nc, a, out)
    r = run_bass_kernel_spmd(nc, [arrays], core_ids=[0])
    return r.results[0]["out_0"].reshape(NSEQ, SEQ, D)
```

```python
from contextlib import ExitStack

import numpy as np
import concourse.bass as bass
from concourse import mybir

F32 = mybir.dt.float32
F32R = mybir.dt.float32r
ALU = mybir.AluOpType
ACT = mybir.ActivationFunctionType
AX = mybir.AxisListType

NSEQ, SEQ, D = 8, 512, 128
P = 128
NT = SEQ // P
EPS = 1e-5
E = 8
HID = 512
HC = HID // P
INNER, NST, RANK, TAPS = 256, 16, 8, 4
NH = INNER // P
HEADS, WIN = 16, 64
HD = D // HEADS
HG = 4
QB = 32
PAD = WIN // 2
KW = 96

ENGINES = ("pe", "act", "dve", "pool", "sp")
HEADROOM = 1 << 14


class Sems:

    def __init__(self, nc, ctx):
        self.nc, self.ctx = nc, ctx
        self.sem = {e: ctx.enter_context(nc.semaphore("done_" + e)) for e in ENGINES}
        self.at = {e: HEADROOM for e in ENGINES}
        self.started = False

    def dma(self, name, start):
        self.sem[name] = self.ctx.enter_context(self.nc.semaphore("dma_" + name))
        self.at[name] = start


class Steps:

    def __init__(self):
        self.steps = []

    def add(self, engine, name, emit, after=()):
        self.steps.append((engine, name, emit, after.split() if isinstance(after, str) else list(after), False))

    def dma(self, name, emit, after="", engine="sp"):
        self.steps.append((engine, name, emit, after.split(), True))


def run(nc, sems, before=None, loop=None, count=0, after=None):
    parts = [(p, n) for p, n in ((before, 1), (loop, count), (after, 1)) if p is not None]
    place, new, at = {}, [], dict(sems.at)
    per_part = []
    for part, n in parts:
        per, base = {}, {}
        looped = part is loop
        for engine, name, _, _, is_dma in part.steps:
            assert name not in place, name
            if is_dma:
                if name not in sems.sem:
                    sems.dma(name, 0 if engine == "pool" else HEADROOM)
                    at[name] = sems.at[name]
                    if engine != "pool":
                        new.append(name)
                s, k = name, 16
                per[s] = 16
            else:
                s = engine
                k = per[s] = per.get(s, 0) + 1
            base.setdefault(s, at[s])
            place[name] = (s, k, looped, base)
        for s in per:
            at[s] += per[s] * n
        per_part.append(per)
    new_engines, sems.started = not sems.started, True

    def emit_all(part, n, per, engine, eng, i):
        waited = {}
        for who, name, emit, after_, is_dma in part.steps:
            if who != engine:
                continue
            for a in after_:
                what, _, lag = a.partition("@")
                s, k, looped, base = place[what]
                inside = looped and part is loop
                if inside:
                    rel = k - int(lag or 0) * per[s]
                else:
                    rel = k + (per_part[parts.index((loop, count))][s] * (count - 1) if looped else 0)
                key, value = (s, inside), base[s] + rel
                if waited.get(key, -HEADROOM) >= value:
                    continue
                waited[key] = value
                eng.wait_ge(sems.sem[s], i * per[s] + value if inside else value)
            emit(eng, i).then_inc(sems.sem[name if is_dma else engine], 16 if is_dma else 1)

    def stream(engine):
        def body(eng):
            if new_engines:
                eng.sem_inc(sems.sem[engine], HEADROOM)
            if engine == "sp":
                for n in new:
                    eng.sem_inc(sems.sem[n], HEADROOM)
            for (part, n), per in zip(parts, per_part):
                if part is not loop:
                    emit_all(part, n, per, engine, eng, None)
                elif any(s[0] == engine for s in part.steps):
                    with eng.Fori(0, count) as i:
                        emit_all(part, n, per, engine, eng, i)
            if engine == "sp":
                for part, _ in parts:
                    for s in part.steps:
                        if s[4]:
                            eng.wait_ge(sems.sem[s[1]], at[s[1]])
        return body

    with nc.Block() as block:
        block.sync(stream("sp"))
        block.gpsimd(stream("pool"))
        block.scalar(stream("act"))
        block.vector(stream("dve"))
        block.tensor(stream("pe"))
    sems.at.update(at)


def weave(main, side):
    out, j = [], 0
    for k, b in enumerate(main):
        out.append(b)
        while j < len(side) and (j + 1) * len(main) <= (k + 1) * len(side):
            out.append(side[j])
            j += 1
    return out + side[j:]


def merge(main, side):
    out, n, m = [], len(main.steps), len(side.steps)
    j = 0
    for k, s in enumerate(main.steps):
        out.append(s)
        while j < m and (j + 1) * n <= (k + 1) * m:
            out.append(side.steps[j])
            j += 1
    out += side.steps[j:]
    main.steps = out
    return main


def tokens(dram, g):
    return dram[bass.ds(g * SEQ, SEQ), :].rearrange("(k p) d -> p k d", p=P)


def group_of(i, par, ahead=0):
    if i is None:
        return par
    return i * 2 + (par + ahead) if par + ahead < 2 else (i * 2 + 2) % NSEQ


def layernorm(st, n, src, dst, T, after, write_after=""):
    stats, mv, sd, rs = T["stats"], T["mv"], T["sd"], T["rs"]

    def bn(eng, i):
        for k in range(NT):
            x = eng.bn_stats(stats[:, k, :], src[:, k, :])
        return x

    def agg(eng, i):
        eng.memset(T["tick"][:], 0.0)
        for k in range(NT):
            x = eng.bn_aggr(mv[:, k, :], stats[:, k, :])
        return x

    def norm(eng, i):
        for k in range(NT):
            x = eng.tensor_scalar(dst[:, k, :], src[:, k, :], mv[:, k, 0:1], rs[:, k:k + 1], ALU.subtract, ALU.mult)
        return x

    st.add("dve", n + ".stats", bn, after)
    st.add("dve", n + ".mv", agg, n + ".stats")
    st.add("act", n + ".sd", lambda eng, i: eng.activation(sd[:], mv[:, :, 1], ACT.Sqrt, bias=T["eps"][:, 0:1]), n + ".mv")
    st.add("dve", n + ".rs", lambda eng, i: eng.reciprocal(rs[:], sd[:]), n + ".sd")
    st.add("dve", n + ".out", norm, n + ".rs " + write_after)


def ln_tiles(sb):
    return dict(stats=sb("stats", [P, NT, 6]), mv=sb("mv", [P, NT, 2]), sd=sb("sd", [P, NT]), rs=sb("rs", [P, NT]), tick=sb("tick", [P, 1]))


def transposes(out, src, ident, n=NT):
    def emit(eng, i):
        for k in range(n):
            x = eng.transpose(out[:, k * P:(k + 1) * P], src[:, k, :], ident[:])
        return x
    return emit


def split_weight(st, name, dram, raw, hi, lo, free=""):
    st.dma(name, lambda eng, i: eng.dma_start(raw, dram), free)
    st.add("pool", name + ".hi", lambda eng, i: eng.tensor_copy(hi, raw), name)
    st.add("pool", name + ".lo", lambda eng, i: eng.tensor_tensor(lo, raw, hi.bitcast(F32), ALU.subtract), name + ".hi")


def three(eng, out, ahi, alo, bhi, blo, start, stop, skip=False):
    eng.matmul(out, ahi, bhi, start=start, stop=False, skip_group_check=skip)
    eng.matmul(out, ahi, blo, start=False, stop=False, skip_group_check=skip)
    return eng.matmul(out, alo, bhi, start=False, stop=stop, skip_group_check=skip)


def before_first(names):
    return " ".join(n + (" s" + n[1:-2] if n.startswith("p0.") and n.endswith("@1") else "") for n in names.split())


def ffn0(nc, sems, C, bank, xin, xout, w, spare=0, xs=None):
    with ExitStack() as ctx:
        def sb(name, shape, dt=F32):
            return ctx.enter_context(nc.sbuf_tensor(name + w["tag"], shape, dt))

        T = ln_tiles(sb)
        T["eps"] = C["eps"]
        up_hi, up_lo = sb("up_hi", [P, E, HID], F32R), sb("up_lo", [P, E, HID], F32R)
        dn = sb("dn", [P, E, HC, D])
        wg = sb("wg", [P, E])
        b1, b1_rows = sb("b1", [P, E, HC]), sb("b1_rows", [E * HC, P])
        b2 = sb("b2", [E, D])
        raw = [sb(f"raw{r}", [P, HID]) for r in range(4)]
        xp, xn = sb("xp", [P, NT, D]), sb("xn", [P, NT, D])
        xT = [sb(f"xT{p}", [P, SEQ]) for p in range(2)]
        xT_hi = [sb(f"xT_hi{p}", [P, SEQ], F32R) for p in range(2)]
        xT_lo = [sb(f"xT_lo{p}", [P, SEQ], F32R) for p in range(2)]
        lg = sb("lg", [P, NT, E])
        top = sb("top", [P, NT, 8])
        sel, ex, den = sb("sel", [P, NT, E]), sb("ex", [P, NT, E]), sb("den", [P, NT])
        mk = [sb(f"mk{p}", [P, NT, E]) for p in range(2)]
        mkT = sb("mkT", [E, SEQ])
        acc = [sb(f"acc{p}", [P, NT, D]) for p in range(2)]
        NR = 4
        hf = [sb(f"hf{r}", [P, SEQ]) for r in range(NR)]
        HB, YB = bank[0:4], bank[4:6]
        TB, GB = bank[6], bank[7]

        st = Steps()
        st.dma("wg", lambda eng, i: eng.dma_start(wg[:], w["gate"]))
        st.dma("b1.ld", lambda eng, i: eng.dma_start(b1_rows[:], w["b1"]))
        st.dma("b2.ld", lambda eng, i: eng.dma_start(b2[:], w["b2"]))
        st.add("pe", "b1.T", lambda eng, i: eng.transpose(GB[:, 0:E * HC], b1_rows[:], C["ident"][0:E * HC, 0:E * HC]), "b1.ld")
        st.add("dve", "b1", lambda eng, i: eng.tensor_copy(b1[:].rearrange("p e c -> p (e c)"), GB[:, 0:E * HC]), "b1.T")
        wl = Steps()
        for e in range(E):
            split_weight(wl, f"w{e}", w["up"](e), raw[e % 4][:], up_hi[:, e, :], up_lo[:, e, :], f"w{e - 4}.lo" if e >= 4 else "")
            wl.dma(f"wd{e}", (lambda e: lambda eng, i: eng.dma_start(dn[:, e, :, :], w["down"](e)))(e))

        def prep(st, par, ahead, q):
            n = f"p{q}" if ahead else f"s{q}"
            last = lambda names: before_first(names) if ahead else ""
            back = "@1" if q == 1 else ""
            prev = f"p{1 - q}"
            st.dma(f"{n}.x", lambda eng, i: eng.dma_start(xp[:], tokens(xin, group_of(i, par, ahead) + spare)), last(f"{prev}.ln.out{back}"))
            layernorm(st, n + ".ln", xp, xn, T, f"{n}.x", last(f"{prev}.T{back}"))
            st.add("pe", n + ".T", transposes(TB, xn, C["ident"]), n + ".ln.out " + last(f"{prev}.xlo{back}"))
            free = last(f"h{q}.last{back}")
            st.add("act", n + ".xT", lambda eng, i: eng.copy(xT[q][:], TB[:]), n + ".T " + last(f"{n}.gate@1"))
            st.add("act", n + ".xhi", lambda eng, i: eng.copy(xT_hi[q][:], TB[:]), free)
            st.add("dve", n + ".xlo", lambda eng, i: eng.tensor_tensor(xT_lo[q][:], TB[:], xT_hi[q][:].bitcast(F32), ALU.subtract), n + ".xhi")

            def gate(eng, i):
                for k in range(NT):
                    x = eng.matmul(GB[:, k * E:(k + 1) * E], xT[q][:, k * P:(k + 1) * P], wg[:], start=True, stop=True)
                return x
            st.add("pe", n + ".gate", gate, n + ".xT " + last(f"{prev}.lg{back} c{1 - q}.acc"))
            st.add("dve", n + ".lg", lambda eng, i: eng.tensor_copy(lg[:], GB[:, 0:NT * E].rearrange("p (k e) -> p k e", e=E)), n + ".gate")

            def top8(eng, i):
                eng.memset(T["tick"][:], 0.0)
                for k in range(NT):
                    x = eng.max(top[:, k, :], lg[:, k, :])
                return x
            st.add("dve", n + ".top", top8, n + ".lg")
            second, first = top[:, :, 1:2].to_broadcast([P, NT, E]), top[:, :, 0:1].to_broadcast([P, NT, E])
            st.add("dve", n + ".sel", lambda eng, i: eng.tensor_tensor(sel[:], lg[:], second, ALU.is_ge), n + ".top")
            st.add("dve", n + ".sub", lambda eng, i: eng.tensor_tensor(lg[:], lg[:], first, ALU.subtract), n + ".sel")
            st.add("act", n + ".exp", lambda eng, i: eng.activation(ex[:], lg[:], ACT.Exp), n + ".sub")
            st.add("dve", n + ".pick", lambda eng, i: eng.tensor_tensor(ex[:], ex[:], sel[:], ALU.mult), n + ".exp")
            st.add("dve", n + ".sum", lambda eng, i: eng.reduce_sum(den[:], ex[:], AX.X), n + ".pick")
            st.add("dve", n + ".rec", lambda eng, i: eng.reciprocal(den[:], den[:]), n + ".sum")
            st.add("dve", n + ".wsum", lambda eng, i: eng.tensor_tensor(ex[:], ex[:], den[:, :, None].to_broadcast([P, NT, E]), ALU.mult), n + ".rec")
            st.add("dve", n + ".mk", lambda eng, i: eng.tensor_scalar(mk[q][:], ex[:], 0.5 / E, None, ALU.mult), n + ".wsum " + last(f"acc{q}.last{back}"))

        pre = Steps()
        prep(pre, 0, 0, 0)
        needs = {"s0.gate": ["wg", "b1"]}
        st.steps += [(a, b, c, d + needs.get(b, []), f) for a, b, c, d, f in pre.steps] + wl.steps
        if xs is not None:
            zero = sb("zero", [P, CLEAR, D])
            st.add("pool", "zero", lambda eng, i: eng.memset(zero[:], 0.0))

        loop = Steps()
        for q in range(2):
            main, side = Steps(), Steps()
            jobs = [(e, c) for e in range(E) for c in range(HC)]
            back = "" if q else "@1"
            pn, px = before_first(f"p{q}.mk{back}"), before_first(f"p{q}.xlo{back}")

            main.dma(f"acc{q}.x", lambda eng, i, q=q: eng.dma_start(acc[q][:], tokens(xin, group_of(i, q) + spare)), f"out{q}@1")

            def mT(eng, i, q=q):
                for k in range(NT):
                    x = eng.transpose(GB[0:E, k * P:(k + 1) * P], mk[q][:, k, :], C["ident"][:])
                return x
            bias = Steps()
            bias.add("pe", f"c{q}.T", mT, before_first(f"p{q}.mk{back} p{q}.lg{back}") + f" c{1 - q}.acc{back}")
            bias.add("act", f"c{q}.mT", lambda eng, i: eng.copy(mkT[:], GB[0:E, :]), f"c{q}.T c{1 - q}.mm{back}")

            def b2mm(eng, i):
                for k in range(NT):
                    x = eng.matmul(GB[:, k * P:(k + 1) * P], mkT[:, k * P:(k + 1) * P], b2[:], start=True, stop=True)
                return x
            bias.add("pe", f"c{q}.mm", b2mm, f"c{q}.mT b2.ld")
            bias.add("dve", f"c{q}.acc", lambda eng, i, q=q: eng.tensor_tensor(acc[q][:], acc[q][:], GB[:].rearrange("p (k d) -> p k d", d=D), ALU.add), f"c{q}.mm a{q}.2")

            def nm(kind, j, dj=0):
                k = j - dj
                return f"{kind}{q}.{k}" if k >= 0 else f"{kind}{1 - q}.{k + len(jobs)}{back}"

            def up(j, q=q):
                e, c = jobs[j]
                s, r = slice(c * P, (c + 1) * P), j % NR
                name = f"h{q}.last" if j == len(jobs) - 1 else f"h{q}.{j}"
                weight = f" w{e}.lo" if c == 0 else ""
                main.add("pe", name, lambda eng, i: three(eng, HB[j % 4][:], up_hi[:, e, s], up_lo[:, e, s], xT_hi[q][:], xT_lo[q][:], True, True),
                         px + " " + nm("f", j, 4) + weight)
                b = b1[:, e, c:c + 1]
                if j % 5 in (1, 3):
                    main.add("dve", f"f{q}.{j}", lambda eng, i: eng.tensor_scalar(hf[r][:], HB[j % 4][:], b, 0.0, ALU.add, ALU.max), name + " " + nm("y", j, NR) + " b1")
                else:
                    main.add("act", f"f{q}.{j}", lambda eng, i: eng.activation(hf[r][:], HB[j % 4][:], ACT.Relu, bias=b), name + " " + nm("y", j, NR) + " b1")

            def down(j, q=q):
                e, c = jobs[j]
                r, Y = j % NR, YB[e % 2]

                def emit(eng, i):
                    for k in range(NT):
                        t = slice(k * P, (k + 1) * P)
                        x = eng.matmul(Y[:, t], hf[r][:, t], dn[:, e, c, :], start=c == 0 and k == 0, stop=c == HC - 1 and k == NT - 1, skip_group_check=True)
                    return x
                free = (f"a{q}.{e - 2}" if e >= 2 else f"a{1 - q}.{E - 2}{back}" if e == 0 else f"acc{1 - q}.last{back}") if c == 0 else ""
                main.add("pe", f"y{q}.{j}", emit, f"f{q}.{j} wd{e} " + free)
                if c == HC - 1:
                    def accum(eng, i):
                        for k in range(NT):
                            x = eng.scalar_tensor_tensor(acc[q][:, k, :], Y[:, k * P:(k + 1) * P], mk[q][:, k, e:e + 1], acc[q][:, k, :], ALU.mult, ALU.add)
                        return x
                    prev = f"acc{q}.x" if e == 0 else f"a{q}.{e - 1}"
                    main.add("dve", f"acc{q}.last" if e == E - 1 else f"a{q}.{e}", accum, f"y{q}.{j} {pn} " + prev + (f" c{q}.acc" if e == 3 else ""))

            LEAD = 2
            for j in range(len(jobs) + LEAD):
                if j < len(jobs):
                    up(j)
                if j >= LEAD:
                    down(j - LEAD)
                if j in (4, 8, 12, 16):
                    main.steps.append(bias.steps[j // 4 - 1])
            main.dma(f"out{q}", lambda eng, i, q=q: eng.dma_start(tokens(xout, group_of(i, q)), acc[q][:]), f"acc{q}.last")
            prep(side, q, 1, 1 - q)
            a, b = len(main.steps) * 3 // 8, len(main.steps) * 7 // 8
            mid = Steps()
            mid.steps = main.steps[a:b]
            loop.steps += main.steps[:a] + merge(mid, side).steps + main.steps[b:]
            if xs is not None and q == 0:
                loop.dma("clear", lambda eng, i: eng.dma_start(xs[bass.ds(i * (CLEAR * P), CLEAR * P), :].rearrange("(k p) d -> p k d", p=P), zero[:]), "zero")
        run(nc, sems, before=st, loop=loop, count=NSEQ // 2)


def consts(nc, sems, sb):
    C = dict(ident=sb("ident", [P, P]), eps=sb("eps", [P, 1]), one=sb("one", [P, 1]), pow2=sb("pow2", [P, E]))
    st = Steps()
    st.add("pool", "c.id0", lambda eng, i: eng.memset(C["ident"][:], 0.0))
    st.add("pool", "c.id", lambda eng, i: eng.affine_select(out=C["ident"][:], in_=C["ident"][:], compare_op=ALU.not_equal, fill=1.0,
                                                          base=0, pattern=[[-1, P]], channel_multiplier=1), "c.id0")
    st.add("pool", "c.one", lambda eng, i: eng.memset(C["one"][:], 1.0))
    st.add("pool", "c.eps", lambda eng, i: eng.memset(C["eps"][:], EPS))

    def powers(eng, i):
        for e in range(E):
            x = eng.memset(C["pow2"][:, e:e + 1], float(1 << (E - 1 - e)))
        return x
    st.add("pool", "c.pow2", powers)
    run(nc, sems, before=st)
    return C


def ffn0_weights(a):
    return dict(tag="_f0", up=lambda e: a["L0_ffn_W1"][e], down=lambda e: a["L0_ffn_W2"][e].rearrange("(c p) d -> p c d", p=P),
                gate=a["L0_ffn_W_gate"], b1=a["L0_ffn_b1"].rearrange("e (c p) -> (e c) p", p=P), b2=a["L0_ffn_b2"])


def ffn1_weights(a):
    def pick(shared, routed):
        return lambda e: a[routed][e] if e < E else a[shared]
    return dict(tag="_f1", up=[pick("L1_ffn_w1s", "L1_ffn_W1"), pick("L1_ffn_w2s", "L1_ffn_W2")],
                down=lambda e: pick("L1_ffn_w3s", "L1_ffn_W3")(e).rearrange("(c p) d -> p c d", p=P), gate=a["L1_ffn_Wg"])


def mamba(nc, sems, C, bank, xin, xout, a):
    with ExitStack() as ctx:
        def sb(name, shape, dt=F32):
            return ctx.enter_context(nc.sbuf_tensor(name + "_m", shape, dt))

        def two(name, shape, dt=F32):
            return [sb(name + str(p), shape, dt) for p in range(2)]

        T = ln_tiles(sb)
        T["eps"] = C["eps"]
        w_in = sb("w_in", [P, 2 * INNER])
        w_bc = sb("w_bc", [P, NH, P])
        w_dt = sb("w_dt", [P, NH, RANK])
        w_dt2 = sb("w_dt2", [RANK, INNER])
        w_out = sb("w_out", [P, NH, D])
        w_glu = sb("w_glu", [P, 2 * D])
        b_glu = sb("b_glu", [1, 2 * D])
        ones = sb("ones", [1, P])
        rows = sb("rows", [64, P])
        cols = sb("cols", [P, 64])
        a_log = sb("a_log", [P, NH, NST])
        a_neg = sb("a_neg", [P, NH, NST])
        conv_w = sb("conv_w", [P, NH, TAPS])
        diag = sb("diag", [P, NH, TAPS, P])
        sel = sb("sel", [P, NST, P], F32R)
        sel_f = sb("sel_f", [P, NST, P])
        xp = sb("xp", [P, NT, D])
        xn = sb("xn", [P, NT, D])
        xm = sb("xm", [P, NT, D])
        skip = two("skip", [P, NT, D])
        hT = sb("hT", [P, SEQ])
        xi = sb("xi", [P, NH, TAPS - 1 + SEQ])
        u = two("u", [P, NH, SEQ])
        sz = two("sz", [P, NH, SEQ])
        bc_rows = two("bc_rows", [P, SEQ], F32R)
        dtr = sb("dtr", [RANK, SEQ])
        v, ab = two("v", [P, SEQ]), two("ab", [P, SEQ])
        dt = two("dt", [P, NH, SEQ])
        du = two("du", [P, NH, SEQ])
        RA, RP = 8, 4
        da = [sb(f"da{r}", [P, SEQ]) for r in range(RA)]
        db = [sb(f"db{r}", [P, SEQ]) for r in range(4)]
        hs = [sb(f"hs{r}", [P, SEQ]) for r in range(4)]
        ph = [sb(f"ph{r}", [P, SEQ]) for r in range(RP)]
        y2 = [sb(f"y2{r}", [P, SEQ]) for r in range(2)]
        gT = sb("gT", [P, SEQ])
        sg = sb("sg", [P, NT, D])
        o = two("o", [P, NT, D])
        SB, SC, SY, SX = bank[0:2], bank[2:4], bank[4:6], bank[6:8]
        GAM, BET, CB, DV, DB, = 0, 1, 2, 4, 6

        st = Steps()
        row = lambda ap: ap.rearrange("(h p) -> h p", p=P)
        for k, (nm, ap, n) in enumerate([("L0_attn_ln_gamma", GAM, 1), ("L0_attn_ln_beta", BET, 1), ("L0_attn_conv_b", CB, 2),
                                         ("L0_attn_D", DV, 2), ("L0_attn_dt_proj_b", DB, 2)]):
            st.dma(f"mv{k}", lambda eng, i, nm=nm, ap=ap, n=n: eng.dma_start(rows[ap:ap + n, :], row(a[nm])))
        st.add("pe", "rowsT", lambda eng, i: eng.transpose(SX[0][:, 0:8], rows[0:8, :], C["ident"][0:8, 0:8]), "mv0 mv1 mv2 mv3 mv4")
        st.add("dve", "cols", lambda eng, i: eng.tensor_copy(cols[:, 0:8], SX[0][:, 0:8]), "rowsT")
        st.dma("mw0", lambda eng, i: eng.dma_start(w_in[:], a["L0_attn_in_proj_w"]))
        xw = a["L0_attn_x_proj_w"].rearrange("(h p) n -> p h n", p=P)
        st.add("pool", "z0", lambda eng, i: eng.memset(w_bc[:], 0.0))
        st.dma("mw1", lambda eng, i: eng.dma_start(w_dt[:], xw[:, :, 0:RANK]))
        for k, (at, o0) in enumerate([(0, RANK), (32, RANK), (64, RANK + NST), (96, RANK + NST)]):
            st.dma(f"mx{k}", lambda eng, i, at=at, o0=o0: eng.dma_start(w_bc[:, :, at:at + NST], xw[:, :, o0:o0 + NST]), "z0")
        st.dma("mw2", lambda eng, i: eng.dma_start(w_dt2[:], a["L0_attn_dt_proj_w"]))
        st.dma("mw3", lambda eng, i: eng.dma_start(w_out[:], a["L0_attn_out_proj_w"].rearrange("(h p) n -> p h n", p=P)))
        st.dma("mw4", lambda eng, i: eng.dma_start(w_glu[:], a["L0_attn_glu_w"]))
        st.dma("mw5", lambda eng, i: eng.dma_start(b_glu[:], a["L0_attn_glu_b"].rearrange("(o n) -> o n", o=1)))
        st.dma("mw6", lambda eng, i: eng.dma_start(a_log[:], a["L0_attn_A_log"].rearrange("(h p) n -> p h n", p=P)))
        st.dma("mw7", lambda eng, i: eng.dma_start(conv_w[:], a["L0_attn_conv_w"].rearrange("(h p) n -> p h n", p=P)))
        st.add("pool", "z2", lambda eng, i: eng.memset(ones[:], 1.0))
        st.add("pool", "z3", lambda eng, i: eng.memset(xi[:, :, 0:TAPS - 1], 0.0))
        st.add("pool", "z4", lambda eng, i: eng.memset(sel_f[:], 0.0))
        for k, off in enumerate((0, 32, 64, 96)):
            st.add("pool", f"z5{k}", lambda eng, i, off=off: eng.affine_select(
                out=sel_f[:], in_=sel_f[:], compare_op=ALU.not_equal, fill=1.0, base=-off, pattern=[[-1, NST], [0, P]],
                channel_multiplier=1), "z4" if k == 0 else f"z5{k - 1}")
        st.add("dve", "sel", lambda eng, i: eng.tensor_copy(sel[:], sel_f[:]), "z53")
        st.add("act", "a.exp", lambda eng, i: eng.activation(a_neg[:], a_log[:], ACT.Exp), "mw6")
        st.add("dve", "a.neg", lambda eng, i: eng.tensor_scalar(a_neg[:], a_neg[:], -1.0, None, ALU.mult), "a.exp")

        def taps(eng, i):
            for h in range(NH):
                for k in range(TAPS):
                    x = eng.tensor_scalar(diag[:, h, k, :], C["ident"][:], conv_w[:, h, k:k + 1], None, ALU.mult)
            return x
        st.add("dve", "diag", taps, "mw7")

        def prep(q, start=False):
            n = "s0" if start else f"p{q}"
            back = "@1" if q == 1 else ""
            last = lambda names: "" if start else " " + before_first(names)
            prev = f"p{1 - q}"
            g = lambda i: 0 if start else i * 2 + 1 if q else (i * 2 + 2) % NSEQ
            free = last(f"fin{q}")
            out, st = [], Steps()

            def bundle(gap=0):
                out.append(list(st.steps))
                st.steps.clear()
                out.extend([] for _ in range(gap))

            st.dma(n + ".x", lambda eng, i: eng.dma_start(xp[:], tokens(xin, g(i))), last(f"{prev}.skip{back}"))
            layernorm(st, n + ".ln", xp, xn, T, n + ".x", last(f"{prev}.skip{back}"))
            st.add("dve", n + ".skip", lambda eng, i: eng.tensor_tensor(skip[q][:], xp[:], xn[:], ALU.add), n + ".ln.out" + free)
            layernorm(st, n + ".l2", xn, xm, T, n + ".ln.out", last(f"{prev}.T{back}"))
            for x in st.steps:
                out.append([x])
                if x[1].endswith((".mv", ".sd")):
                    out.append([])
            st.steps.clear()
            st.add("pe", n + ".T", transposes(SX[0], xm, C["ident"]), n + ".l2.out" + last(f"{prev}.v1{back} go{q}.1"))
            bundle(1)
            st.add("dve", n + ".h", lambda eng, i: eng.tensor_scalar(hT[:], SX[0][:], cols[:, GAM:GAM + 1], cols[:, BET:BET + 1], ALU.mult, ALU.add),
                   n + ".T" + last(f"{prev}.in3{back}"))
            bundle()

            def inp(c):
                X = SX[(c + 1) % 2]
                busy = {0: last(f"{prev}.v0{back} go{q}.0"), 1: ""}.get(c) if c < 2 else f" {n}.e{c - 2}"
                st.add("pe", f"{n}.in{c}", lambda eng, i: eng.matmul(X[:], w_in[:, c * P:(c + 1) * P], hT[:], start=True, stop=True), f"{n}.h" + busy)

            def gate_or_inner(c):
                X = SX[(c + 1) % 2]
                if c < NH:
                    st.add("act", f"{n}.e{c}", lambda eng, i: eng.copy(xi[:, c, TAPS - 1:], X[:]), f"{n}.in{c}" + last(f"{prev}.c{c}.1{back}"))
                else:
                    st.add("act", f"{n}.e{c}", lambda eng, i: eng.activation(sz[q][:, c - NH, :], X[:], ACT.Silu), f"{n}.in{c}" + free)

            for step in (inp, gate_or_inner):
                for c in range(NH):
                    step(c)
                    bundle()
                out.append([])
            for c in (2, 3):
                inp(c)
                bundle()
            gate_or_inner(2)
            gate_or_inner(3)
            bundle()
            for h in range(NH):
                for part in range(2):
                    def conv(eng, i, h=h, part=part):
                        for k in (2 * part, 2 * part + 1):
                            x = eng.matmul(SX[(h + 1) % 2][:], diag[:, h, k, :], xi[:, h, k:k + SEQ], start=k == 0, stop=k == TAPS - 1)
                        return x
                    st.add("pe", f"{n}.c{h}.{part}", conv, f"{n}.e{h} {n}.e{h + 2}")
                    bundle(part)
            for h in range(NH):
                st.add("act", f"{n}.u{h}", (lambda h: lambda eng, i: eng.activation(u[q][:, h, :], SX[(h + 1) % 2][:], ACT.Silu, bias=cols[:, CB + h:CB + h + 1]))(h),
                       f"{n}.c{h}.1" + free)
            bundle()

            def proj(X, w, m):
                def emit(eng, i):
                    for h in range(NH):
                        x = eng.matmul(X[0:m, :], w[:, h, :], u[q][:, h, :], start=h == 0, stop=h == NH - 1)
                    return x
                return emit
            st.add("pe", f"{n}.bc", proj(SX[1], w_bc, P), f"{n}.u1 {n}.e2")
            bundle(1)
            st.add("pe", n + ".dtr", proj(SX[0], w_dt, RANK), f"{n}.u1 {n}.e3")
            bundle()
            st.add("act", f"{n}.sph", lambda eng, i: eng.copy(bc_rows[q][:], SX[1][:]), f"{n}.bc" + free)
            bundle(1)
            for k in range(2):
                p = slice(64 * k + 32, 64 * k + 64)
                st.add("dve", f"{n}.spl{k}", (lambda p: lambda eng, i: eng.tensor_tensor(bc_rows[q][p, :], SX[1][p, :], bc_rows[q][p, :].bitcast(F32), ALU.subtract))(p),
                       f"{n}.sph")
            bundle()
            st.add("act", n + ".dtr.s", lambda eng, i: eng.copy(dtr[:], SX[0][0:RANK, :]), n + ".dtr" + last(f"{prev}.dt1{back}"))
            bundle(1)
            for h in range(NH):
                st.add("pe", f"{n}.dt{h}", (lambda h: lambda eng, i: eng.matmul(SX[(h + 1) % 2][:], w_dt2[:, h * P:(h + 1) * P], dtr[:], start=True, stop=True))(h),
                       f"{n}.dtr.s {n}.spl1")
                bundle(h)
            for h in range(NH):
                bias = cols[:, DB + h:DB + h + 1]
                st.add("act", f"{n}.v{h}", (lambda h, bias: lambda eng, i: eng.activation(v[h][:], SX[(h + 1) % 2][:], ACT.Identity, bias=bias))(h, bias),
                       f"{n}.dt{h}" + last(f"{prev}.sp{h}{back}"))
                st.add("act", f"{n}.a{h}", (lambda h: lambda eng, i: eng.activation(ab[h][:], v[h][:], ACT.Abs))(h), f"{n}.v{h}")
                st.add("act", f"{n}.x{h}", (lambda h: lambda eng, i: eng.activation(ab[h][:], ab[h][:], ACT.Exp, scale=-1.0))(h), f"{n}.a{h}")
                bundle()
            for h in range(NH):
                st.add("act", f"{n}.l{h}", (lambda h: lambda eng, i: eng.activation(ab[h][:], ab[h][:], ACT.Ln, bias=C["one"][:, 0:1]))(h), f"{n}.x{h}")
            bundle(6)
            for h in range(NH):
                st.add("dve", f"{n}.sp{h}", (lambda h: lambda eng, i: eng.scalar_tensor_tensor(dt[q][:, h, :], v[h][:], 0.0, ab[h][:], ALU.max, ALU.add))(h), f"{n}.l{h}" + free)
                bundle()
                st.add("dve", f"{n}.du{h}", (lambda h: lambda eng, i: eng.tensor_tensor(du[q][:, h, :], dt[q][:, h, :], u[q][:, h, :], ALU.mult))(h), f"{n}.sp{h}")
                bundle()
            return out

        def tail(q, end=False):
            tag = "e." if end else ""
            back = "@1" if q == 1 and not end else ""
            half = 1 - q
            other = "" if end or half else "@1"
            out = []

            def put(*steps):
                out.append([(e, tag + n, f, af.split(), d) for e, n, f, af, d in steps])
            prev = lambda name: f"{name}" if end else name + other
            for h in range(NH):
                put(("dve", f"yd{q}.{h}", (lambda h: lambda eng, i: eng.scalar_tensor_tensor(y2[h][:], u[q][:, h, :], cols[:, DV + h:DV + h + 1], SY[h][:], ALU.mult, ALU.add))(h),
                     f"ys{q}.{2 * NST - NH + h}{back} {prev(f'op{1 - q}')}" + ("" if end else " s.mem"), False))
                put(("dve", f"y2{q}.{h}", (lambda h: lambda eng, i: eng.tensor_tensor(y2[h][:], y2[h][:], sz[q][:, h, :], ALU.mult))(h), f"{tag}yd{q}.{h}", False))

            def outp(eng, i):
                for h in range(NH):
                    x = eng.matmul(SX[0][:], w_out[:, h, :], y2[h][:], start=h == 0, stop=h == NH - 1)
                return x
            ready = "p0.v1 p0.v0" if end else before_first(f"p{q ^ 1}.v1" + ("@1" if half == 0 else "") + f" p{q ^ 1}.v0" + ("@1" if half == 0 else ""))
            put(("pe", f"op{q}", outp, f"{tag}y2{q}.0 {tag}y2{q}.1 " + ready, False))
            put(("act", f"gT{q}", lambda eng, i: eng.activation(gT[:], SX[0][:], ACT.Gelu), f"{tag}op{q} " + prev(f"gl{1 - q}"), False))
            glus = (SX[1], SX[0])

            def glu(eng, i):
                for k in range(NT):
                    dst = glus[k // 2][:, (k % 2) * 2 * D:(k % 2 + 1) * 2 * D]
                    eng.matmul(dst, gT[:, k * P:(k + 1) * P], w_glu[:], start=True, stop=False)
                    x = eng.matmul(dst, ones[:], b_glu[:], start=False, stop=True)
                return x
            put(("pe", f"gl{q}", glu, f"{tag}gT{q}", False))
            G = [t[:].rearrange("p (k c) -> p k c", k=2) for t in glus]
            put(*[("act", f"sg{q}.{k}", (lambda k: lambda eng, i: eng.activation(sg[:, 2 * k:2 * k + 2, :], G[k][:, :, D:2 * D], ACT.Sigmoid))(k),
                   f"{tag}gl{q} " + prev(f"go{1 - q}.1"), False) for k in range(2)])
            for k in range(2):
                put(("dve", f"go{q}.{k}", (lambda k: lambda eng, i: eng.tensor_tensor(o[q][:, 2 * k:2 * k + 2, :], G[k][:, :, 0:D], sg[:, 2 * k:2 * k + 2, :], ALU.mult))(k),
                     f"{tag}sg{q}.{k} " + (f"st{q}" if end else f"st{q}@1"), False))
            put(("dve", f"fin{q}", lambda eng, i: eng.tensor_tensor(o[q][:], o[q][:], skip[q][:], ALU.add), f"{tag}go{q}.0 {tag}go{q}.1", False))
            row = lambda i: NSEQ if end else i * 2 + (1 - q)
            put(("sp", f"st{q}", lambda eng, i: eng.dma_start(tokens(xout, row(i)), o[q][:]), f"{tag}fin{q}", True))
            return out

        def memory(eng, i):
            for t in (u[1], sz[1], skip[1]):
                x = eng.memset(t[:], 0.0)
            return x
        st.add("pool", "s.mem0", memory)
        st.add("dve", "s.mem", lambda eng, i: [eng.memset(SY[h][:], 0.0) for h in range(NH)][-1], "s.mem0")
        needs = {"s0.h": ["cols"], "s0.in0": ["mw0"], "s0.u0": ["cols"], "s0.e0": ["z3"], "s0.c0.0": ["diag"], "s0.dtr": ["mw1"],
                 "s0.bc": ["mx0", "mx1", "mx2", "mx3"], "s0.dt0": ["mw2"], "s0.T": ["cols"], "s0.v0": ["cols"]}
        parts = prep(0, True)
        norms = next(k for k, part in enumerate(parts) if part and part[0][1] == "s0.T")
        st.steps = [x for part in parts[:norms] for x in part] + st.steps
        st.steps += [(e, nm, f, list(af) + needs.get(nm, []), d) for part in parts[norms:] for e, nm, f, af, d in part]

        loop = Steps()
        once = {"op1": ["mw3"], "gl1": ["mw4", "mw5", "z2"]}
        jobs = [(n, h) for n in range(NST) for h in range(NH)]
        NJ = len(jobs)
        AHEAD = 4
        LEAD = {("bb", 0), ("bb", 1), ("bc", 0)} | {("da", j) for j in range(AHEAD)}

        class Jobs:

            def __init__(self, now, start=False):
                self.now, self.start, self.out = now, start, []

            def ref(self, kind, G, j):
                total = NJ if kind in ("da", "db", "hs", "ph", "ys") else NST
                G, j = G + j // total, j % total
                back = -((G - ((kind, j) in LEAD)) // 2)
                if self.start:
                    return f"s.{kind}{G % 2}.{j}" if G >= 0 else ""
                name = f"{kind}{G % 2}.{j}" + (f"@{back}" if back else "")
                return name + (f" s.{kind}{G % 2}.{j}" if back and G == 0 and (kind, j) in LEAD else "")

            def ready(self, G):
                if self.start:
                    return "s0.du1 s0.spl1 s0.spl0"
                back = "@1" if G == 0 else ""
                return before_first(" ".join(f"p{G % 2}.{k}{back}" for k in ("du1", "spl1", "spl0")))

            def add(self, engine, kind, G, j, emit, after):
                self.out.append([(engine, ("s." if self.start else "") + f"{kind}{G % 2}.{j}", emit, after.split(), False)])

            def bcast_b(self, G, n):
                G, n = G + n // NST, n % NST
                self.add("pe", "bb", G, n, lambda eng, i: eng.matmul(SB[n % 2][:], sel[0:64, n, :], bc_rows[G % 2][0:64, :], start=True, stop=True),
                         self.ready(G) + " " + self.ref("db", G, 2 * n - 3))

            def bcast_c(self, G, n):
                G, n = G + n // NST, n % NST
                self.add("pe", "bc", G, n, lambda eng, i: eng.matmul(SC[n % 2][:], sel[64:P, n, :], bc_rows[G % 2][64:P, :], start=True, stop=True),
                         self.ready(G) + " " + self.ref("ph", G, 2 * n - 3))

            def decay(self, G, j):
                G, j = G + j // NJ, j % NJ
                n, h = jobs[j]
                self.add("act", "da", G, j, lambda eng, i: eng.activation(da[j % RA][:], dt[G % 2][:, h, :], ACT.Exp, scale=a_neg[:, h, n:n + 1]),
                         self.ready(G) + " " + self.ref("hs", G, j - RA))

            def times_b(self, G, j):
                G, j = G + j // NJ, j % NJ
                n, h = jobs[j]
                B = in_b(j)
                self.add("dve", "db", G, j, lambda eng, i: eng.tensor_tensor(B[:], du[G % 2][:, h, :], SB[n % 2][:], ALU.mult), self.ref("bb", G, n))

            def scan(self, G, j):
                B = in_b(j)
                self.add("dve", "hs", G, j, lambda eng, i: eng.tensor_tensor_scan(hs[j % 4][:], da[j % RA][:], B[:], 0.0, ALU.mult, ALU.add),
                         self.ref("da", G, j) + " " + self.ref("db", G, j))

            def times_c(self, G, j):
                n, h = jobs[j]
                self.add("dve", "ph", G, j, lambda eng, i: eng.tensor_tensor(ph[j % RP][:], hs[j % 4][:], SC[n % 2][:], ALU.mult),
                         self.ref("hs", G, j) + " " + self.ref("bc", G, n) + " " + self.ref("ys", G, j - RP))

            def ysum(self, G, j):
                n, h = jobs[j]
                y_free = "" if n else f"yd{1 - G % 2}.{h}"
                self.add("pe", "ys", G, j, lambda eng, i: eng.matmul(SY[h][:], C["ident"][:], ph[j % RP][:], start=n == 0, stop=n == NST - 1, skip_group_check=True),
                         self.ref("ph", G, j) + " " + y_free)

        assert NJ % RA == 0 and NJ % RP == 0 and NJ % 4 == 0
        in_b = lambda j: db[j % 4]
        lead = Jobs(0, start=True)
        for n in range(2):
            lead.bcast_b(0, n)
        for j in range(AHEAD):
            lead.decay(0, j)
        lead.bcast_c(0, 0)
        st.steps += [(e, nm, f, list(af) + {"s.bb0.0": ["sel"], "s.da0.0": ["a.neg"]}.get(nm, []), d) for part in lead.out for e, nm, f, af, d in part]
        for q in range(2):
            J = Jobs(q)
            J.times_b(q, 0)
            for j, (n, h) in enumerate(jobs):
                J.decay(q, j + AHEAD)
                if j + 1 < NJ:
                    J.times_b(q, j + 1)
                J.scan(q, j)
                if j >= 1:
                    J.times_c(q, j - 1)
                if h == 0:
                    J.bcast_b(q, n + 2)
                    J.bcast_c(q, n + 1)
                if j >= 1:
                    J.ysum(q, j - 1)
            J.times_c(q, NJ - 1)
            J.ysum(q, NJ - 1)
            main = J.out
            yd0, y20, yd1, y21, out_proj, gelu, glu, sigmoid, *last_steps = tail(1 - q)
            cut = next(k for k, b in enumerate(main) if b[0][1] == f"ys{q}.0")
            head, rest = main[:cut] + [yd0, yd1], main[cut:]
            gap = [[]]
            side = [y20, y21, out_proj] + gap + [gelu] + gap + [glu] + gap + [sigmoid] + gap * 4 + last_steps + prep(1 - q)
            end = next(k for k, b in enumerate(rest) if b[0][1] in ("bb1.0", "bb0.0", "da1.0", "da0.0"))
            parts = head + weave(rest[:end], side) + rest[end:]
            loop.steps += [(e, n_, f, list(af) + once.get(n_, []), d) for part in parts for e, n_, f, af, d in part]
        fin = Steps()
        fin.steps = [x for part in tail(1, end=True) for x in part]
        run(nc, sems, before=st, loop=loop, count=NSEQ // 2, after=fin)


def attention(nc, sems, C, bank, xin, xout, a):
    NB = SEQ // QB
    KP = SEQ + 2 * PAD
    BB = 4
    UB = 2 * BB
    GU = HG * NB // UB
    NU = 2 * GU
    VW = HG * HD + 1
    PVW = 96
    with ExitStack() as ctx:
        def sb(name, shape, dt=F32):
            return ctx.enter_context(nc.sbuf_tensor(name + "_a", shape, dt))

        T = ln_tiles(sb)
        T["eps"] = C["eps"]
        w_q, w_k = sb("w_q", [P, HG, P]), sb("w_k", [P, HG, P])
        w_v, w_o = sb("w_v", [P, D]), sb("w_o", [P, D])
        b_rows, b_cols = sb("b_rows", [2 * HG, P]), sb("b_cols", [P, 2 * HG])
        b_vo, b_all = sb("b_vo", [1, 2 * D]), sb("b_all", [P, 2, D])
        ones = sb("ones", [1, P])
        band = sb("band", [P, KW])
        own = sb("own", [P, HG * HD])
        fold = sb("fold", [P, QB])
        xp, xn = sb("xp", [P, NT, D]), sb("xn", [P, NT, D])
        xT = sb("xT", [P, KP])
        two = lambda name, shape: [sb(name + str(p), shape) for p in range(2)]
        qd = [[sb(f"qd{p}{g}", [P, NB, HG, QB]) for g in range(HG)] for p in range(2)]
        kT = [[sb(f"kT{p}{g}", [P, KP]) for g in range(HG)] for p in range(2)]
        vb = two("vb", [KW, NB * HG * VW + PVW - VW])
        vb4 = [v[:, 0:NB * HG * VW].rearrange("p (b g c) -> p b g c", b=NB, g=HG) for v in vb]
        s = [sb(f"s{r}", [P, UB, KW]) for r in range(4)]
        mx = [sb(f"mx{r}", [P, UB]) for r in range(4)]
        pT = two("pT", [KW, UB, P])
        rc = two("rc", [P, UB])
        o1 = two("o1", [P, UB, HG * HD])
        oT = sb("oT", [P, SEQ])
        o = two("o", [P, NT, D])
        BS, BT, BO, BZ, BX = bank[0:2], bank[2:4], bank[4], bank[5], bank[6:8]

        st = Steps()
        wT = a["L1_attn_Wqkv"]
        heads = lambda w: w[:].rearrange("p g (r c) -> p (g r) c", r=HG)[:, :, 0:HD]
        st.add("pool", "z0", lambda eng, i: eng.memset(w_q[:], 0.0))
        st.add("pool", "z1", lambda eng, i: eng.memset(w_k[:], 0.0))
        st.add("pool", "z2", lambda eng, i: eng.memset(b_rows[:], 0.0))
        for k, w in enumerate((w_q, w_k)):
            st.dma(f"mx{k}", lambda eng, i, k=k, w=w: eng.dma_start(heads(w), wT[:, k * D:(k + 1) * D].rearrange("p (h c) -> p h c", c=HD)), f"z{k}")
            st.dma(f"mv{k}", lambda eng, i, k=k: eng.dma_start(b_rows[k * HG:(k + 1) * HG, :].rearrange("g (r c) -> g r c", r=HG)[:, :, 0:HD],
                                                             a["L1_attn_bqkv"][k * D:(k + 1) * D].rearrange("(g r c) -> g r c", g=HG, r=HG)), "z2")
        st.dma("mw0", lambda eng, i: eng.dma_start(w_v[:], wT[:, 2 * D:3 * D]))
        st.dma("mw1", lambda eng, i: eng.dma_start(w_o[:], a["L1_attn_Wout"]))
        st.dma("mw2", lambda eng, i: eng.dma_start(b_vo[:, 0:D], a["L1_attn_bqkv"][2 * D:3 * D].rearrange("(o n) -> o n", o=1)))
        st.dma("mw3", lambda eng, i: eng.dma_start(b_vo[:, D:2 * D], a["L1_attn_bout"].rearrange("(o n) -> o n", o=1)))
        st.add("pe", "bT", lambda eng, i: eng.transpose(BX[0][:, 0:2 * HG], b_rows[:], C["ident"][0:2 * HG, 0:2 * HG]), "mv0 mv1")
        st.add("dve", "b_cols", lambda eng, i: eng.tensor_copy(b_cols[:], BX[0][:, 0:2 * HG]), "bT")
        st.add("pool", "ones", lambda eng, i: eng.memset(ones[:], 1.0))
        st.add("pe", "ball", lambda eng, i: eng.matmul(BX[1][:, 0:2 * D], ones[:], b_vo[:], start=True, stop=True), "ones mw2 mw3")
        st.add("dve", "b_all", lambda eng, i: eng.tensor_copy(b_all[:].rearrange("p a d -> p (a d)"), BX[1][:, 0:2 * D]), "ball")
        st.add("pool", "c0", lambda eng, i: eng.memset(band[:], 0.0))
        st.add("pool", "c1", lambda eng, i: eng.memset(own[:], 0.0))
        st.add("pool", "c2", lambda eng, i: eng.memset(fold[:], 0.0))

        def quadrants(name, emit, after):
            for r in range(HG):
                last = r == HG - 1
                st.add("pool", name if last else f"{name}.{r}", lambda eng, i, r=r: emit(eng, r, slice(32 * r, 32 * r + 32)), after if r == 0 else f"{name}.{r - 1}")
        quadrants("c3", lambda eng, r, p: eng.affine_select(out=band[p, :], in_=band[p, :], compare_op=ALU.is_ge, fill=-1e30, base=0,
                                                          pattern=[[1, KW]], channel_multiplier=-1), "c2")
        quadrants("c4", lambda eng, r, p: eng.affine_select(out=band[p, :], in_=band[p, :], compare_op=ALU.is_ge, fill=-1e30, base=WIN - 1,
                                                          pattern=[[-1, KW]], channel_multiplier=1), "c3")
        quadrants("c5", lambda eng, r, p: eng.memset(own[p, HD * r:HD * r + HD], 1.0), "c4")
        quadrants("c6", lambda eng, r, p: eng.affine_select(out=fold[p, :], in_=fold[p, :], compare_op=ALU.not_equal, fill=1.0, base=0,
                                                          pattern=[[-1, QB]], channel_multiplier=1), "c5")
        st.add("pool", "c7", lambda eng, i: eng.memset(xT[:, 0:PAD], 0.0), "c6")
        st.add("pool", "c8", lambda eng, i: eng.memset(xT[:, PAD + SEQ:], 0.0))

        def zeros(eng, i):
            for p in range(2):
                for g in range(HG):
                    eng.memset(kT[p][g][:, 0:PAD], 0.0)
                    eng.memset(kT[p][g][:, PAD + SEQ:], 0.0)
                x = eng.memset(vb[p][:], 1.0)
            return x
        st.add("pool", "c9", zeros, "c8")

        for n, (p, g) in enumerate((p, g) for p in range(2) for g in range(HG)):
            engine = "dve" if n < 3 else "pool"
            st.add(engine, f"mq{p}{g}", lambda eng, i, p=p, g=g: eng.memset(qd[p][g][:], 0.0))
        st.add("pool", "s.pe1.15", lambda eng, i: eng.memset(pT[1][:], 1.0))
        st.add("pool", "s.om.14", lambda eng, i: eng.memset(o1[0][:], 0.0))
        st.add("pool", "s.ob.1", lambda eng, i: eng.memset(o[1][:], 0.0))
        st.add("dve", "s.bz", lambda eng, i: eng.memset(BZ[:], 0.0))

        def load_x(part, name, group, after=""):
            part.dma(name, lambda eng, i: eng.dma_start(xp[:], tokens(xin, group(i))), after)

        USES = [("T", "xT"), ("m0", "e0"), ("m1", "e1"), ("op", "r"), ("m2", "e2"), ("m3", "e3"), ("vm0", "v0"), ("vm1", "v1"),
                ("vm2", "v2"), ("vm3", "v3"), ("m4", "e4"), ("m5", "e5"), ("m6", "e6"), ("m7", "e7")]

        def bx(name):
            return BX[[u[0] for u in USES].index(name) % 2]

        def bank_free(name, half, start):
            k = [u[0] for u in USES].index(name) - 2
            if start:
                skip = k - 2 if k >= 0 and USES[k][0] == "op" else k
                return f"s.{USES[skip][1]}.0" if skip >= 0 else ""
            if k >= 0:
                h, back = half, ""
            else:
                h, back = 1 - half, "" if half else "@1"
            return f"{USES[k][1]}.{1 - h}{back}"

        def prep(q, start=False):
            half, tag = 1 - q, "s." if start else ""
            steps = {}

            def put(engine, name, emit, after):
                steps[name] = (engine, f"{tag}{name}.{q}", emit, after.split(), False)
            me = lambda name: f"{tag}{name}.{q}"
            free = lambda name: bank_free(name, half, start)
            sc_free = lambda g: "" if start else f"sc1.{GU * q + 2 * g + 1}" + ("@1" if q or g == 0 else "")
            v_free = "" if start else f"pv1.{GU * q + GU - 1}"
            put("pe", "T", transposes(bx("T"), xn, C["ident"]), ("s.ln0.out " if start else f"ln{q}.out" + ("@1 " if q else " ")) + free("T"))
            old = "" if start else f"m7.{1 - q}" + ("" if half else "@1")
            put("act", "xT", lambda eng, i: eng.copy(xT[:, PAD:PAD + SEQ], bx("T")[:]), me("T") + " " + old)
            for k in range(2 * HG):
                g, w = k // 2, k % 2
                X, W = bx(f"m{k}"), (w_q, w_k)[w]
                put("pe", f"m{k}", (lambda X, W, g: lambda eng, i: eng.matmul(X[:], W[:, g, :], xT[:, PAD:PAD + SEQ], start=True, stop=True))(X, W, g),
                    me("xT") + " " + free(f"m{k}"))
                if w == 0:
                    def evac(eng, i, X=X, g=g):
                        for r in range(HG):
                            p = slice(32 * r, 32 * r + 32)
                            x = eng.activation(qd[q][g][p, :, r, :], X[p, :].rearrange("p (b q) -> p b q", q=QB), ACT.Identity, bias=b_cols[p, g:g + 1])
                        return x
                    zero = "mq13" if not start else ""
                    put("act", f"e{k}", evac, f"{me(f'm{k}')} {sc_free(g)} {zero}")
                else:
                    bias = b_cols[:, HG + g:HG + g + 1]
                    put("dve", f"e{k}", (lambda X, g, bias: lambda eng, i: eng.tensor_scalar(kT[q][g][:, PAD:PAD + SEQ], X[:], bias, None, ALU.add))(X, g, bias),
                        f"{me(f'm{k}')} {sc_free(g)}")
            for k in range(NB // BB):
                X = bx(f"vm{k}")

                def vals(eng, i, X=X, k=k):
                    for j in range(BB):
                        b = BB * k + j
                        x = eng.matmul(X[0:KW, j * D:(j + 1) * D], xT[:, b * QB:b * QB + KW], w_v[:], start=True, stop=True)
                    return x
                put("pe", f"vm{k}", vals, me("xT") + " " + free(f"vm{k}"))
                put("dve", f"v{k}", (lambda X, k: lambda eng, i: eng.tensor_tensor(
                    vb4[q][:, BB * k:BB * k + BB, :, 0:VW - 1], X[0:KW, :].rearrange("p (b g c) -> p b g c", b=BB, g=HG),
                    b_all[0:KW, 0:1, :].rearrange("p a (g c) -> p a g c", g=HG).to_broadcast([KW, BB, HG, VW - 1]), ALU.add))(X, k),
                    f"{me(f'vm{k}')} {v_free}")
            put("dve", "vz0", lambda eng, i: eng.memset(vb4[q][0:PAD, 0, :, 0:VW - 1], 0.0), me("v0"))
            put("dve", "vz1", lambda eng, i: eng.memset(vb4[q][KW - PAD:KW, NB - 1, :, 0:VW - 1], 0.0), me("v3"))
            return steps

        scale = float(1.0 / np.sqrt(np.float32(HD)))
        LEAD = dict(sc0=-2, sc1=-2, sm0=-2, sm1=-2, mx=-2, sb=-2, ex=-2, pt0=0, pt1=0, pe0=0, pe1=0, pv0=1, pv1=1, rc=1, on=1, om=1, ot=2)

        def ref(slot, *wanted):
            out = []
            for kind, u in wanted:
                back = -((u + LEAD[kind]) // NU)
                assert back >= 0 and u + LEAD[kind] <= slot
                out.append(f"{kind}.{u % NU}" + (f"@{back}" if back else ""))
            return " ".join(out)

        def scores(part, u, ready, start=False):
            tag, slot = ("s." if start else ""), u - 2
            q, g, half = u // GU % 2, u % GU // 2, u % 2
            S, M = s[u % 4], mx[u % 4]
            me = lambda kind: f"{tag}{kind}.{u % NU}"
            r = lambda *x: "" if start else w(ref(slot, *x))
            for c in range(2):
                X = BS[c]

                def mm(eng, i, X=X, c=c):
                    for j in range(BB):
                        b = half * UB + c * BB + j
                        x = eng.matmul(X[:, j * KW:(j + 1) * KW], qd[q][g][:, b, :, :].rearrange("p r q -> p (r q)"), kT[q][g][:, b * QB:b * QB + KW], start=True, stop=True)
                    return x
                bank = r((f"sm{c}", u - 1)) if not start else f"s.sm{c}.{u - 1}" if u else ""
                part.add("pe", me(f"sc{c}"), mm, f"{ready} {bank}")
                part.add("dve", me(f"sm{c}"), lambda eng, i, X=X, c=c: eng.scalar_tensor_tensor(
                    S[:, c * BB:(c + 1) * BB, :], X[:, 0:BB * KW].rearrange("p (b k) -> p b k", k=KW), scale, band[:, None, :].to_broadcast([P, BB, KW]), ALU.mult, ALU.add),
                    me(f"sc{c}") + " " + r(("pt1", u - 4)))
            part.add("dve", me("mx"), lambda eng, i: eng.reduce_max(M[:], S[:], AX.X), me("sm1"))
            part.add("dve", me("sb"), lambda eng, i: eng.tensor_tensor(S[:], S[:], M[:, :, None].to_broadcast([P, UB, KW]), ALU.subtract), me("mx"))
            part.add("act", me("ex"), lambda eng, i: eng.activation(S[:], S[:], ACT.Exp), me("sb"))

        def turn(part, u):
            S, W = s[u % 4], pT[u % 2]
            for c in range(2):
                def tr(eng, i, c=c):
                    for j in range(BB):
                        x = eng.transpose(BT[c][0:KW, j * P:(j + 1) * P], S[:, c * BB + j, :], C["ident"][:])
                    return x
                part.add("pe", f"pt{c}.{u}", tr, w(ref(u, ("ex", u), (f"pe{c}", u - 1))))
                part.add("act", f"pe{c}.{u}", lambda eng, i, c=c: eng.copy(W[:, c * BB:(c + 1) * BB, :].rearrange("p b q -> p (b q)"), BT[c][0:KW, :]),
                         f"pt{c}.{u} " + ref(u, ("pv1", u - 2)))

        def outputs(part, slot, tag=""):
            u = slot - 1
            q, g, half = u // GU % 2, u % GU // 2, u % 2
            W, Z, R = pT[u % 2], o1[u % 2], rc[u % 2]
            me = lambda kind: f"{tag}{kind}.{u % NU}"
            r = (lambda *x: w(ref(slot, *x))) if not tag else (lambda *x: " ".join(f"{k}.{v}" for k, v in x))
            values = (f"v3.{q} vz0.{q} vz1.{q}" if tag or (q == 1 and 0 <= u) else f"v3.{q}@1 vz0.{q}@1 vz1.{q}@1")
            for c in range(2):
                def pv(eng, i, c=c):
                    for j in range(BB):
                        b = half * UB + c * BB + j
                        at, v = (c * BB + j) * VW, (b * HG + g) * VW
                        x = eng.matmul(BO[:, at:at + PVW], W[:, c * BB + j, :], vb[q][:, v:v + PVW], start=True, stop=True)
                    return x
                part.add("pe", me(f"pv{c}"), pv, r((f"pe{c}", u)) + " " + r(("on", u - 1)) + " " + w(values))
            O = BO[:, 0:UB * VW].rearrange("p (b c) -> p b c", c=VW)
            part.add("dve", me("rc"), lambda eng, i: eng.reciprocal(R[:], O[:, :, VW - 1]), me("pv1"))
            part.add("dve", me("on"), lambda eng, i: eng.tensor_tensor(Z[:], O[:, :, 0:VW - 1], R[:, :, None].to_broadcast([P, UB, HG * HD]), ALU.mult),
                     me("rc") + " " + r(("ot", u - 2)))
            part.add("dve", me("om"), lambda eng, i: eng.tensor_tensor(Z[:], Z[:], own[:, None, :].to_broadcast([P, UB, HG * HD]), ALU.mult), me("on"))

        def gather(part, slot, om, tag=""):
            u = slot - 2
            g, half = u % GU // 2, u % 2
            Z = o1[u % 2]

            def ot(eng, i):
                for j in range(UB):
                    b = half * UB + j
                    x = eng.matmul(BZ[32 * g:32 * g + 32, b * QB:(b + 1) * QB], Z[:, j, :], fold[:], start=True, stop=True)
                return x
            first = u % GU == 0 and not tag
            part.add("pe", f"{tag}ot.{u % NU}", ot, om + (f" oc.{1 - u // GU % 2}" if first else "") + " s.bz")

        def project(q, tag=""):
            me = lambda name: f"{tag}{name}.{q}"
            ot = f"{tag}ot.{GU * q + GU - 1}"
            old = f"op.{1 - q}" + ("@1" if q == 1 else "")
            copy = ("act", me("oc"), lambda eng, i: eng.copy(oT[:], BZ[:]), (ot + " " + (old if not tag else "op.0")).split(), False)

            def proj(eng, i):
                for k in range(NT):
                    t = slice(k * P, (k + 1) * P)
                    x = eng.matmul(bx("op")[:, t], oT[:, t], w_o[:], start=True, stop=True)
                return x
            free = bank_free("op", 1 - q, False) if not tag else "e7.0 e6.0"
            mm = ("pe", me("op"), proj, f"{me('oc')} {free}".split(), False)
            add = ("dve", me("r"), lambda eng, i: eng.tensor_tensor(o[q][:], o[q][:], bx("op")[:].rearrange("p (k d) -> p k d", d=D), ALU.add),
                   (me("op") + " " + ("ob.1" if tag else w("ob.1@1") if q else "ob.0")).split(), False)
            row = lambda i: NSEQ if tag else i * 2 + (1 - q)
            store = ("sp", me("st"), lambda eng, i: eng.dma_start(tokens(xout, row(i)), o[q][:]), [me("r")], True)
            return copy, mm, add, store

        first = Steps()
        load_x(first, "s.x.0", lambda i: 0)
        layernorm(first, "s.ln0", xp, xn, T, "s.x.0")
        st.steps = first.steps + st.steps
        load_x(st, "s.x.1", lambda i: 1, "s.ln0.out")
        start = prep(0, True)
        needs = {"m0": ["mx0", "mx1", "c8", "b_all"], "e0": ["b_cols", "mq00"], "e2": ["mq01"], "e4": ["mq02"], "e6": ["mq03"], "e1": ["b_cols", "c9"], "vm0": ["mw0", "c8"], "v0": ["c9", "b_all"], "T": ["b_cols"]}
        order = [x for pair in USES if pair[0] != "op" for x in pair] + ["vz0", "vz1"]
        for name in order:
            e, n, f, af, d = start[name]
            st.steps.append((e, n, f, af + needs.get(name, []), d))
        layernorm(st, "s.ln1", xp, xn, T, "s.x.1", "s.T.0")
        load_x(st, "s.x.2", lambda i: 2, "s.ln1.out")
        for u in range(2):
            scores(st, u, "s.e0.0 s.e1.0 c6", start=True)
        alias = {"x.0": "s.x.2", "pe0.15": "s.pe1.15", "v3.1": "c9"}
        names = {x[1] for x in st.steps}

        def w(wanted):
            out = []
            for n in wanted.split():
                out.append(n)
                base = n.partition("@")[0]
                start = alias.get(base, "s." + base)
                if "@" in n and start in names:
                    out.append(start)
            return " ".join(out)

        loop = Steps()
        for slot in range(NU):
            q, k = slot // GU, slot % GU
            side = prep(1 - q)
            for name, (e, n, f, af, d) in side.items():
                side[name] = (e, n, f, w(" ".join(af)).split(), d)
            turn_of = {0: ["T"], 1: ["m0", "m1"], 2: ["op", "m2", "m3"], 3: ["vm0", "vm1"], 4: ["vm2", "vm3"], 5: ["m4", "m5"], 6: ["m6", "m7"]}
            queue = []
            for name in turn_of.get(k, []):
                if name == "op":
                    queue.append(list(project(1 - q)))
                else:
                    reader = dict(USES)[name]
                    queue.append([side[name], side[reader]] + [side[z] for z in {"v0": ["vz0"], "v3": ["vz1"]}.get(reader, [])])
            v = slot + 2
            g, qv = v % GU // 2, v // GU % 2
            ready = w(" ".join(f"e{n}.{qv}" + ("@1" if 2 <= v < GU else "") for n in (2 * g, 2 * g + 1))) + " c6"
            sc, tr, pv, ot = Steps(), Steps(), Steps(), Steps()
            scores(sc, v, ready)
            turn(tr, slot)
            outputs(pv, slot)
            gather(ot, slot, w(ref(slot, ("om", slot - 2))))
            sc, tr, pv, ot = sc.steps, tr.steps, pv.steps, ot.steps
            pieces = [sc[0:2], sc[2:6], tr[0:2], tr[2:4] + sc[6:7], pv[0:1], pv[1:], ot]
            for n, piece in enumerate(pieces):
                loop.steps += piece
                if n in (1, 3, 5) and queue:
                    loop.steps += queue.pop(0)
            if k == GU - 1:
                layernorm(loop, f"ln{q}", xp, xn, T, w(f"x.{q}" + ("@1" if q == 0 else "")), f"T.{1 - q}")
                loop.dma(f"x.{1 - q}", (lambda q: lambda eng, i: eng.dma_start(xp[:], tokens(xin, (i * 2 + (q + 3)) % NSEQ)))(q), f"ln{q}.out")
            if k == 4:
                loop.dma(f"ox.{q}", (lambda q: lambda eng, i: eng.dma_start(o[q][:], tokens(xin, group_of(i, q))))(q), "st.0@1" if q == 0 else "st.1")
                loop.add("pool", f"ob.{q}", (lambda q: lambda eng, i: eng.tensor_tensor(o[q][:], o[q][:], b_all[:, 1:2, :].to_broadcast([P, NT, D]), ALU.add))(q), f"ox.{q}")
        end = Steps()
        outputs(end, NU, "e.")
        gather(end, NU, "om.14", "e.")
        gather(end, NU + 1, "e.om.15", "e.")
        end.steps += project(1, "e.")
        run(nc, sems, before=st, loop=loop, count=NSEQ // 2, after=end)


RT = NSEQ * NT + E
SPARE = 2
XS_TILES = -(-(SPARE + RT) // (NSEQ // 2)) * (NSEQ // 2)
TILES = NSEQ * NT
CLEAR = XS_TILES // (NSEQ // 2)


def ffn1(nc, sems, C, bank, xin, xout, w, xs, ys):
    NU, U, R = 2, 4, 4
    with ExitStack() as ctx:
        def sb(name, shape, dt=F32):
            return ctx.enter_context(nc.sbuf_tensor(name + w["tag"], shape, dt))

        U32, I32 = mybir.dt.uint32, mybir.dt.int32
        two = lambda name, shape, dt=F32: [sb(name + str(p), shape, dt) for p in range(2)]
        T = ln_tiles(sb)
        T["eps"] = C["eps"]
        up_hi = [sb(f"up_hi{u}", [P, E + 1, HID], F32R) for u in range(NU)]
        up_lo = [sb(f"up_lo{u}", [P, E + 1, HID], F32R) for u in range(NU)]
        dn = sb("dn", [P, E + 1, HC, D])
        wg = sb("wg", [P, E])
        raw = [sb(f"raw{r}", [P, HID]) for r in range(3)]
        xp, xn, xT = two("xp", [P, NT, D]), two("xn", [P, NT, D]), two("xT", [P, SEQ])
        xn_all = sb("xn_all", [P, TILES, D])
        xT_hi, xT_lo = sb("xT_hi", [P, NSEQ * SEQ], F32R), sb("xT_lo", [P, NSEQ * SEQ], F32R)
        acc_all = sb("acc_all", [P, TILES, D])
        lg = sb("lg", [P, TILES, E])
        mx, ge, wt, v1 = sb("mx", [P, TILES]), sb("ge", [P, TILES, E]), sb("wt", [P, TILES, E]), sb("v1", [P, TILES])
        oh, ohr = sb("oh", [P, TILES, E]), sb("ohr", [P, TILES * E], F32R)
        tri, one_r = sb("tri", [P, P], F32R), sb("one_r", [P, P], F32R)
        tri_f, one_f = sb("tri_f", [P, P]), sb("one_f", [P, E * TILES])
        tot, cum, exc = sb("tot", [P, E, TILES]), sb("cum", [P, E, TILES]), sb("exc", [P, E, TILES])
        cnt, ntl, tcum, base = sb("cnt", [P, E]), sb("ntl", [P, E]), sb("tcum", [P, E]), sb("base", [P, E])
        steps128 = sb("steps128", [P, TILES])
        tile_no = sb("tile_no", [1, RT])
        many = sb("many", [P, E, TILES])
        slot_f, slot = sb("slot_f", [P, TILES]), sb("slot", [P, TILES], U32)
        te_f, te_c, te = sb("te_f", [1, RT]), sb("te_c", [1, RT, E - 1]), sb("te", [1, RT], I32)
        four = lambda name, shape, dt=F32: [sb(name + str(p), shape, dt) for p in range(R)]
        xg = four("xg", [P, D])
        x_hi, x_lo = four("x_hi", [P, P], F32R), four("x_lo", [P, P], F32R)
        te_tab = sb("te_tab", [1, RT // U + 1, U + 2], I32)
        gel, hf = two("gel", [P, HID]), four("hf", [P, HID])
        hT, yb = raw[0:2], [raw[2][:, r * D:(r + 1) * D] for r in range(2)]
        HB, HT, XB, YB = bank[0:4], bank[4:6], bank[6], bank[7]

        st, loop = Steps(), Steps()
        ring = [""] * 3

        def weights(st, experts):
            for e in experts:
                for u in range(NU):
                    r, name = (NU * e + u) % 3, f"w{u}.{e}"
                    split_weight(st, name, w["up"][u](e), raw[r][:], up_hi[u][:, e, :], up_lo[u][:, e, :], ring[r])
                    ring[r] = name + ".lo"
                st.dma(f"wd{e}", (lambda e: lambda eng, i: eng.dma_start(dn[:, e, :, :], w["down"](e)))(e))
        first, second = [E] + list(range(5)), list(range(5, E))
        st.dma("wg", lambda eng, i: eng.dma_start(wg[:], w["gate"]))
        for q in range(2):
            st.dma(f"s.x{q}", (lambda q: lambda eng, i: eng.dma_start(xp[q][:], tokens(xin, q)))(q))
        weights(st, first)
        halves = []
        for q in range(2):
            half = Steps()
            halves.append(half)
            Tq = T if q == 0 else T | {k: sb(k + "_b", t.shape) for k, t in T.items() if k != "eps"}
            at = lambda i, q=q: bass.ds((i * 2 + q) * NT, NT)
            cols = lambda i, q=q: bass.ds((i * 2 + q) * SEQ, SEQ)
            layernorm(half, f"ln{q}", xp[q], xn[q], Tq, f"x{q}@1 s.x{q}", f"T{q}@1 keep{q}@1")
            half.add("pe", f"T{q}", transposes(HB[q], xn[q], C["ident"]), f"ln{q}.out xT{q}@1 lo{q}@1")
            half.add("act", f"xT{q}", (lambda q: lambda eng, i: eng.copy(xT[q][:], HB[q][:]))(q), f"T{q} gt{q}@1")
            half.add("act", f"hi{q}", (lambda q, cols: lambda eng, i: eng.copy(xT_hi[:, cols(i)], HB[q][:]))(q, cols))
            half.add("dve", f"lo{q}", (lambda q, cols: lambda eng, i: eng.tensor_tensor(xT_lo[:, cols(i)], HB[q][:], xT_hi[:, cols(i)].bitcast(F32), ALU.subtract))(q, cols), f"hi{q}")
            half.add("act", f"keep{q}", (lambda q, at: lambda eng, i: eng.copy(xn_all[:, at(i), :], xn[q][:]))(q, at))
            half.dma(f"x{q}", (lambda q: lambda eng, i: eng.dma_start(xp[q][:], tokens(xin, (i * 2 + (q + 2)) % NSEQ)))(q), f"ln{q}.out", engine="act")

            def gate(eng, i, q=q):
                for k in range(NT):
                    x = eng.matmul(HT[q][:, k * E:(k + 1) * E], xT[q][:, k * P:(k + 1) * P], wg[:], start=True, stop=True)
                return x
            half.add("pe", f"gt{q}", gate, f"xT{q} lg{q}@1 wg")
            half.add("dve", f"lg{q}", (lambda q, at: lambda eng, i: eng.tensor_copy(lg[:, at(i), :], HT[q][:, 0:NT * E].rearrange("p (k e) -> p k e", e=E)))(q, at), f"gt{q}")
        for pair in zip(*(h.steps for h in halves)):
            loop.steps += pair

        rt = Steps()
        every = lambda ap, n: ap[:, :, None].to_broadcast([P, TILES, n])
        pow2 = C["pow2"][:, None, :].to_broadcast([P, TILES, E])
        chain = [""]

        def dve(name, emit, extra=""):
            rt.add("dve", name, emit, f"{chain[0]} {extra}")
            chain[0] = name
        tt = lambda out, a, b, op: (lambda eng, i: eng.tensor_tensor(out, a, b, op))
        dve("r.max", lambda eng, i: eng.reduce_max(mx[:], lg[:], AX.X), "lg0 lg1")
        dve("r.ge", tt(ge[:], lg[:], every(mx, E), ALU.is_ge))
        dve("r.wt", tt(wt[:], ge[:], pow2, ALU.mult))
        dve("r.v1", lambda eng, i: eng.reduce_sum(v1[:], wt[:], AX.X))
        dve("r.st", tt(wt[:], every(v1, E), pow2, ALU.is_ge))
        dve("r.o0", lambda eng, i: eng.tensor_copy(oh[:, :, 0:1], wt[:, :, 0:1]))
        dve("r.oh", tt(oh[:, :, 1:E], wt[:, :, 1:E], wt[:, :, 0:E - 1], ALU.subtract))
        dve("r.ohr", lambda eng, i: eng.tensor_copy(ohr[:], oh[:].rearrange("p t e -> p (t e)")))
        rt.add("pe", "r.rank", lambda eng, i: eng.matmul(XB[:, 0:TILES * E], tri[:], ohr[:], start=True, stop=True), "r.ohr t.tri")
        rt.add("pe", "r.tot", lambda eng, i: eng.matmul(YB[:, 0:TILES * E], one_r[:], ohr[:], start=True, stop=True), "r.ohr t.one")
        dve("r.t", lambda eng, i: eng.tensor_copy(tot[:], YB[:, 0:TILES * E].rearrange("p (t e) -> p e t", e=E)), "r.tot")
        flat = lambda t: t[:].rearrange("p e t -> p (e t)")
        dve("r.cum", lambda eng, i: eng.tensor_tensor_scan(flat(cum), one_f[:], flat(tot), 0.0, ALU.mult, ALU.add), "t.onef")
        dve("r.exc", tt(exc[:], cum[:], tot[:], ALU.subtract))
        dve("r.cnt", tt(cnt[:], cum[:, :, TILES - 1], exc[:, :, 0], ALU.subtract))
        dve("r.many", tt(many[:], cnt[:, :, None].to_broadcast([P, E, TILES]), steps128[:, None, :].to_broadcast([P, E, TILES]), ALU.is_gt), "t.s128")
        dve("r.ntl", lambda eng, i: eng.reduce_sum(ntl[:], many[:], AX.X))
        dve("r.tc", lambda eng, i: eng.tensor_tensor_scan(tcum[:], one_f[:, 0:E], ntl[:], 0.0, ALU.mult, ALU.add))
        dve("r.b0", tt(base[:], tcum[:], ntl[:], ALU.subtract))
        dve("r.b1", lambda eng, i: eng.tensor_scalar(base[:], base[:], float(P), float(SPARE * P), ALU.mult, ALU.add))
        dve("r.b2", tt(base[:], base[:], exc[:, :, 0], ALU.subtract))
        dve("r.pos", tt(exc[:], exc[:], base[:, :, None].to_broadcast([P, E, TILES]), ALU.add))
        dve("r.row", tt(wt[:], XB[:, 0:TILES * E].rearrange("p (t e) -> p t e", e=E), exc[:].rearrange("p e t -> p t e"), ALU.add), "r.rank")
        dve("r.own", tt(wt[:], wt[:], oh[:], ALU.mult))
        dve("r.sum", lambda eng, i: eng.reduce_sum(slot_f[:], wt[:], AX.X))
        dve("r.slot", lambda eng, i: eng.tensor_copy(slot[:], slot_f[:]))
        dve("r.te", tt(te_c[:], tile_no[:, :, None].to_broadcast([1, RT, E - 1]), tcum[0:1, None, 0:E - 1].to_broadcast([1, RT, E - 1]), ALU.is_ge), "t.no")
        dve("r.tf", lambda eng, i: eng.reduce_sum(te_f[:], te_c[:], AX.X))
        dve("r.ti", lambda eng, i: eng.tensor_copy(te[:], te_f[:]))

        tb = Steps()
        tb.add("pool", "t.0", lambda eng, i: eng.memset(tri_f[:], 1.0))
        tb.add("pool", "t.1", lambda eng, i: eng.affine_select(out=tri_f[:], in_=tri_f[:], compare_op=ALU.is_gt, fill=0.0, base=0, pattern=[[1, P]], channel_multiplier=-1), "t.0")
        tb.add("pool", "t.tri", lambda eng, i: eng.tensor_copy(tri[:], tri_f[:]), "t.1")
        tb.add("pool", "t.onef", lambda eng, i: eng.memset(one_f[:], 1.0))
        tb.add("pool", "t.one", lambda eng, i: eng.tensor_copy(one_r[:], one_f[:, 0:P]), "t.onef")
        tb.add("pool", "t.s128", lambda eng, i: eng.iota(steps128[:], [[P, TILES]], base=0, channel_multiplier=0, allow_small_or_imprecise_dtypes=True), "t.one")
        tb.add("pool", "t.no", lambda eng, i: eng.iota(tile_no[:], [[1, RT]], base=0, channel_multiplier=0, allow_small_or_imprecise_dtypes=True), "t.s128")

        tb.steps += st.steps
        run(nc, sems, before=tb, loop=loop, count=NSEQ // 2, after=rt)

        sc, loop = Steps(), Steps()
        for t in range(TILES):
            sc.dma(f"sc{t}", (lambda t: lambda eng, i: eng.indirect_dma_start(
                xs[:, :], bass.IndirectOffsetOnAxis(slot[:, t:t + 1], 0), xn_all[:, t, :], None))(t), engine="pool")
        ring = [""] * 3
        weights(sc, second)
        by_slot = te[:].rearrange("o (n u) -> o n u", u=U)
        sc.add("dve", "te.0", lambda eng, i: eng.memset(te_tab[:], 0))
        sc.add("dve", "te.1", lambda eng, i: eng.tensor_copy(te_tab[:, 0:RT // U, 2:U + 2], by_slot), "te.0")
        sc.add("dve", "te.2", lambda eng, i: eng.tensor_copy(te_tab[:, 1:RT // U + 1, 0:2], by_slot[:, :, U - 2:U]), "te.1")
        for q in range(2):
            sc.dma(f"s.a{q}", (lambda q: lambda eng, i: eng.dma_start(xp[q][:], tokens(xin, q)))(q), engine="act")
        jobs = [(q, c) for q in range(2) for c in range(HC)]
        nm = lambda kind, j: f"{kind}{j}" if j >= 0 else f"{kind}{j + len(jobs)}@1"

        def up(j):
            q, c = jobs[j]
            s, r = slice(c * P, (c + 1) * P), j % 2

            def emit(eng, i):
                at = bass.ds((i * 2 + q) * SEQ, SEQ)
                for u in range(NU):
                    x = three(eng, HB[2 * r + u][:], up_hi[u][:, E, s], up_lo[u][:, E, s], xT_hi[:, at], xT_lo[:, at], True, True)
                return x
            loop.add("pe", f"up{j}", emit, nm("f", j - 2))
            loop.add("act", f"g{j}", lambda eng, i: eng.activation(gel[r][:], HB[2 * r][:], ACT.Gelu), f"up{j} " + nm("f", j - 2))
            loop.add("dve", f"f{j}", lambda eng, i: eng.tensor_tensor(hf[j % 4][:], gel[r][:], HB[2 * r + 1][:], ALU.mult), f"g{j} " + nm("y", j - 4))

        def shared_down(j):
            q, c = jobs[j]
            Y = HT[q]

            def emit(eng, i):
                for k in range(NT):
                    t = slice(k * P, (k + 1) * P)
                    x = eng.matmul(Y[:, t], hf[j % 4][:, t], dn[:, E, c, :], start=c == 0 and k == 0, stop=c == HC - 1 and k == NT - 1, skip_group_check=True)
                return x
            loop.add("pe", f"y{j}", emit, f"f{j}" + (f" a{q}@1" if c == 0 else ""))
            if c == HC - 1:
                loop.add("dve", f"a{q}", lambda eng, i: eng.scalar_tensor_tensor(
                    acc_all[:, bass.ds((i * 2 + q) * NT, NT), :], Y[:].rearrange("p (k d) -> p k d", d=D), 0.5, xp[q][:], ALU.mult, ALU.add), f"y{j} x{q}@1 s.a{q}")
                loop.dma(f"x{q}", lambda eng, i: eng.dma_start(xp[q][:], tokens(xin, (i * 2 + (q + 2)) % NSEQ)), f"a{q}", engine="act")

        for j in range(len(jobs) + 2):
            if j < len(jobs):
                up(j)
            if j >= 2:
                shared_down(j - 2)
        run(nc, sems, before=sc, loop=loop, count=NSEQ // 2)

        LEAD = dict(ld=-4, T=-2, xh=-2, xl=-2, up=0, g=0, f=0, ht=1, hc=1, dn=2, yc=2, st=2)

        def tile_loop():
            pre, loop, post = Steps(), Steps(), Steps()
            regs = {}

            def ref(h, *wanted):
                out = []
                for kind, d in wanted:
                    back = -((h + d + LEAD[kind]) // U)
                    assert back >= 0
                    out.append(f"{kind}{(h + d) % U}" + (f"@{back}" if back else ""))
                return " ".join(out)

            def turn_in(part, name, t, after):
                part.add("pe", f"{name}T{t}", lambda eng, i: eng.transpose(XB[:, 0:P], xg[t % R][:], C["ident"][:]), after[0])
                part.add("act", f"{name}xh{t}", lambda eng, i: eng.copy(x_hi[t % R][:], XB[:, 0:P]), f"{name}T{t} " + after[1])
                part.add("dve", f"{name}xl{t}", lambda eng, i: eng.tensor_tensor(x_lo[t % R][:], XB[:, 0:P], x_hi[t % R][:].bitcast(F32), ALU.subtract), f"{name}xh{t}")

            def turn_hidden(part, name, h, after):
                t, r = (h - 1) % U, (h - 1) % 2

                def ht(eng, i):
                    for c in range(HC):
                        x = eng.transpose(HT[r][:, c * P:(c + 1) * P], hf[r][:, c * P:(c + 1) * P], C["ident"][:])
                    return x
                part.add("pe", f"{name}ht{t}", ht, after[0])
                part.add("act", f"{name}hc{t}", lambda eng, i: eng.copy(hT[r][:], HT[r][:]), f"{name}ht{t} " + after[1])

            def down(part, name, h, row, after):
                t, r = (h - 2) % U, h % 2

                def dn_(eng, i):
                    e = regs["down"][h]
                    W = lambda c: dn[:, bass.ds(e, 1), c, :].rearrange("p a n -> p (a n)")
                    for c in range(HC):
                        x = eng.matmul(YB[:, 0:D], hT[r][:, c * P:(c + 1) * P], W(c), start=c == 0, stop=c == HC - 1)
                    return x
                part.add("pe", f"{name}dn{t}", dn_, after[0])
                part.add("dve", f"{name}yc{t}", lambda eng, i: eng.tensor_copy(yb[r], YB[:, 0:D]), f"{name}dn{t} " + after[1])
                part.dma(f"{name}st{t}", lambda eng, i: eng.dma_start(ys[row(i), :], yb[r]), f"{name}yc{t}")

            def experts(eng, at, n):
                _, r = nc.values_load_multi_w_load_instructions(te_tab[0:1, at, 0:n], engines=(mybir.EngineType.PE,), min_val=0, max_val=E - 1)
                return list(r)

            for t in range(R):
                pre.dma(f"p.ld{t}", (lambda t: lambda eng, i: eng.dma_start(xg[t][:], xs[(SPARE + t) * P:(SPARE + t + 1) * P, :]))(t))
            turn_in(pre, "p.", 0, ("p.ld0", ""))
            turn_in(pre, "p.", 1, ("p.ld1 p.xl0", ""))
            pre.add("dve", "p.f", lambda eng, i: eng.memset(hf[1][:], 0.0))
            pre.add("dve", "p.h", lambda eng, i: eng.memset(hT[0][:], 0.0))
            for h in range(U):
                r = h % 2

                def up(eng, i, h=h, r=r):
                    if h == 0:
                        x = experts(eng, i, U + 2)
                        regs.update(up=x[2:], down=x[:U])
                    e = regs["up"][h]
                    W = lambda t: t[:, bass.ds(e, 1), :].rearrange("p a n -> p (a n)")
                    for u in range(NU):
                        x = three(eng, HB[2 * r + u][:], x_hi[h % R][:], x_lo[h % R][:], W(up_hi[u]), W(up_lo[u]), True, True)
                    return x
                loop.add("pe", f"up{h}", up, "p.xl1 " + ref(h, ("xl", 0), ("f", -2)))
                loop.add("act", f"g{h}", (lambda r: lambda eng, i: eng.activation(gel[r][:], HB[2 * r][:], ACT.Gelu))(r), ref(h, ("up", 0), ("f", -2)))
                loop.add("dve", f"f{h}", (lambda r: lambda eng, i: eng.tensor_tensor(hf[r][:], gel[r][:], HB[2 * r + 1][:], ALU.mult))(r), ref(h, ("g", 0), ("ht", -2)))
                turn_in(loop, "", (h + 2) % U, (ref(h, ("ld", 2), ("xl", 1)) + (f" p.ld{h + 2}" if h + 2 < R else "") + " p.xl1", ref(h, ("up", -2))))
                loop.dma(f"ld{(h + 4) % U}", (lambda h: lambda eng, i: eng.dma_start(xg[h % R][:], xs[bass.ds(((i * U + (h + 4)) % RT) * P + SPARE * P, P), :]))(h),
                         ref(h, ("T", 0)) + " p.T1")
                turn_hidden(loop, "", h, (ref(h, ("f", -1), ("hc", -3)) + " p.f", ref(h, ("dn", -3))))
                down(loop, "", h, (lambda h: lambda i: bass.ds(i * U * P + (h - 2 + SPARE) * P, P))(h), (ref(h, ("hc", -2), ("yc", -3)) + " p.h", ref(h, ("st", -4))))
            end = lambda k: slice((SPARE + RT - k) * P, (SPARE + RT - k + 1) * P)
            turn_hidden(post, "e.", U, (f"f{U - 1} hc{U - 3}", f"dn{U - 3}"))

            def last_experts(eng, i):
                regs["down"] = dict(zip((U, U + 1), experts(eng, slice(RT // U, RT // U + 1), 2)))
                return eng.transpose(XB[:, 0:P], xg[0][:], C["ident"][:])
            post.add("pe", "e.regs", last_experts, "xl1 ld0")
            down(post, "e.", U, lambda i: end(2), (f"hc{U - 2} yc{U - 3}", f"st{U - 4}"))
            down(post, "e.", U + 1, lambda i: end(1), (f"e.hc{U - 1} e.yc{U - 2}", f"st{U - 3}"))
            run(nc, sems, before=pre, loop=loop, count=RT // U, after=post)

        tile_loop()
        fin = Steps()
        for g in range(NSEQ):
            t0 = g * NT
            for t in range(t0, t0 + NT):
                fin.dma(f"sc{t}", (lambda t: lambda eng, i: eng.indirect_dma_start(
                    xn_all[:, t, :], None, ys[:, :], bass.IndirectOffsetOnAxis(slot[:, t:t + 1], 0)))(t), engine="pool")
            A, R = acc_all[:, t0:t0 + NT, :], xn_all[:, t0:t0 + NT, :]
            fin.add("dve", f"fb{g}", (lambda A, R: lambda eng, i: eng.scalar_tensor_tensor(A, R, 0.5, A, ALU.mult, ALU.add))(A, R),
                    " ".join(f"sc{t}" for t in range(t0, t0 + NT)))
            fin.dma(f"fo{g}", (lambda g, A: lambda eng, i: eng.dma_start(tokens(xout, g), A))(g, A), f"fb{g}")
        run(nc, sems, before=fin)


NAMES = ["L0_attn_x", "L0_attn_ln_gamma", "L0_attn_ln_beta", "L0_attn_in_proj_w", "L0_attn_conv_w", "L0_attn_conv_b",
         "L0_attn_x_proj_w", "L0_attn_dt_proj_w", "L0_attn_dt_proj_b", "L0_attn_A_log", "L0_attn_D", "L0_attn_out_proj_w",
         "L0_attn_glu_w", "L0_attn_glu_b", "L0_ffn_W_gate", "L0_ffn_W1", "L0_ffn_b1", "L0_ffn_W2", "L0_ffn_b2",
         "L1_attn_Wqkv", "L1_attn_bqkv", "L1_attn_Wout", "L1_attn_bout", "L1_ffn_w1s", "L1_ffn_w2s", "L1_ffn_w3s",
         "L1_ffn_W1", "L1_ffn_W2", "L1_ffn_W3", "L1_ffn_Wg"]
TRANSPOSED = ("L1_attn_Wqkv", "L1_attn_Wout")


def program(nc, a, out):
    with ExitStack() as ctx:
        sems = Sems(nc, ctx)
        C = consts(nc, sems, lambda name, shape, dt=F32: ctx.enter_context(nc.sbuf_tensor(name, shape, dt)))
        bank = [ctx.enter_context(nc.psum_tensor(f"bank{b}", [P, SEQ], F32)) for b in range(8)]
        x = [a["L0_attn_x"]] + [nc.dram_tensor(f"x{k}", [NSEQ * SEQ, D], F32, kind="Internal").ap() for k in range(1, 5)]
        x[2] = nc.dram_tensor("x2s", [(NSEQ + 1) * SEQ, D], F32, kind="Internal").ap()
        x5 = nc.dram_tensor("x5", [(NSEQ + 1) * SEQ, D], F32, kind="Internal").ap()
        xs = nc.dram_tensor("xs", [XS_TILES * P, D], F32, kind="Internal").ap()
        ys = nc.dram_tensor("ys", [(SPARE + RT) * P, D], F32, kind="Internal").ap()
        f0, f1 = ffn0_weights(a), ffn1_weights(a)
        ffn0(nc, sems, C, bank, x[0], x[1], f0, xs=xs)
        mamba(nc, sems, C, bank, x[1], x[2], a)
        ffn0(nc, sems, C, bank, x[2], x[3], f0 | {"tag": "_f0b"}, spare=1)
        ffn1(nc, sems, C, bank, x[3], x[4], f1, xs, ys)
        attention(nc, sems, C, bank, x[4], x5, a)
        ffn1(nc, sems, C, bank, x5[SEQ:, :], out, f1 | {"tag": "_f1b"}, xs, ys)


def kernel(**inputs):
    import concourse.bacc as bacc
    from concourse.bass_utils import run_bass_kernel_spmd

    nc = bacc.Bacc("TRN2", target_bir_lowering=False, num_devices=1)
    arrays, a = {}, {}
    for name in NAMES:
        v = np.asarray(inputs[name])
        if name == "L0_attn_x":
            v = v.reshape(NSEQ * SEQ, D)
        if name in TRANSPOSED:
            v = v.T
        v = np.ascontiguousarray(v)
        arrays["in_" + name] = v
        a[name] = nc.dram_tensor("in_" + name, v.shape, mybir.dt.from_np(v.dtype), kind="ExternalInput").ap()
    out = nc.dram_tensor("out_0", [NSEQ * SEQ, D], F32, kind="ExternalOutput").ap()
    program(nc, a, out)
    r = run_bass_kernel_spmd(nc, [arrays], core_ids=[0])
    return r.results[0]["out_0"].reshape(NSEQ, SEQ, D)
```
